# Optimizing a Trainium2 kernel written in Bass

```python
import numpy as np
import jax
import jax.numpy as jnp

def _softmax(x, axis=-1):
    return jax.nn.softmax(x, axis=axis)

def _gelu(x):
    return jax.nn.gelu(x, approximate=True)

def _silu(x):
    return jax.nn.silu(x)

def _sigmoid(x):
    return jax.nn.sigmoid(x)

def _layernorm(x, axis=-1, eps=1e-05):
    m = jnp.mean(x, axis=axis, keepdims=True)
    v = jnp.var(x, axis=axis, keepdims=True)
    return (x - m) / jnp.sqrt(v + eps)

def _scatter_add(tgt, idx, src, axis=0):
    return tgt.at[idx].add(src)

def _segment_sum(src, seg, n):
    return jax.ops.segment_sum(src, seg, n)
kernel_name = 'mk_vit_tower_d1_tok_img1024_r4_26cbeb'

def setup_inputs(seed: int=0):
    np.random.seed(seed)
    _w = jnp.asarray

    def _rec_inputs():
        import jax
        import jax.numpy as jnp
        _rk = jax.random.key(seed)
        x = -0.00016672 + 0.999947 * jax.random.normal(jax.random.fold_in(_rk, 1), (32, 3, 112, 112), jnp.float32)
        return x
    x = _rec_inputs()

    def _L0_tok_setup():
        import jax, jax.numpy as jnp
        import numpy as np
        IMG = 96
        P = 16
        C = 3
        D = 256
        B = 64
        key = jax.random.key(seed)
        kx, kw, kb = jax.random.split(key, 3)
        fan_in = C * P * P
        bound = 1.0 / np.sqrt(fan_in)
        x = jax.random.normal(kx, (B, C, IMG, IMG), dtype=jnp.float32)
        W = jax.random.uniform(kw, (D, fan_in), dtype=jnp.float32, minval=-bound, maxval=bound)
        b = jax.random.uniform(kb, (D,), dtype=jnp.float32, minval=-bound, maxval=bound)
        return {'x': x, 'W': W, 'b': b}
    _L0_tok_all = _L0_tok_setup()
    _L0_tok_in = {k: v for k, v in _L0_tok_all.items() if k in ('W', 'b')}
    del _L0_tok_all

    def _L0_attn_setup():
        import jax, jax.numpy as jnp
        import numpy as np
        import math
        N_EMBD = 256
        N_HEAD = 16
        HEAD_DIM = N_EMBD // N_HEAD // 2
        DEPTH = 1
        LAMBDA_INIT = 0.8 - 0.6 * math.exp(-0.3 * (DEPTH - 1))
        EPS = 1e-05
        key = jax.random.key(seed)
        ks = jax.random.split(key, 8)
        B, T, C = (4, 256, N_EMBD)
        x = jax.random.normal(ks[0], (B, T, C), dtype=jnp.float32)
        w_attn = jax.random.normal(ks[1], (C, 3 * C), dtype=jnp.float32) * (1.0 / math.sqrt(C))
        w_proj = jax.random.normal(ks[2], (C, C), dtype=jnp.float32) * (1.0 / math.sqrt(C))
        lambda_q1 = jax.random.normal(ks[3], (HEAD_DIM,), dtype=jnp.float32) * 0.1
        lambda_q2 = jax.random.normal(ks[4], (HEAD_DIM,), dtype=jnp.float32) * 0.1
        lambda_k1 = jax.random.normal(ks[5], (HEAD_DIM,), dtype=jnp.float32) * 0.1
        lambda_k2 = jax.random.normal(ks[6], (HEAD_DIM,), dtype=jnp.float32) * 0.1
        gamma = jnp.ones((2 * HEAD_DIM,), dtype=jnp.float32)
        return {'x': x, 'w_attn': w_attn, 'w_proj': w_proj, 'lambda_q1': lambda_q1, 'lambda_q2': lambda_q2, 'lambda_k1': lambda_k1, 'lambda_k2': lambda_k2, 'gamma': gamma}
    _L0_attn_all = _L0_attn_setup()
    _L0_attn_in = {k: v for k, v in _L0_attn_all.items() if k in ('w_attn', 'w_proj', 'lambda_q1', 'lambda_q2', 'lambda_k1', 'lambda_k2', 'gamma')}
    del _L0_attn_all

    def _L0_ffn_setup():
        import jax, jax.numpy as jnp
        import numpy as np
        DIM = 256
        MOE_HID = 128
        SHARED_HID = 512
        N_EXPERTS = 16
        TOP_K = 2
        NORM_TOPK_PROB = True
        key = jax.random.key(seed)
        ks = jax.random.split(key, 9)
        s = 0.02
        x = jax.random.normal(ks[0], (2, 256, DIM), dtype=jnp.float32)
        Wg = jax.random.normal(ks[1], (N_EXPERTS, DIM), dtype=jnp.float32) * s
        We_gate = jax.random.normal(ks[2], (N_EXPERTS, MOE_HID, DIM), dtype=jnp.float32) * s
        We_up = jax.random.normal(ks[3], (N_EXPERTS, MOE_HID, DIM), dtype=jnp.float32) * s
        We_down = jax.random.normal(ks[4], (N_EXPERTS, DIM, MOE_HID), dtype=jnp.float32) * s
        Ws_gate = jax.random.normal(ks[5], (SHARED_HID, DIM), dtype=jnp.float32) * s
        Ws_up = jax.random.normal(ks[6], (SHARED_HID, DIM), dtype=jnp.float32) * s
        Ws_down = jax.random.normal(ks[7], (DIM, SHARED_HID), dtype=jnp.float32) * s
        Wsg = jax.random.normal(ks[8], (1, DIM), dtype=jnp.float32) * s
        return {'x': x, 'Wg': Wg, 'We_gate': We_gate, 'We_up': We_up, 'We_down': We_down, 'Ws_gate': Ws_gate, 'Ws_up': Ws_up, 'Ws_down': Ws_down, 'Wsg': Wsg}
    _L0_ffn_all = _L0_ffn_setup()
    _L0_ffn_in = {k: v for k, v in _L0_ffn_all.items() if k in ('Wg', 'We_gate', 'We_up', 'We_down', 'Ws_gate', 'Ws_up', 'Ws_down', 'Wsg')}
    del _L0_ffn_all
    return {'x': x, 'L0_tok_W': _L0_tok_in['W'], 'L0_tok_b': _L0_tok_in['b'], 'L0_attn_w_attn': _L0_attn_in['w_attn'], 'L0_attn_w_proj': _L0_attn_in['w_proj'], 'L0_attn_lambda_q1': _L0_attn_in['lambda_q1'], 'L0_attn_lambda_q2': _L0_attn_in['lambda_q2'], 'L0_attn_lambda_k1': _L0_attn_in['lambda_k1'], 'L0_attn_lambda_k2': _L0_attn_in['lambda_k2'], 'L0_attn_gamma': _L0_attn_in['gamma'], 'L0_ffn_Wg': _L0_ffn_in['Wg'], 'L0_ffn_We_gate': _L0_ffn_in['We_gate'], 'L0_ffn_We_up': _L0_ffn_in['We_up'], 'L0_ffn_We_down': _L0_ffn_in['We_down'], 'L0_ffn_Ws_gate': _L0_ffn_in['Ws_gate'], 'L0_ffn_Ws_up': _L0_ffn_in['Ws_up'], 'L0_ffn_Ws_down': _L0_ffn_in['Ws_down'], 'L0_ffn_Wsg': _L0_ffn_in['Wsg']}

def reference(x, L0_tok_W, L0_tok_b, L0_attn_w_attn, L0_attn_w_proj, L0_attn_lambda_q1, L0_attn_lambda_q2, L0_attn_lambda_k1, L0_attn_lambda_k2, L0_attn_gamma, L0_ffn_Wg, L0_ffn_We_gate, L0_ffn_We_up, L0_ffn_We_down, L0_ffn_Ws_gate, L0_ffn_Ws_up, L0_ffn_Ws_down, L0_ffn_Wsg):
    import jax
    import jax.numpy as jnp

    def _L0_tok_ref(x, W, b):
        import jax, jax.numpy as jnp
        import numpy as np
        IMG = 96
        P = 16
        C = 3
        D = 256
        B = 64
        Bsz, Cc, H, Wd = x.shape
        gh, gw = (H // P, Wd // P)
        patches = x.reshape(Bsz, Cc, gh, P, gw, P).transpose(0, 2, 4, 1, 3, 5)
        patches = patches.reshape(Bsz, gh * gw, Cc * P * P)
        return jnp.einsum('bnf,df->bnd', patches, W) + b

    def _L0_attn_ref(x, w_attn, w_proj, lambda_q1, lambda_q2, lambda_k1, lambda_k2, gamma):
        import jax, jax.numpy as jnp
        import numpy as np
        import math
        N_EMBD = 256
        N_HEAD = 16
        HEAD_DIM = N_EMBD // N_HEAD // 2
        DEPTH = 1
        LAMBDA_INIT = 0.8 - 0.6 * math.exp(-0.3 * (DEPTH - 1))
        EPS = 1e-05
        B, T, C = x.shape
        H, hd = (N_HEAD, HEAD_DIM)
        qkv = x @ w_attn
        q, k, v = jnp.split(qkv, 3, axis=-1)
        q = q.reshape(B, T, 2 * H, hd).transpose(0, 2, 1, 3)
        k = k.reshape(B, T, 2 * H, hd).transpose(0, 2, 1, 3)
        v = v.reshape(B, T, H, 2 * hd).transpose(0, 2, 1, 3)
        q = q * hd ** (-0.5)
        att = jnp.einsum('bhtd,bhsd->bhts', q, k) * (1.0 / math.sqrt(hd))
        causal = jnp.tril(jnp.ones((T, T), dtype=bool))
        att = jnp.where(causal, att, -jnp.inf)
        att = jax.nn.softmax(att, axis=-1)
        lam1 = jnp.exp(jnp.sum(lambda_q1 * lambda_k1))
        lam2 = jnp.exp(jnp.sum(lambda_q2 * lambda_k2))
        lambda_full = lam1 - lam2 + LAMBDA_INIT
        att = att.reshape(B, H, 2, T, T)
        att = att[:, :, 0] - lambda_full * att[:, :, 1]
        out = jnp.einsum('bhts,bhsd->bhtd', att, v)
        rms = jax.lax.rsqrt(jnp.mean(out * out, axis=-1, keepdims=True) + EPS)
        out = out * rms * gamma
        out = (1.0 - LAMBDA_INIT) * out
        out = out.transpose(0, 2, 1, 3).reshape(B, T, C)
        return out @ w_proj

    def _L0_ffn_ref(x, Wg, We_gate, We_up, We_down, Ws_gate, Ws_up, Ws_down, Wsg):
        import jax, jax.numpy as jnp
        import numpy as np
        DIM = 256
        MOE_HID = 128
        SHARED_HID = 512
        N_EXPERTS = 16
        TOP_K = 2
        NORM_TOPK_PROB = True
        B, S, D = x.shape
        xt = x.reshape(-1, D)
        gates = jax.nn.softmax(xt @ Wg.T, axis=-1)
        scores, inds = jax.lax.top_k(gates, TOP_K)
        if NORM_TOPK_PROB:
            scores = scores / jnp.sum(scores, axis=-1, keepdims=True)
        g = jnp.einsum('td,ehd->teh', xt, We_gate)
        u = jnp.einsum('td,ehd->teh', xt, We_up)
        h = jax.nn.silu(g) * u
        y_all = jnp.einsum('teh,edh->ted', h, We_down)
        y_sel = jnp.take_along_axis(y_all, inds[:, :, None], axis=1)
        y = jnp.sum(y_sel * scores[:, :, None], axis=1)
        shared = jax.nn.silu(xt @ Ws_gate.T) * (xt @ Ws_up.T) @ Ws_down.T
        y = y + jax.nn.sigmoid(xt @ Wsg.T) * shared
        return y.reshape(B, S, D)
    h = _L0_tok_ref(x, L0_tok_W, L0_tok_b)
    h = h + _L0_attn_ref(_layernorm(h, axis=-1), L0_attn_w_attn, L0_attn_w_proj, L0_attn_lambda_q1, L0_attn_lambda_q2, L0_attn_lambda_k1, L0_attn_lambda_k2, L0_attn_gamma)
    h = h + _L0_ffn_ref(_layernorm(h, axis=-1), L0_ffn_Wg, L0_ffn_We_gate, L0_ffn_We_up, L0_ffn_We_down, L0_ffn_Ws_gate, L0_ffn_Ws_up, L0_ffn_Ws_down, L0_ffn_Wsg)
    return h

_drawn_inputs = setup_inputs


def setup_inputs(seed=0):
    import zlib

    import numpy as np

    out = dict(_drawn_inputs(seed))
    spreads = {'L0_attn_gamma': (1.0, 0.2)}
    factors = {'L0_attn_lambda_q1': 3.704,
     'L0_attn_lambda_q2': 6.018,
     'L0_attn_lambda_k1': 7.092,
     'L0_ffn_Wg': 6.968,
     'L0_ffn_We_gate': 6.686,
     'L0_ffn_We_up': 6.469,
     'L0_ffn_We_down': 6.463,
     'L0_ffn_Ws_gate': 4.851,
     'L0_ffn_Ws_up': 4.825,
     'L0_ffn_Ws_down': 4.817,
     'L0_ffn_Wsg': 8.0}
    for name, (base, spread) in spreads.items():
        noise = np.random.default_rng([zlib.crc32(name.encode()), seed]).standard_normal(out[name].shape)
        drawn = base * np.exp(spread * noise) if base else spread * noise
        out[name] = jnp.asarray(drawn.astype(out[name].dtype))
    for name, factor in factors.items():
        out[name] = (out[name] * factor).astype(out[name].dtype)
    return out
```

```python
from contextlib import ExitStack

import concourse.bass as bass
from concourse import mybir

F32 = mybir.dt.float32
F32R = mybir.dt.float32r
BF16 = mybir.dt.bfloat16
I32 = mybir.dt.int32
U32 = mybir.dt.uint32
ALU = mybir.AluOpType
ACT = mybir.ActivationFunctionType
AX = mybir.AxisListType

IMAGES, S, D, PIX = 32, 49, 256, 768
TOK = IMAGES * S
TT = 2 * S
NT = TOK // TT
KP = PIX // 128
KD = D // 128
HP = 8
VW = 34
SLOT = 64
PARTS = 6
QPART = (0, 0, 1, 1, 0, 2)
KPART = (0, 1, 0, 1, 2, 0)
CHUNK = 4 * S
NCHUNK = TOK // CHUNK
E, TOPK, HID, SH_HID = 16, 2, 128, 512
BLK = 128
NBLK = (TOK * TOPK + E * (BLK - 1)) // BLK
SH = 8 * S
NSH = TOK // SH
SB = SH_HID // 128
EGU = E * KD * 2 * HID
WE = EGU + E * D
SGU = SB * KD * 2 * HID
WSH = SGU + SB * D
STG = 1024
EPS = 1e-5
LAMBDA_INIT = 0.8 - 0.6
BIG = -1e30

C_ID = 0
C_UP = C_ID + 128
C_ONE = C_UP + 128
C_SEL = C_ONE + 128
C_MASK = C_SEL + 128
C_RESET = C_MASK + S
C_IOTA = C_RESET + E * NT
C_BLK = C_IOTA + E
C_END = C_BLK + NBLK


def constants():
    import numpy as np
    c = np.zeros((128, C_END), np.float32)
    p = np.arange(128)
    c[:, C_ID:C_ID + 128] = p[:, None] == p[None, :]
    c[:, C_UP:C_UP + 128] = p[:, None] < p[None, :]
    c[:, C_ONE:C_ONE + 128] = 1.0
    c[:S, C_SEL:C_SEL + 128] = p[:S, None] == (p[None, :] % SLOT)
    c[:S, C_MASK:C_MASK + S] = np.where(p[None, :S] > p[:S, None], BIG, 0.0)
    c[:, C_RESET:C_RESET + E * NT] = (np.arange(E * NT) % NT != 0)
    c[:, C_IOTA:C_IOTA + E] = np.arange(E)
    c[:, C_BLK:C_BLK + NBLK] = np.arange(NBLK)
    return c


def build(nc, xt, wt, tb, wa, wp, gam, lam, wg, we, wsh, cst, out):
    ctx = ExitStack()
    with ctx:
        V, A, T, G, SP = nc.vector, nc.scalar, nc.tensor, nc.gpsimd, nc.sync

        def sem(name):
            return ctx.enter_context(nc.semaphore(name))

        def bc(ap, shape):
            return ap.broadcast_to(shape)

        slots_x = nc.dram_tensor("slots_x", (NBLK * BLK, D), F32, kind="Internal").ap()
        slots_y = nc.dram_tensor("slots_y", (NBLK * BLK, D), F32, kind="Internal").ap()
        h2_dram = nc.dram_tensor("h2_dram", (TOK, D), F32, kind="Internal").ap()
        acc_dram = nc.dram_tensor("acc_dram", (TOK, D), F32, kind="Internal").ap()

        def keep(name, shape, dt=F32):
            return ctx.enter_context(nc.sbuf_tensor(name, shape, dt))

        cs = keep("cs", [128, C_END])
        ident = cs[:, C_ID:C_ID + 128]
        eps = keep("eps", [128, 1])
        hn2 = keep("hn2", [TT, NT, D])
        hn2T_h = keep("hn2T_h", [128, KD, TOK], F32R)
        hn2T_l = keep("hn2T_l", [128, KD, TOK], F32R)
        logits = keep("logits", [TT, NT, E + 1])
        slot_u = keep("slot_u", [TT, TOPK, NT], U32)
        w1 = keep("w1", [TT, NT])
        w2 = keep("w2", [TT, NT])
        sig = keep("sig", [TT, NT])
        eid = keep("eid", [1, NBLK], I32)
        one_bf = keep("one_bf", [128, 128], BF16)
        up_bf = keep("up_bf", [128, 128], BF16)

        early = ExitStack()

        def ea(name, shape, dt=F32):
            return early.enter_context(nc.sbuf_tensor(name, shape, dt))

        wa_h = ea("wa_h", [128, KD, 3 * D], F32R)
        wa_l = ea("wa_l", [128, KD, 3 * D], F32R)
        wpr = ea("wpr", [128, 2, D])
        wpg = ea("wpg", [128, 2, D])
        wp_h = ea("wp_h", [128, 2, D], F32R)
        wp_l = ea("wp_l", [128, 2, D], F32R)
        wg_sb = ea("wg_sb", [128, KD, E + 1])
        gam_sb = ea("gam_sb", [128, 1])
        lam_sb = ea("lam_sb", [128, 4, 8])
        lamt = ea("lamt", [128, 2, 8])
        lam2 = ea("lam2", [128, 2])
        laml = ea("laml", [128, 2])
        lamd = ea("lamd", [128, 1])
        neglam = ea("neglam", [128, 1])
        bias = ea("bias", [TT, D])
        h = ea("h", [TT, NT, D])
        mv1 = ea("mv1", [TT, NT, 2])
        mvb = ea("mvb", [TT, 2, 2])
        sd1 = ea("sd1", [TT, NT])
        rs1 = ea("rs1", [TT, NT])
        hT_h = ea("hT_h", [128, KD, TOK], F32R)
        hT_l = ea("hT_l", [128, KD, TOK], F32R)
        vst = ea("vst", [TT, NT, HP, VW])
        vx = [ea(f"vx{n}", [TT, 2, HP * VW]) for n in range(4)]
        sel_bf = ea("sel_bf", [S, 128], BF16)
        mask_bf = ea("mask_bf", [S, 8, S], BF16)
        zero = ea("zero", [128, 1280])
        first = ExitStack()

        def fa(name, shape, dt=F32):
            return first.enter_context(nc.sbuf_tensor(name, shape, dt))

        wraw = fa("wraw", [128, KP * D])
        wt_h = fa("wt_h", [128, KP, D], F32R)
        wt_l = fa("wt_l", [128, KP, D], F32R)
        war = fa("war", [128, KD, 3 * D])
        xr = [fa(f"xr{n}", [128, KP, TT]) for n in range(2)]
        x_h = [fa(f"x_h{n}", [128, KP, TT], F32R) for n in range(2)]
        x_l = [fa(f"x_l{n}", [128, KP, TT], F32R) for n in range(2)]
        st1 = fa("st1", [TT, 2, 6])
        hn = [fa(f"hn{n}", [TT, D]) for n in range(2)]
        first.close()
        parts = ea("parts", [128, 4, 3, CHUNK], BF16)
        rest = [ea(f"rest{n}", [128, CHUNK]) for n in range(2)]
        Qs = [ea(f"Qs{n}", [112, 2 * HP, CHUNK], BF16) for n in range(2)]
        Ks = [ea(f"Ks{n}", [112, 2 * HP, CHUNK], BF16) for n in range(2)]
        smax = [ea(f"smax{n}", [128, 8]) for n in range(2)]
        Sm = [ea(f"Sm{n}", [128, 4, TT]) for n in range(2)]
        PT = [ea(f"PT{n}", [TT, 4, 128]) for n in range(2)]
        rz = ea("rz", [128, 8])
        on = ea("on", [128, 8, 16])
        att = [ea(f"att{n}", [128, 2, HP, 16]) for n in range(2)]
        sq = ea("sq", [128, 2 * HP, 16])
        ms = ea("ms", [128, 2 * HP])
        ms2 = ea("ms2", [128, 2 * HP])
        lnr = ea("lnr", [128, 2 * HP])
        r0 = ea("r0", [128, 2 * HP])
        nt1 = ea("nt1", [128, 2 * HP])
        nt2 = ea("nt2", [128, 2 * HP])
        nt3 = ea("nt3", [128, 2 * HP])
        rr = ea("rr", [128, 2 * HP])
        ao = ea("ao", [128, 2, HP, 16])
        aT_h = ea("aT_h", [128, 2, 2, S], F32R)
        aT_l = ea("aT_l", [128, 2, 2, S], F32R)
        h2 = [ea(f"h2{n}", [TT, D]) for n in range(2)]
        hn2w = [ea(f"hn2w{n}", [TT, D]) for n in range(2)]
        st2 = ea("st2", [TT, 6])
        mv2 = ea("mv2", [TT, 2])
        ve2 = ea("ve2", [TT, 1])
        ln2 = ea("ln2", [TT, 1])
        q0 = ea("q0", [TT, 1])
        q1 = ea("q1", [TT, 1])
        q2 = ea("q2", [TT, 1])
        q3 = ea("q3", [TT, 1])
        rs2 = ea("rs2", [TT, 1])
        h2T = ea("h2T", [128, KD, TT])
        early.close()

        def la(name, shape, dt=F32):
            return ctx.enter_context(nc.sbuf_tensor(name, shape, dt))

        we_h = la("we_h", [128, WE], F32R)
        we_l = la("we_l", [128, WE], F32R)
        h2r = [la(f"h2r{n}", [TT, D]) for n in range(2)]
        acc = [la(f"acc{n}", [TT, D]) for n in range(2)]

        middle = ExitStack()

        def ma(name, shape, dt=F32):
            return middle.enter_context(nc.sbuf_tensor(name, shape, dt))

        stg = [ma(f"stg{n}", [128, STG]) for n in range(3)]
        wsh_h = ma("wsh_h", [128, WSH], F32R)
        wsh_l = ma("wsh_l", [128, WSH], F32R)
        sgl = ma("sgl", [128, SH])
        hs = ma("hs", [128, SH])
        with nc.sbuf_tensor("ecmp", [1, NBLK, E], F32) as ecmp:
            pass
        hs_h = ma("hs_h", [128, SB, SH], F32R)
        hs_l = ma("hs_l", [128, SB, SH], F32R)
        mx8 = ma("mx8", [TT, NT, 8])
        ix8 = ma("ix8", [TT, NT, 8], U32)
        ixf = ma("ixf", [TT, TOPK, NT])
        oh = ma("oh", [TT, TOPK, E, NT])
        both = ma("both", [TT, E, NT], BF16)
        cuminc = ma("cuminc", [TT, E, NT])
        excl = ma("excl", [TT, E, NT])
        cnt = ma("cnt", [TT, E], I32)
        cnts = ma("cnts", [TT, E], I32)
        nblk = ma("nblk", [TT, E])
        cumb = ma("cumb", [TT, E])
        base = ma("base", [TT, E])
        slotf = ma("slotf", [TT, E, NT])
        slot2 = ma("slot2", [TT, E, NT])
        pick = ma("pick", [TT, E, NT])
        slotr = ma("slotr", [TT, TOPK, NT])
        esum = ma("esum", [1, NBLK])
        dl = ma("dl", [TT, NT])
        ed = ma("ed", [TT, NT])
        ed1 = ma("ed1", [TT, NT])
        ez = ma("ez", [TT, NT])
        ez1 = ma("ez1", [TT, NT])
        middle.close()

        bx = [la(f"bx{n}", [BLK, D]) for n in range(2)]
        bxT_h = [la(f"bxT_h{n}", [128, KD, BLK], F32R) for n in range(2)]
        bxT_l = [la(f"bxT_l{n}", [128, KD, BLK], F32R) for n in range(2)]
        bsg = [la(f"bsg{n}", [BLK, HID]) for n in range(2)]
        bh = [la(f"bh{n}", [BLK, HID]) for n in range(2)]
        bhT_h = [la(f"bhT_h{n}", [HID, BLK], F32R) for n in range(2)]
        bhT_l = [la(f"bhT_l{n}", [HID, BLK], F32R) for n in range(2)]
        by = [la(f"by{n}", [BLK, D]) for n in range(2)]
        y1 = [la(f"y1{n}", [TT, D]) for n in range(2)]
        y2 = [la(f"y2{n}", [TT, D]) for n in range(2)]
        psum1 = [la(f"psum1{n}", [TT, D]) for n in range(2)]
        fin = [la(f"fin{n}", [TT, D]) for n in range(2)]

        bank = [ctx.enter_context(nc.psum_tensor(f"bank{n}", [128, 512], F32)) for n in range(8)]

        cst_in = sem("cst_in")
        wt_in = sem("wt_in")
        wa_in = sem("wa_in")
        wp_in = sem("wp_in")
        small_in = sem("small_in")
        x_in = [sem(f"x_in{n}") for n in range(2)]
        init_done = sem("init_done")
        pool_init = sem("pool_init")
        zeroed = sem("zeroed")
        wt_hi, wt_lo = sem("wt_hi"), sem("wt_lo")
        x_hi, x_lo = sem("x_hi"), sem("x_lo")
        embedded = sem("embedded")
        h_done, stat_done = sem("h_done"), sem("stat_done")
        h_stats, h_aggr = sem("h_stats"), sem("h_aggr")
        sd_done, rs_done = sem("sd_done"), sem("rs_done")
        hn_done, hn_turned, hT_hi, hT_lo = sem("hn_done"), sem("hn_turned"), sem("hT_hi"), sem("hT_lo")
        wa_hi, wa_lo, wp_g, wp_hi, wp_lo = sem("wa_hi"), sem("wa_lo"), sem("wp_g"), sem("wp_hi"), sem("wp_lo")
        lam_a, lam_b, lam_c, lam_d, lam_e = (sem(f"lam_{n}") for n in "abcde")
        v_made, v_kept = sem("v_made"), sem("v_kept")
        qk_made, part0, rest1, part1, part2 = (sem(n) for n in ("qk_made", "part0", "rest1", "part1", "part2"))
        stacked = [sem(f"stacked{n}") for n in range(2)]
        vx_in = [sem(f"vx_in{n}") for n in range(4)]
        scored, maxed, centred, turned, exped, weighed = (
            sem(n) for n in ("scored", "maxed", "centred", "turned", "exped", "weighed"))
        rz_done, on_done, att_done = sem("rz_done"), sem("on_done"), sem("att_done")
        sq_done, ms_done, ms2_done, ln_done, r0_done = (
            sem(n) for n in ("sq_done", "ms_done", "ms2_done", "ln_done", "r0_done"))
        newton = sem("newton")
        ao_done, ao_turned, aT_hi, aT_lo, projected = (
            sem(n) for n in ("ao_done", "ao_turned", "aT_hi", "aT_lo", "projected"))
        h2_done, st2_done, mv2_done, ve2_done, ln2_done, q0_done = (
            sem(n) for n in ("h2_done", "st2_done", "mv2_done", "ve2_done", "ln2_done", "q0_done"))
        hn2_kept = sem("hn2_kept")
        newton2, hn2_done, hn2_turned, h2T_done, h2T_hi, h2T_lo = (
            sem(n) for n in ("newton2", "hn2_done", "hn2_turned", "h2T_done", "h2T_hi", "h2T_lo"))
        gated, logit_done = sem("gated"), sem("logit_done")
        h2_out = [sem(f"h2_out{n}") for n in range(2)]
        gate_diff, slots_known, eids_known, weights_known, routing = (
            sem(n) for n in ("gate_diff", "slots_known", "eids_known", "weights_known", "routing"))
        chosen = sem("chosen")
        counted, e_exp = sem("counted"), sem("e_exp")
        scattered = sem("scattered")
        stg_in = [sem(f"stg_in{n}") for n in range(3)]
        w_hi, w_lo = sem("w_hi"), sem("w_lo")
        sh_g, sh_u, sh_silu, sh_h, sh_hi, sh_lo, sh_y, sh_acc = (
            sem(n) for n in ("sh_g", "sh_u", "sh_silu", "sh_h", "sh_hi", "sh_lo", "sh_y", "sh_acc"))
        h2_in = [sem(f"h2_in{n}") for n in range(2)]
        acc_out = [sem(f"acc_out{n}") for n in range(2)]
        bx_in = [sem(f"bx_in{n}") for n in range(2)]
        b_turned, b_hi, b_lo, b_gu, b_silu, b_h, b_hturned, b_hhi, b_hlo, b_y, b_ykept = (
            sem("b_" + n) for n in ("turned", "hi", "lo", "gu", "silu", "h", "hturned", "hhi", "hlo", "y", "ykept"))
        by_out = [sem(f"by_out{n}") for n in range(2)]
        acc_in = [sem(f"acc_in{n}") for n in range(2)]
        y_in = [sem(f"y_in{n}") for n in range(2)]
        part_sum, fin_done = sem("part_sum"), sem("fin_done")
        fin_out = [sem(f"fin_out{n}") for n in range(2)]

        def need(eng, s, value):
            if isinstance(value, int) and value <= 0:
                return
            eng.wait_ge(s, value)

        NZ = NBLK * BLK // (128 * 5)
        assert NZ == NT // 2
        NW, NS = WE // STG, WSH // STG

        def blocks(eng, steps):
            def turn(b, par):
                for ahead, step in steps:
                    if isinstance(b, int) and not 0 <= b + ahead < NBLK:
                        continue
                    step(b + ahead, (par + ahead) % 2)
            for b in range(-1, 4):
                turn(b, b % 2)
            with eng.Fori(2, NBLK // 2 - 1) as t:
                turn(2 * t, 0)
                turn(2 * t + 1, 1)
            for b in range(NBLK - 2, NBLK + 2):
                turn(b, b % 2)

        POSTS = {0: [("P", -2)], 1: [("N", -2)], 2: [("G", -2), ("R", -1)], 3: [("A", -1)],
                 4: [("P", -1)], 5: [("N", -1)], 6: [("G", -1), ("R", 0)], 7: [("A", 0)]}

        def attention(eng, lag0=None, lag1=None, lag2=None, qk=None, post=None):
            def at(step, c, k, cc):
                if k < 0:
                    c, k, cc = c - 1, k + 8, 1 - cc
                if step and not (isinstance(c, int) and not 0 <= c < NCHUNK):
                    step(c, k, cc)

            def chunk(c, cc, last=False):
                for k in range(8):
                    at(lag0, c, k, cc)
                    at(lag1, c, k - 1, cc)
                    at(lag2, c, k - 2, cc)
                    if qk and k < 4 and not last:
                        qk(c + 1, k, 1 - cc)
                    for what, ahead in POSTS[k]:
                        tile = 2 * c + ahead
                        if post and not (isinstance(tile, int) and tile < 0):
                            post(what, tile, ahead % 2, c, k, last)

            chunk(0, 0)
            chunk(1, 1)
            with eng.Fori(1, NCHUNK // 2 - 1) as s:
                chunk(2 * s, 0)
                chunk(2 * s + 1, 1)
            chunk(NCHUNK - 2, 0)
            chunk(NCHUNK - 1, 1, last=True)
            at(lag1, NCHUNK - 1, 7, 1)
            at(lag2, NCHUNK - 1, 6, 1)
            at(lag2, NCHUNK - 1, 7, 1)
            if post:
                for what, tile in (("P", NT - 2), ("N", NT - 2), ("G", NT - 2), ("R", NT - 1), ("A", NT - 1),
                                   ("P", NT - 1), ("N", NT - 1), ("G", NT - 1)):
                    post(what, tile, tile % 2, NCHUNK - 1, 8, True)

        block = ctx.enter_context(nc.Block())

        @block.sync
        def _(sp):
            sp.dma_start(wraw[:], wt).then_inc(wt_in, 16)

            def row(value):
                return value if isinstance(value, int) else sp.snap(value)

            def load_x(i, b):
                r = row(i * 128)
                need(sp, x_lo, i - 1)
                need(sp, x_hi, i - 1)
                sp.dma_start(xr[b][:].rearrange("p k t -> p (k t)"), xt[bass.ds(r, 128), :]).then_inc(x_in[b], 16)

            load_x(0, 0)
            load_x(1, 1)
            sp.dma_start(cs[:], cst).then_inc(cst_in, 16)
            sp.dma_start(bias[:], tb.broadcast_to([TT, D])).then_inc(small_in, 16)
            sp.dma_start(gam_sb[:], gam).then_inc(small_in, 16)
            sp.dma_start(lam_sb[:], lam.broadcast_to([128, 4, 8])).then_inc(small_in, 16)
            sp.dma_start(wg_sb[:], wg).then_inc(small_in, 16)
            with sp.Fori(1, NT // 2) as t:
                load_x(2 * t, 0)
                load_x(2 * t + 1, 1)
            sp.dma_start(war[:], wa).then_inc(wa_in, 16)
            sp.dma_start(wpr[:], wp).then_inc(wp_in, 16)

            def load_vx(n, c):
                tile = row(2 * c + n // 2)
                free = row(8 * c - 6 + 2 * n)
                sp.wait_ge(v_kept, NT)
                need(sp, weighed, free)
                r = 49 * (n % 2)
                for j in range(2):
                    sp.dma_start(vx[n][49 * j:49 * j + 49, j, :],
                                 vst[r:r + 49, bass.ds(tile, 1), :, :].rearrange("p a b c -> p (a b c)")).then_inc(vx_in[n], 16)

            def stack(c, cc):
                free = row(8 * (c - 1))
                for m in range(4):
                    dst = (Qs, Ks)[m // 2][cc]
                    jj = m % 2
                    made = row(4 * c + m + 1)
                    if m == 0:
                        need(sp, scored, free)
                    sp.wait_ge(part2, made)
                    sp.wait_ge(part1, made)
                    for r, part in enumerate((QPART, KPART)[m // 2]):
                        at_row = SLOT * jj + 8 * r
                        sp.dma_start(dst[at_row:at_row + 8, :, :], parts[:, m, part, :]).then_inc(stacked[cc], 16)

            sp.wait_ge(init_done, 1)
            stack(0, 0)
            for n in range(4):
                load_vx(n, 0)

            def chunk(c, cc, last=False):
                if not last:
                    stack(c + 1, 1 - cc)
                for p in range(2):
                    if not (isinstance(c, int) and c == 0):
                        store_h2(2 * c - 2 + p, p)
                    if not last:
                        load_vx(2 * p, c + 1)
                        load_vx(2 * p + 1, c + 1)

            def store_h2(pair, b):
                r = row(pair * TT)
                sp.wait_ge(h2_done, pair + 1)
                sp.dma_start(h2_dram[bass.ds(r, TT), :], h2[b][:]).then_inc(h2_out[b], 16)

            chunk(0, 0)
            chunk(1, 1)
            with sp.Fori(1, NCHUNK // 2 - 1) as s:
                chunk(2 * s, 0)
                chunk(2 * s + 1, 1)
            chunk(NCHUNK - 2, 0)
            chunk(NCHUNK - 1, 1, last=True)
            store_h2(NT - 2, 0)
            store_h2(NT - 1, 1)

            sp.wait_ge(logit_done, NT)
            for b in range(2):
                sp.wait_ge(h2_out[b], 16 * NT // 2)

            def stage(n, b, weights, at):
                at = row(at)
                need(sp, w_lo, n - 2)
                sp.dma_start(stg[b][:], weights[:, bass.ds(at, STG)]).then_inc(stg_in[b], 16)

            def load_h2r(t, b):
                r = row(t * TT)
                need(sp, sh_acc, t - 1)
                sp.dma_start(h2r[b][:], h2_dram[bass.ds(r, TT), :]).then_inc(h2_in[b], 16)

            def store_acc(t, b):
                r = row(t * TT)
                sp.wait_ge(sh_acc, t + 1)
                sp.dma_start(acc_dram[bass.ds(r, TT), :], acc[b][:]).then_inc(acc_out[b], 16)

            def shared(c, last=False):
                for j in range(NW // NSH):
                    n = NW // NSH * c + j
                    stage(NS + n, j, we, n * STG)
                for tt in range(4):
                    if not (last and tt >= 2):
                        load_h2r(4 * c + tt + 2, tt % 2)
                    store_acc(4 * c + tt, tt % 2)

            for n in range(NS):
                stage(n, n, wsh, n * STG)
            load_h2r(0, 0)
            load_h2r(1, 1)
            with sp.Fori(0, NSH - 1) as c:
                shared(c)
            shared(NSH - 1, last=True)

            def load_block(b, par):
                r = row(b * BLK)
                need(sp, b_turned, b - 1)
                sp.dma_start(bx[par][:], slots_x[bass.ds(r, BLK), :]).then_inc(bx_in[par], 16)

            def store_block(b, par):
                r = row(b * BLK)
                sp.wait_ge(b_ykept, b + 1)
                sp.dma_start(slots_y[bass.ds(r, BLK), :], by[par][:]).then_inc(by_out[par], 16)

            sp.wait_ge(scattered, 16 * TOPK * NT)
            for b in range(4):
                load_block(b, b % 2)
            with sp.Fori(0, NBLK // 2 - 2) as t:
                store_block(2 * t, 0)
                load_block(2 * t + 4, 0)
                store_block(2 * t + 1, 1)
                load_block(2 * t + 5, 1)
            for b in range(NBLK - 4, NBLK):
                store_block(b, b % 2)

            def load_acc(t, par):
                r = row(t * TT)
                need(sp, part_sum, t - 1)
                sp.dma_start(h2r[par][:], acc_dram[bass.ds(r, TT), :]).then_inc(acc_in[par], 16)

            def store_out(t, par):
                r = row(t * TT)
                sp.wait_ge(fin_done, t + 1)
                sp.dma_start(out[bass.ds(r, TT), :], fin[par][:]).then_inc(fin_out[par], 16)

            for p in range(2):
                sp.wait_ge(acc_out[p], 16 * NT // 2)
            load_acc(0, 0)
            load_acc(1, 1)
            with sp.Fori(0, NT // 2 - 1) as t:
                load_acc(2 * t + 2, 0)
                store_out(2 * t, 0)
                load_acc(2 * t + 3, 1)
                store_out(2 * t + 1, 1)
            store_out(NT - 2, 0)
            store_out(NT - 1, 1)
            sp.wait_ge(fin_out[0], 16 * NT // 2)
            sp.wait_ge(fin_out[1], 16 * NT // 2)

        @block.gpsimd
        def _(pool):
            G.memset(zero[:], 0.0).then_inc(pool_init, 1)
            G.memset(eps[:], EPS).then_inc(pool_init, 1)
            for n in range(4):
                G.memset(vx[n][:], 0.0).then_inc(pool_init, 1)
            G.memset(vst[:], 1.0).then_inc(pool_init, 1)

            zx = slots_x.rearrange("(n p r) d -> n p (r d)", p=128, r=5)

            def norm_tile(tile, b):
                pool.wait_ge(att_done, 4 * tile + 4)
                need(pool, ms_done, tile)
                a = att[b][:].rearrange("p i h d -> p (i h) d")
                G.tensor_tensor(sq[:], a, a, ALU.mult).then_inc(sq_done, 1)
                pool.wait_ge(newton, 4 * tile + 4)
                need(pool, ao_turned, tile)
                G.tensor_tensor(ao[:].rearrange("p i h d -> p (i h) d"), a,
                                bc(rr[:].unsqueeze(2), [128, 2 * HP, 16]), ALU.mult).then_inc(ao_done, 1)

            pool.wait_ge(pool_init, 7)
            with pool.Fori(0, NZ) as t:
                G.dma_start(zx[bass.ds(t, 1)].rearrange("a p n -> (a p) n"), zero[:]).then_inc(zeroed, 16)
                norm_tile(2 * t, 0)
                norm_tile(2 * t + 1, 1)
            pool.wait_ge(slots_known, 1)
            pool.wait_ge(zeroed, 16 * NZ)
            for k in range(TOPK):
                for i in range(NT):
                    G.indirect_dma_start(out=slots_x, out_offset=bass.IndirectOffsetOnAxis(ap=slot_u[:, k, i:i + 1], axis=0),
                                         in_=hn2[:, i, :], in_offset=None).then_inc(scattered, 16)
            for p in range(2):
                pool.wait_ge(by_out[p], 16 * NBLK // 2)
            for i in range(NT):
                if i >= 2:
                    pool.wait_ge(fin_done, i - 1)
                for k, y in enumerate((y1, y2)):
                    G.indirect_dma_start(out=y[i % 2][:], out_offset=None, in_=slots_y,
                                         in_offset=bass.IndirectOffsetOnAxis(ap=slot_u[:, k, i:i + 1], axis=0)).then_inc(y_in[i % 2], 16)

        @block.scalar
        def _(act):
            act.wait_ge(wt_in, 16)
            A.activation(wt_h[:].rearrange("p k n -> p (k n)"), wraw[:], ACT.Copy).then_inc(wt_hi, 1)

            def split_x(i, b):
                act.wait_ge(x_in[b], 8 * i + 16 - 8 * b)
                need(act, embedded, i - 1)
                A.activation(x_h[b][:], xr[b][:], ACT.Copy).then_inc(x_hi, 1)

            split_x(0, 0)
            split_x(1, 1)
            with act.Fori(1, NT // 2) as t:
                split_x(2 * t, 0)
                split_x(2 * t + 1, 1)
            act.wait_ge(wa_in, 16)
            A.activation(wa_h[:], war[:], ACT.Copy).then_inc(wa_hi, 1)
            act.wait_ge(lam_b, 1)
            A.activation(laml[:], lam2[:], ACT.Exp).then_inc(lam_c, 1)
            act.wait_ge(stat_done, NT)
            act.wait_ge(pool_init, 2)
            A.activation(sd1[:], mv1[:, :, 1], ACT.Sqrt, bias=eps[0:TT, :]).then_inc(sd_done, 1)

            def keep_hT(i, b):
                act.wait_ge(hn_turned, i + 1)
                A.activation(hT_h[:, :, bass.ds(i * TT, TT)],
                             bank[4 + b][:, 0:KD * TT].rearrange("p (k t) -> p k t", k=KD), ACT.Copy).then_inc(hT_hi, 1)

            with act.Fori(0, NT // 2) as t:
                keep_hT(2 * t, 0)
                keep_hT(2 * t + 1, 1)
            act.wait_ge(wp_g, 1)
            A.activation(wp_h[:], wpg[:], ACT.Copy).then_inc(wp_hi, 1)

            def qk(c, m, cc):
                act.wait_ge(qk_made, 4 * c + m + 1)
                need(act, stacked[1 - cc], 192 * (c + cc))
                A.activation(parts[:, m, 0, :], bank[6 + m % 2][:, 0:CHUNK], ACT.Copy,
                             scale=0.125 if m < 2 else 1.0).then_inc(part0, 1)
                act.wait_ge(rest1, 4 * c + m + 1)
                A.activation(parts[:, m, 1, :], rest[m % 2][:], ACT.Copy).then_inc(part1, 1)

            for m in range(4):
                qk(0, m, 0)
            act.wait_ge(pool_init, 7)
            for i in range(NT):
                act.wait_ge(v_made, i + 1)
                A.activation(vst[:, i, :, 0:32], bank[4 + i % 2][0:TT, 0:D].rearrange("p (h n) -> p h n", h=HP),
                             ACT.Copy).then_inc(v_kept, 1)

            def exp_half(c, k, cc):
                u, b = 8 * c + k, k % 2
                act.wait_ge(turned, u + 1)
                need(act, weighed, u - 1)
                A.activation(PT[b][:].rearrange("p a t -> p (a t)"), bank[2 + b][0:TT, :], ACT.Exp).then_inc(exped, 1)

            def post(what, tile, b, c, k, last):
                if what == "R":
                    act.wait_ge(ms2_done, tile + 1)
                    A.activation(lnr[:], ms2[:], ACT.Ln).then_inc(ln_done, 1)
                    act.wait_ge(ln_done, tile + 1)
                    need(act, newton, 4 * tile)
                    A.activation(r0[:], lnr[:], ACT.Exp, scale=-0.5).then_inc(r0_done, 1)
                elif what == "A":
                    act.wait_ge(ao_turned, tile + 1)
                    need(act, projected, tile)
                    A.activation(aT_h[:], bank[6][:, 0:256].rearrange("p (i j t) -> p j i t", i=2, j=2)[:, :, :, 0:S],
                                 ACT.Copy).then_inc(aT_hi, 1)
                elif what == "P":
                    act.wait_ge(ve2_done, tile + 1)
                    A.activation(ln2[:], ve2[:], ACT.Ln).then_inc(ln2_done, 1)
                    act.wait_ge(ln2_done, tile + 1)
                    need(act, newton2, 4 * tile)
                    A.activation(q0[:], ln2[:], ACT.Exp, scale=-0.5).then_inc(q0_done, 1)
                elif what == "N":
                    act.wait_ge(hn2_done, tile + 1)
                    A.activation(hn2[:, bass.ds(tile, 1), :].rearrange("p a n -> p (a n)"), hn2w[b][:], ACT.Copy).then_inc(hn2_kept, 1)
                    act.wait_ge(hn2_turned, tile + 1)
                    need(act, h2T_lo, tile)
                    need(act, gated, tile)
                    A.activation(h2T[:].rearrange("p k t -> p (k t)"), bank[6][:, 0:KD * TT], ACT.Copy).then_inc(h2T_done, 1)

            attention(act, lag1=exp_half, qk=qk, post=post)

            act.wait_ge(gate_diff, 1)
            A.activation(ed[:], dl[:], ACT.Exp).then_inc(e_exp, 1)
            A.activation(ez[:], logits[:, :, E], ACT.Exp, scale=-1.0).then_inc(e_exp, 1)

            def split_hi(n, b, dst):
                act.wait_ge(stg_in[b], 16 * ((n - b) // 3 + 1) if isinstance(n, int) else 16 * (n + 1))
                A.activation(dst, stg[b][:], ACT.Copy).then_inc(w_hi, 1)

            for n in range(NS):
                split_hi(n, n, wsh_h[:, n * STG:(n + 1) * STG])
            with act.Fori(0, NSH) as c:
                for b in range(SB):
                    u = SB * c + b
                    act.wait_ge(sh_g, u + 1)
                    act.wait_ge(sh_h, u)
                    A.activation(sgl[:], bank[(2 * b) % 4][:, 0:SH], ACT.Silu).then_inc(sh_silu, 1)
                    act.wait_ge(sh_h, u + 1)
                    act.wait_ge(sh_y, 4 * c)
                    A.activation(hs_h[:, b, :], hs[:], ACT.Copy).then_inc(sh_hi, 1)
                    if b < NW // NSH:
                        act.wait_ge(stg_in[b], 16 * c + 32)
                        A.activation(we_h[:, bass.ds((NW // NSH * c + b) * STG, STG)], stg[b][:], ACT.Copy).then_inc(w_hi, 1)

            def block_hi(b, par):
                act.wait_ge(b_turned, b + 1)
                need(act, b_gu, b - 1)
                A.activation(bxT_h[par][:].rearrange("p k t -> p (k t)"), bank[par][:, 0:D], ACT.Copy).then_inc(b_hi, 1)

            def block_silu(b, par):
                act.wait_ge(b_gu, b + 1)
                need(act, b_h, b - 1)
                A.activation(bsg[par][:], bank[2 + par][:, 0:HID], ACT.Silu).then_inc(b_silu, 1)

            def block_hhi(b, par):
                act.wait_ge(b_hturned, b + 1)
                need(act, b_y, b - 1)
                A.activation(bhT_h[par][:], bank[4 + par][:, 0:BLK], ACT.Copy).then_inc(b_hhi, 1)

            def block_keep(b, par):
                act.wait_ge(b_y, b + 1)
                need(act, by_out[par], 8 * b - 8 * par)
                A.activation(by[par][:], bank[6 + par][:, 0:D], ACT.Copy).then_inc(b_ykept, 1)

            blocks(act, [(1, block_hi), (0, block_silu), (-1, block_hhi), (-2, block_keep)])

        @block.vector
        def _(dve):
            dve.wait_ge(wt_hi, 1)
            V.tensor_tensor(wt_l[:].rearrange("p k n -> p (k n)"), wraw[:],
                            wt_h[:].rearrange("p k n -> p (k n)").bitcast(F32), ALU.subtract).then_inc(wt_lo, 1)

            def split_x(i, b):
                dve.wait_ge(x_hi, i + 1)
                need(dve, embedded, i - 1)
                V.tensor_tensor(x_l[b][:], xr[b][:], x_h[b][:].bitcast(F32), ALU.subtract).then_inc(x_lo, 1)

            def embed_out(i, b):
                dve.wait_ge(embedded, i + 1)
                V.tensor_tensor(h[:, bass.ds(i, 1), :].rearrange("p a n -> p (a n)"), bank[6 + b][0:TT, 0:D], bias[:], ALU.add).then_inc(h_done, 1)
                dve.wait_ge(small_in, 64)
                dve.wait_ge(h_done, i + 1)
                V.bn_stats(st1[:, b, :], h[:, bass.ds(i, 1), :].rearrange("p a n -> p (a n)")).then_inc(h_stats, 1)
                dve.wait_ge(small_in, 64)
                dve.wait_ge(h_stats, i + 1)
                V.bn_aggr(mvb[:, b, :], st1[:, b, :]).then_inc(h_aggr, 1)
                dve.wait_ge(h_aggr, i + 1)
                V.tensor_copy(mv1[:, bass.ds(i, 1), :].rearrange("p a n -> p (a n)"), mvb[:, b, :]).then_inc(stat_done, 1)

            split_x(0, 0)
            dve.wait_ge(small_in, 64)
            with dve.Fori(0, NT // 2 - 1) as t:
                split_x(2 * t + 1, 1)
                embed_out(2 * t, 0)
                split_x(2 * t + 2, 0)
                embed_out(2 * t + 1, 1)
            split_x(NT - 1, 1)
            embed_out(NT - 2, 0)
            embed_out(NT - 1, 1)

            dve.wait_ge(wa_hi, 1)
            V.tensor_tensor(wa_l[:], war[:], wa_h[:].bitcast(F32), ALU.subtract).then_inc(wa_lo, 1)
            V.tensor_tensor(lamt[:], lam_sb[:, 0:2, :], lam_sb[:, 2:4, :], ALU.mult).then_inc(lam_a, 1)
            dve.wait_ge(lam_a, 1)
            V.tensor_reduce(lam2[:], lamt[:], AX.X, ALU.add).then_inc(lam_b, 1)
            dve.wait_ge(lam_c, 1)
            V.tensor_tensor(lamd[:], laml[:, 1:2], laml[:, 0:1], ALU.subtract).then_inc(lam_d, 1)
            dve.wait_ge(lam_d, 1)
            V.tensor_scalar(neglam[:], lamd[:], -LAMBDA_INIT, None, ALU.add).then_inc(lam_e, 1)
            dve.wait_ge(wp_in, 16)
            V.tensor_scalar(wpg[:], wpr[:], gam_sb[:], 1.0 - LAMBDA_INIT, ALU.mult, ALU.mult).then_inc(wp_g, 1)
            dve.wait_ge(cst_in, 16)
            V.tensor_copy(sel_bf[:], cs[0:S, C_SEL:C_SEL + 128]).then_inc(init_done, 1)
            V.tensor_copy(mask_bf[:], bc(cs[0:S, C_MASK:C_MASK + S].unsqueeze(1), [S, 8, S])).then_inc(init_done, 1)
            V.tensor_copy(one_bf[:], cs[:, C_ONE:C_ONE + 128]).then_inc(init_done, 1)
            V.tensor_copy(up_bf[:], cs[:, C_UP:C_UP + 128]).then_inc(init_done, 1)

            dve.wait_ge(sd_done, 1)
            V.reciprocal(rs1[:], sd1[:]).then_inc(rs_done, 1)
            dve.wait_ge(rs_done, 1)

            def norm(i, b):
                need(dve, hn_turned, i - 1)
                V.tensor_scalar(hn[b][:], h[:, bass.ds(i, 1), :].rearrange("p a n -> p (a n)"),
                                mv1[:, bass.ds(i, 1), 0], rs1[:, bass.ds(i, 1)],
                                ALU.subtract, ALU.mult).then_inc(hn_done, 1)

            def keep_lo(i, b):
                dve.wait_ge(hT_hi, i + 1)
                V.tensor_tensor(hT_l[:, :, bass.ds(i * TT, TT)],
                                bank[4 + b][:, 0:KD * TT].rearrange("p (k t) -> p k t", k=KD),
                                hT_h[:, :, bass.ds(i * TT, TT)].bitcast(F32), ALU.subtract).then_inc(hT_lo, 1)

            norm(0, 0)
            with dve.Fori(0, NT // 2 - 1) as t:
                norm(2 * t + 1, 1)
                keep_lo(2 * t, 0)
                norm(2 * t + 2, 0)
                keep_lo(2 * t + 1, 1)
            norm(NT - 1, 1)
            keep_lo(NT - 2, 0)
            keep_lo(NT - 1, 1)
            dve.wait_ge(wp_hi, 1)
            V.tensor_tensor(wp_l[:], wpg[:], wp_h[:].bitcast(F32), ALU.subtract).then_inc(wp_lo, 1)

            def qk(c, m, cc):
                scale = 0.125 if m < 2 else 1.0
                dve.wait_ge(part0, 4 * c + m + 1)
                V.scalar_tensor_tensor(rest[m % 2][:], bank[6 + m % 2][:, 0:CHUNK], scale, parts[:, m, 0, :],
                                       ALU.mult, ALU.subtract).then_inc(rest1, 1)
                dve.wait_ge(part1, 4 * c + m + 1)
                V.tensor_tensor(parts[:, m, 2, :], rest[m % 2][:], parts[:, m, 1, :], ALU.subtract).then_inc(part2, 1)

            for m in range(4):
                qk(0, m, 0)

            def centre(c, k, cc):
                u, b = 8 * c + k, k % 2
                s3 = bank[b][:, 0:8 * S].rearrange("p (m s) -> p m s", m=8)
                dve.wait_ge(scored, u + 1)
                V.tensor_reduce(smax[b][:], s3, AX.X, ALU.max).then_inc(maxed, 1)
                dve.wait_ge(maxed, u + 1)
                need(dve, turned, u - 1)
                V.tensor_tensor(Sm[b][:].rearrange("p m (j s) -> p (m j) s", j=2), s3,
                                bc(smax[b][:].unsqueeze(2), [128, 8, S]), ALU.subtract).then_inc(centred, 1)

            dve.wait_ge(lam_e, 1)

            def epilogue(c, k, cc):
                u, b, tile, tb_, img = 8 * c + k, k % 2, 2 * c + k // 4, k // 4, k // 2 % 2
                O = bank[4 + b][:, 0:4 * 2 * VW].rearrange("p (m n) -> p m n", n=VW)
                dve.wait_ge(weighed, u + 1)
                V.reciprocal(rz[:], O[:, :, 32]).then_inc(rz_done, 1)
                dve.wait_ge(rz_done, u + 1)
                for jj in range(2):
                    r = slice(SLOT * jj, SLOT * jj + SLOT)
                    V.tensor_tensor(on[r, :, :], O[r, :, 16 * jj:16 * jj + 16],
                                    bc(rz[r, :].unsqueeze(2), [SLOT, 8, 16]), ALU.mult).then_inc(on_done, 1)
                dve.wait_ge(on_done, 2 * u + 2)
                o4 = on[:].rearrange("p (m j) d -> p m j d", j=2)
                need(dve, ao_done, tile - 1)
                V.scalar_tensor_tensor(att[tb_][:, img, 4 * b:4 * b + 4, :], o4[:, :, 1, :], neglam[:, 0:1], o4[:, :, 0, :],
                                       ALU.mult, ALU.add).then_inc(att_done, 1)

            def newton_step(s, tile, x, y0, a1, a2, a3, y):
                V.tensor_tensor(a1, y0, y0, ALU.mult).then_inc(s, 1)
                dve.wait_ge(s, 4 * tile + 1)
                V.tensor_tensor(a2, a1, x, ALU.mult).then_inc(s, 1)
                dve.wait_ge(s, 4 * tile + 2)
                V.tensor_scalar(a3, a2, -0.5, 1.5, ALU.mult, ALU.add).then_inc(s, 1)
                dve.wait_ge(s, 4 * tile + 3)
                V.tensor_tensor(y, y0, a3, ALU.mult).then_inc(s, 1)

            def post(what, tile, b, c, k, last):
                if what == "R":
                    dve.wait_ge(sq_done, tile + 1)
                    V.tensor_reduce(ms[:], sq[:], AX.X, ALU.add).then_inc(ms_done, 1)
                    dve.wait_ge(ms_done, tile + 1)
                    V.tensor_scalar(ms2[:], ms[:], 1.0 / 16.0, EPS, ALU.mult, ALU.add).then_inc(ms2_done, 1)
                    dve.wait_ge(r0_done, tile + 1)
                    need(dve, ao_done, tile)
                    newton_step(newton, tile, ms2[:], r0[:], nt1[:], nt2[:], nt3[:], rr[:])
                elif what == "A":
                    dve.wait_ge(aT_hi, tile + 1)
                    V.tensor_tensor(aT_l[:], bank[6][:, 0:256].rearrange("p (i j t) -> p j i t", i=2, j=2)[:, :, :, 0:S],
                                    aT_h[:].bitcast(F32), ALU.subtract).then_inc(aT_lo, 1)
                elif what == "P":
                    dve.wait_ge(projected, tile + 1)
                    need(dve, h2_out[b], 8 * tile - 8 * b)
                    V.tensor_tensor(h2[b][:], bank[7][0:TT, 0:D], h[:, bass.ds(tile, 1), :].rearrange("p a n -> p (a n)"),
                                    ALU.add).then_inc(h2_done, 1)
                    dve.wait_ge(h2_done, tile + 1)
                    V.bn_stats(st2[:], h2[b][:]).then_inc(st2_done, 1)
                    dve.wait_ge(small_in, 64)
                    dve.wait_ge(st2_done, tile + 1)
                    V.bn_aggr(mv2[:], st2[:]).then_inc(mv2_done, 1)
                    dve.wait_ge(mv2_done, tile + 1)
                    V.tensor_scalar(ve2[:], mv2[:, 1:2], EPS, None, ALU.add).then_inc(ve2_done, 1)
                    dve.wait_ge(q0_done, tile + 1)
                    newton_step(newton2, tile, ve2[:], q0[:], q1[:], q2[:], q3[:], rs2[:])
                    dve.wait_ge(newton2, 4 * tile + 4)
                    need(dve, hn2_turned, tile - 1)
                    need(dve, hn2_kept, tile - 1)
                    V.tensor_scalar(hn2w[b][:], h2[b][:], mv2[:, 0:1], rs2[:],
                                    ALU.subtract, ALU.mult).then_inc(hn2_done, 1)
                elif what == "N":
                    dve.wait_ge(h2T_done, tile + 1)
                    tok = bass.ds(tile * TT, TT)
                    V.tensor_copy(hn2T_h[:, :, tok], h2T[:]).then_inc(h2T_hi, 1)
                    dve.wait_ge(h2T_hi, tile + 1)
                    V.tensor_tensor(hn2T_l[:, :, tok], h2T[:], hn2T_h[:, :, tok].bitcast(F32), ALU.subtract).then_inc(h2T_lo, 1)
                elif what == "G":
                    dve.wait_ge(gated, tile + 1)
                    V.tensor_copy(logits[:, bass.ds(tile, 1), :].rearrange("p a n -> p (a n)"),
                                  bank[7][0:TT, 0:E + 1]).then_inc(logit_done, 1)

            attention(dve, lag0=centre, lag2=epilogue, qk=qk, post=post)

            dve.wait_ge(h2_out[0], 16 * NT // 2)
            dve.wait_ge(h2_out[1], 16 * NT // 2)
            dve.wait_ge(logit_done, NT)
            dve.wait_ge(zeroed, 16 * NZ)
            done = [0]

            def link(ins):
                done[0] += 1
                ins.then_inc(routing, 1)
                dve.wait_ge(routing, done[0])

            for i in range(NT):
                V.max(mx8[:, i, :], logits[:, i, 0:E]).then_inc(routing, 1)
            done[0] += NT
            dve.wait_ge(routing, done[0])
            for i in range(NT):
                V.max_index(ix8[:, i, :], mx8[:, i, :], logits[:, i, 0:E]).then_inc(routing, 1)
            V.tensor_tensor(dl[:], mx8[:, :, 1], mx8[:, :, 0], ALU.subtract).then_inc(gate_diff, 1)
            done[0] += NT
            dve.wait_ge(routing, done[0])
            link(V.tensor_copy(ixf[:], ix8[:, :, 0:TOPK].rearrange("p i k -> p k i")))
            iota = cs[0:TT, C_IOTA:C_IOTA + E]
            for k in range(TOPK):
                link(V.tensor_tensor(oh[:, k], bc(iota.unsqueeze(2), [TT, E, NT]), bc(ixf[:, k:k + 1, :], [TT, E, NT]), ALU.is_equal))
            V.tensor_tensor(both[:], oh[:, 0], oh[:, 1], ALU.add).then_inc(chosen, 1)
            dve.wait_ge(counted, 1)
            tot = bank[1][0:TT, 0:E * NT]
            link(V.tensor_tensor_scan(cuminc[:].rearrange("p e i -> p (e i)"), cs[0:TT, C_RESET:C_RESET + E * NT], tot, 0.0, ALU.mult, ALU.add))
            link(V.tensor_tensor(excl[:].rearrange("p e i -> p (e i)"), cuminc[:].rearrange("p e i -> p (e i)"), tot, ALU.subtract))
            link(V.tensor_scalar(cnt[:], cuminc[:, :, NT - 1], float(BLK - 1), None, ALU.add))
            link(V.tensor_scalar(cnts[:], cnt[:], 7, None, ALU.logical_shift_right))
            link(V.tensor_copy(nblk[:], cnts[:]))
            link(V.tensor_tensor_scan(cumb[:], cs[0:TT, C_ONE:C_ONE + E], nblk[:], 0.0, ALU.mult, ALU.add))
            link(V.tensor_tensor(base[:], cumb[:], nblk[:], ALU.subtract))
            link(V.tensor_tensor(slotf[:].rearrange("p e i -> p (e i)"), bank[0][0:TT, 0:E * NT], excl[:].rearrange("p e i -> p (e i)"), ALU.add))
            link(V.scalar_tensor_tensor(slot2[:], bc(base[:].unsqueeze(2), [TT, E, NT]), float(BLK), slotf[:], ALU.mult, ALU.add))
            for k in range(TOPK):
                link(V.tensor_tensor(pick[:], oh[:, k], slot2[:], ALU.mult))
                link(V.tensor_reduce(slotr[:, k], pick[:].rearrange("p e i -> p i e"), AX.X, ALU.add))
            V.tensor_copy(slot_u[:], slotr[:]).then_inc(slots_known, 1)
            link(V.tensor_tensor(ecmp[:], bc(cumb[0:1, :].unsqueeze(1), [1, NBLK, E]),
                                 bc(cs[0:1, C_BLK:C_BLK + NBLK].unsqueeze(2), [1, NBLK, E]), ALU.is_le))
            link(V.tensor_reduce(esum[:], ecmp[:], AX.X, ALU.add))
            V.tensor_scalar(eid[:], esum[:], float(E - 1), None, ALU.min).then_inc(eids_known, 1)
            dve.wait_ge(e_exp, 2)
            link(V.tensor_scalar(ed1[:], ed[:], 1.0, None, ALU.add))
            link(V.reciprocal(w1[:], ed1[:]))
            V.tensor_tensor(w2[:], w1[:], ed[:], ALU.mult).then_inc(weights_known, 1)
            link(V.tensor_scalar(ez1[:], ez[:], 1.0, None, ALU.add))
            V.reciprocal(sig[:], ez1[:]).then_inc(weights_known, 1)

            for n in range(NS):
                dve.wait_ge(w_hi, n + 1)
                V.tensor_tensor(wsh_l[:, n * STG:(n + 1) * STG], stg[n][:], wsh_h[:, n * STG:(n + 1) * STG].bitcast(F32),
                                ALU.subtract).then_inc(w_lo, 1)
            dve.wait_ge(weights_known, 2)
            with dve.Fori(0, NSH) as c:
                for b in range(SB):
                    u = SB * c + b
                    dve.wait_ge(sh_silu, u + 1)
                    dve.wait_ge(sh_u, u + 1)
                    dve.wait_ge(sh_hi, u)
                    dve.wait_ge(sh_lo, u)
                    V.tensor_tensor(hs[:], sgl[:], bank[(2 * b + 1) % 4][:, 0:SH], ALU.mult).then_inc(sh_h, 1)
                    dve.wait_ge(sh_hi, u + 1)
                    dve.wait_ge(sh_y, 4 * c)
                    V.tensor_tensor(hs_l[:, b, :], hs[:], hs_h[:, b, :].bitcast(F32), ALU.subtract).then_inc(sh_lo, 1)
                    if b < NW // NSH:
                        n = NW // NSH * c + b
                        dve.wait_ge(w_hi, NS + n + 1)
                        V.tensor_tensor(we_l[:, bass.ds(n * STG, STG)], stg[b][:], we_h[:, bass.ds(n * STG, STG)].bitcast(F32),
                                        ALU.subtract).then_inc(w_lo, 1)
                for tt in range(4):
                    t = 4 * c + tt
                    dve.wait_ge(sh_y, t + 1)
                    dve.wait_ge(h2_in[tt % 2], 32 * c + 16 * (tt // 2) + 16)
                    dve.wait_ge(acc_out[tt % 2], 32 * c + 16 * (tt // 2))
                    V.scalar_tensor_tensor(acc[tt % 2][:], bank[4 + tt % 2][0:TT, 0:D], sig[:, bass.ds(t, 1)], h2r[tt % 2][:],
                                           ALU.mult, ALU.add).then_inc(sh_acc, 1)

            def block_lo(b, par):
                dve.wait_ge(b_hi, b + 1)
                V.tensor_tensor(bxT_l[par][:].rearrange("p k t -> p (k t)"), bank[par][:, 0:D],
                                bxT_h[par][:].rearrange("p k t -> p (k t)").bitcast(F32), ALU.subtract).then_inc(b_lo, 1)

            def block_h(b, par):
                dve.wait_ge(b_silu, b + 1)
                need(dve, b_hturned, b - 1)
                V.tensor_tensor(bh[par][:], bsg[par][:], bank[2 + par][:, HID:2 * HID], ALU.mult).then_inc(b_h, 1)

            def block_hlo(b, par):
                dve.wait_ge(b_hhi, b + 1)
                V.tensor_tensor(bhT_l[par][:], bank[4 + par][:, 0:BLK], bhT_h[par][:].bitcast(F32), ALU.subtract).then_inc(b_hlo, 1)

            blocks(dve, [(1, block_lo), (0, block_h), (-1, block_hlo)])

            def combine(t, par):
                dve.wait_ge(acc_in[par], 8 * t + 16 - 8 * par)
                dve.wait_ge(y_in[par], 16 * t + 32 - 16 * par)
                need(dve, fin_done, t - 1)
                V.scalar_tensor_tensor(psum1[par][:], y1[par][:], w1[:, bass.ds(t, 1)], h2r[par][:], ALU.mult, ALU.add).then_inc(part_sum, 1)
                dve.wait_ge(part_sum, t + 1)
                need(dve, fin_out[par], 8 * t - 8 * par)
                V.scalar_tensor_tensor(fin[par][:], y2[par][:], w2[:, bass.ds(t, 1)], psum1[par][:], ALU.mult, ALU.add).then_inc(fin_done, 1)

            combine(0, 0)
            combine(1, 1)
            with dve.Fori(1, NT // 2) as t:
                combine(2 * t, 0)
                combine(2 * t + 1, 1)

        @block.tensor
        def _(pe):
            def product(out, pairs):
                n = 3 * len(pairs)
                for m, (lh, ll, rh, rl) in enumerate(pairs):
                    for q, (a, b) in enumerate(((lh, rh), (lh, rl), (ll, rh))):
                        last = T.matmul(out, a, b, start=(3 * m + q == 0), stop=(3 * m + q == n - 1))
                return last

            pe.wait_ge(wt_lo, 1)

            def embed(i, b):
                pe.wait_ge(x_lo, i + 1)
                need(pe, h_done, i - 1)
                product(bank[6 + b][0:TT, 0:D], [(x_h[b][:, k, :], x_l[b][:, k, :], wt_h[:, k, :], wt_l[:, k, :])
                                                 for k in range(KP)]).then_inc(embedded, 1)

            embed(0, 0)
            embed(1, 1)
            with pe.Fori(1, NT // 2) as t:
                embed(2 * t, 0)
                embed(2 * t + 1, 1)
            pe.wait_ge(cst_in, 16)

            def turn_hn(i, b):
                pe.wait_ge(hn_done, i + 1)
                need(pe, hT_lo, i - 1)
                for k in range(KD):
                    last = T.transpose(bank[4 + b][:, k * TT:(k + 1) * TT], hn[b][:, k * 128:(k + 1) * 128], ident[0:TT, 0:TT])
                last.then_inc(hn_turned, 1)

            turn_hn(0, 0)
            turn_hn(1, 1)
            with pe.Fori(1, NT // 2) as t:
                turn_hn(2 * t, 0)
                turn_hn(2 * t + 1, 1)
            pe.wait_ge(wa_lo, 1)
            pe.wait_ge(hT_lo, NT)

            def qk(c, m, cc):
                need(pe, rest1, 4 * c + m - 1)
                need(pe, (aT_lo, h2_done, h2T_done, logit_done)[m], 2 * c - 3)
                tok = bass.ds(c * CHUNK, CHUNK)
                w = slice(m * 128, (m + 1) * 128)
                product(bank[6 + m % 2][:, 0:CHUNK], [(wa_h[:, k, w], wa_l[:, k, w], hT_h[:, k, tok], hT_l[:, k, tok])
                                                      for k in range(KD)]).then_inc(qk_made, 1)

            for m in range(4):
                qk(0, m, 0)
            for i in range(NT):
                need(pe, v_kept, i - 1)
                tok = slice(i * TT, (i + 1) * TT)
                product(bank[4 + i % 2][0:TT, 0:D], [(hT_h[:, k, tok], hT_l[:, k, tok], wa_h[:, k, 2 * D:], wa_l[:, k, 2 * D:])
                                                     for k in range(KD)]).then_inc(v_made, 1)
            pe.wait_ge(v_kept, NT)
            pe.wait_ge(init_done, 4)
            pe.wait_ge(wp_lo, 1)
            pe.wait_ge(small_in, 64)

            def scores(c, k, cc):
                u, b, n = 8 * c + k, k % 2, k // 2
                pe.wait_ge(stacked[cc], 192 * c - 192 * cc + 384)
                need(pe, centred, u - 1)
                T.matmul(bank[b][:, 0:8 * S], sel_bf[:], mask_bf[:].rearrange("p m s -> p (m s)"), start=True, stop=False, skip_group_check=True)
                for m in range(8):
                    for jj in range(2):
                        r = slice(SLOT * jj, SLOT * jj + 8 * PARTS)
                        q = 8 * b + m
                        last = T.matmul(bank[b][SLOT * jj:SLOT * jj + S, m * S:(m + 1) * S], Qs[cc][r, q, n * S:(n + 1) * S],
                                        Ks[cc][r, q, n * S:(n + 1) * S], start=False, stop=(m == 7), skip_group_check=True)
                last.then_inc(scored, 1)

            def turn(c, k, cc):
                u, b = 8 * c + k, k % 2
                pe.wait_ge(centred, u + 1)
                need(pe, exped, u - 1)
                for m in range(4):
                    last = T.transpose(bank[2 + b][0:TT, m * 128:(m + 1) * 128], Sm[b][:, m, :], ident)
                last.then_inc(turned, 1)

            def weigh(c, k, cc):
                u, b, n = 8 * c + k, k % 2, k // 2
                pe.wait_ge(exped, u + 1)
                pe.wait_ge(vx_in[n], 32 * c + 32)
                need(pe, on_done, 2 * (u - 1))
                for m in range(4):
                    h0 = (4 * b + m) * VW
                    last = T.matmul(bank[4 + b][:, m * 2 * VW:(m + 1) * 2 * VW].rearrange("p (j n) -> p j n", j=2), PT[b][:, m, :],
                                    vx[n][:, :, h0:h0 + VW], start=True, stop=True)
                last.then_inc(weighed, 1)

            def post(what, tile, b, c, k, last):
                made6 = 4 * c + 4 + (1, 1, 3, 3, 3, 3, 3, 3)[k] if not last else 4 * NCHUNK
                made7 = 4 * c + 4 + (0, 2, 2, 4, 4, 4, 4, 4)[k] if not last else 4 * NCHUNK
                if what == "A":
                    pe.wait_ge(ao_done, tile + 1)
                    pe.wait_ge(rest1, made6)
                    need(pe, h2T_done, tile)
                    for i in range(2):
                        end = T.transpose(bank[6][:, i * 128:(i + 1) * 128], ao[:, i, :, :].rearrange("p h d -> p (h d)"), ident)
                    end.then_inc(ao_turned, 1)
                elif what == "P":
                    pe.wait_ge(aT_lo, tile + 1)
                    pe.wait_ge(rest1, made7)
                    need(pe, logit_done, tile)
                    product(bank[7][0:TT, 0:D], [(aT_h[:, j].rearrange("p i t -> p (i t)"), aT_l[:, j].rearrange("p i t -> p (i t)"), wp_h[:, j, :], wp_l[:, j, :])
                                                 for j in range(2)]).then_inc(projected, 1)
                elif what == "N":
                    pe.wait_ge(hn2_done, tile + 1)
                    pe.wait_ge(rest1, made6)
                    pe.wait_ge(aT_lo, tile + 1)
                    for k_ in range(KD):
                        end = T.transpose(bank[6][:, k_ * TT:(k_ + 1) * TT], hn2w[b][:, k_ * 128:(k_ + 1) * 128], ident[0:TT, 0:TT])
                    end.then_inc(hn2_turned, 1)
                elif what == "G":
                    pe.wait_ge(h2T_done, tile + 1)
                    pe.wait_ge(rest1, made7)
                    pe.wait_ge(h2_done, tile + 1)
                    for k_ in range(KD):
                        end = T.matmul(bank[7][0:TT, 0:E + 1], h2T[:, k_, :], wg_sb[:, k_, :], start=(k_ == 0), stop=(k_ == KD - 1))
                    end.then_inc(gated, 1)

            attention(pe, lag0=scores, lag1=turn, lag2=weigh, qk=qk, post=post)

            pe.wait_ge(chosen, 1)
            rhs = both[:].rearrange("p e i -> p (e i)")
            T.matmul(bank[0][0:TT, 0:E * NT], up_bf[0:TT, 0:TT], rhs, start=True, stop=True)
            T.matmul(bank[1][0:TT, 0:E * NT], one_bf[0:TT, 0:TT], rhs, start=True, stop=True).then_inc(counted, 1)
            pe.wait_ge(slots_known, 1)

            pe.wait_ge(w_lo, NS)
            with pe.Fori(0, NSH) as c:
                tok = bass.ds(c * SH, SH)
                for b in range(SB):
                    u = SB * c + b
                    for half_, (s_, free) in enumerate(((sh_g, sh_silu), (sh_u, sh_h))):
                        pe.wait_ge(free, SB * c + max(b - 1, 0))
                        cols = [slice((b * KD + k) * 2 * HID + half_ * HID, (b * KD + k) * 2 * HID + (half_ + 1) * HID) for k in range(KD)]
                        product(bank[(2 * b + half_) % 4][:, 0:SH], [(wsh_h[:, cols[k]], wsh_l[:, cols[k]], hn2T_h[:, k, tok], hn2T_l[:, k, tok])
                                                                     for k in range(KD)]).then_inc(s_, 1)
                for tt in range(4):
                    t = 4 * c + tt
                    pe.wait_ge(sh_lo, SB * c + SB)
                    if tt >= 2:
                        pe.wait_ge(sh_acc, t - 1)
                    else:
                        pe.wait_ge(sh_acc, 4 * c)
                    product(bank[4 + tt % 2][0:TT, 0:D], [(hs_h[:, b, tt * TT:(tt + 1) * TT], hs_l[:, b, tt * TT:(tt + 1) * TT],
                                                           wsh_h[:, SGU + b * D:SGU + (b + 1) * D], wsh_l[:, SGU + b * D:SGU + (b + 1) * D])
                                                          for b in range(SB)]).then_inc(sh_y, 1)

            pe.wait_ge(w_lo, NS + NW)
            pe.wait_ge(eids_known, 1)
            pe.wait_ge(sh_acc, NT)

            def block_turn(b, par):
                pe.wait_ge(bx_in[par], 8 * b + 16 - 8 * par)
                need(pe, b_lo, b - 1)
                for k in range(KD):
                    last = T.transpose(bank[par][:, k * BLK:(k + 1) * BLK], bx[par][:, k * 128:(k + 1) * 128], ident)
                last.then_inc(b_turned, 1)

            def expert(b):
                return T.value_load(eid[0:1, bass.ds(b, 1)], min_val=0, max_val=E - 1)

            def block_gu(b, par):
                e = expert(b)
                pe.wait_ge(b_lo, b + 1)
                need(pe, b_h, b - 1)
                product(bank[2 + par][:, 0:2 * HID], [(bxT_h[par][:, k, :], bxT_l[par][:, k, :],
                                                       we_h[:, bass.ds(e * (KD * 2 * HID) + k * 2 * HID, 2 * HID)],
                                                       we_l[:, bass.ds(e * (KD * 2 * HID) + k * 2 * HID, 2 * HID)])
                                                      for k in range(KD)]).then_inc(b_gu, 1)

            def block_hturn(b, par):
                pe.wait_ge(b_h, b + 1)
                need(pe, b_hlo, b - 1)
                T.transpose(bank[4 + par][:, 0:BLK], bh[par][:], ident).then_inc(b_hturned, 1)

            def block_down(b, par):
                e = expert(b)
                pe.wait_ge(b_hlo, b + 1)
                need(pe, b_ykept, b - 1)
                product(bank[6 + par][:, 0:D], [(bhT_h[par][:], bhT_l[par][:], we_h[:, bass.ds(e * D + EGU, D)],
                                                 we_l[:, bass.ds(e * D + EGU, D)])]).then_inc(b_y, 1)

            blocks(pe, [(1, block_turn), (0, block_gu), (-1, block_hturn), (-2, block_down)])


def kernel(**inputs):
    import numpy as np
    import concourse.bacc as bacc
    from concourse import mybir as mb
    from concourse.bass_utils import run_bass_kernel_spmd

    a = {k: np.asarray(v) for k, v in inputs.items()}
    P_, G_ = 16, 7
    x = a["x"].reshape(IMAGES, 3, G_, P_, G_, P_).transpose(1, 3, 5, 0, 2, 4).reshape(KP, 128, NT, TT)
    wq, wk, wv = (a["L0_attn_w_attn"][:, n * D:(n + 1) * D] for n in range(3))
    turned = [w.reshape(D, HP, 2, 2, 8).transpose(0, 2, 4, 1, 3).reshape(D, D) for w in (wq, wk)]
    wa = np.concatenate(turned + [wv], axis=1)
    gu = np.concatenate([a["L0_ffn_We_gate"], a["L0_ffn_We_up"]], axis=1)
    sgu = np.concatenate([a["L0_ffn_Ws_gate"].reshape(SB, HID, D), a["L0_ffn_Ws_up"].reshape(SB, HID, D)], axis=1)

    def gate_up(w):
        return w.reshape(w.shape[0], 2 * HID, KD, 128).transpose(3, 0, 2, 1).reshape(128, -1)

    arrays = {
        "xt": x.transpose(2, 1, 0, 3).reshape(NT * 128, KP * TT),
        "wt": a["L0_tok_W"].T.reshape(KP, 128, D).transpose(1, 0, 2).reshape(128, KP * D),
        "tb": a["L0_tok_b"].reshape(1, D),
        "wa": wa.reshape(KD, 128, 3 * D).transpose(1, 0, 2),
        "wp": a["L0_attn_w_proj"].reshape(HP, 2, 16, D).transpose(0, 2, 1, 3).reshape(128, 2, D),
        "gam": np.tile(a["L0_attn_gamma"], HP).reshape(128, 1),
        "lam": np.stack([a["L0_attn_lambda_" + n] for n in ("q1", "q2", "k1", "k2")]).reshape(1, 4, 8),
        "wg": np.concatenate([a["L0_ffn_Wg"], a["L0_ffn_Wsg"]]).T.reshape(KD, 128, E + 1).transpose(1, 0, 2),
        "we": np.concatenate([gate_up(gu), a["L0_ffn_We_down"].transpose(2, 0, 1).reshape(HID, -1)], axis=1),
        "wsh": np.concatenate([gate_up(sgu), a["L0_ffn_Ws_down"].reshape(D, SB, HID).transpose(2, 1, 0).reshape(HID, -1)], axis=1),
        "cst": constants(),
    }
    arrays = {k: np.ascontiguousarray(v) for k, v in arrays.items()}
    nc = bacc.Bacc("TRN2", target_bir_lowering=False, num_devices=1)
    aps = [nc.dram_tensor(k, v.shape, mb.dt.from_np(v.dtype), kind="ExternalInput").ap() for k, v in arrays.items()]
    aps.append(nc.dram_tensor("out", (TOK, D), F32, kind="ExternalOutput").ap())
    build(nc, *aps)
    r = run_bass_kernel_spmd(nc, [arrays], core_ids=[0])
    return np.asarray(r.results[0]["out"]).reshape(IMAGES, S, D)
```

```python
from contextlib import ExitStack

import concourse.bass as bass
from concourse import mybir

F32 = mybir.dt.float32
F32R = mybir.dt.float32r
BF16 = mybir.dt.bfloat16
I32 = mybir.dt.int32
U32 = mybir.dt.uint32
ALU = mybir.AluOpType
ACT = mybir.ActivationFunctionType
AX = mybir.AxisListType

IMAGES, S, D, PIX = 32, 49, 256, 768
TOK = IMAGES * S
TT = 2 * S
NT = TOK // TT
WTP = 3
KP = PIX // 128
KD = D // 128
HP = 8
VW = 34
SLOT = 64
PARTS = 6
QPART = (0, 0, 1, 1, 0, 2)
KPART = (0, 1, 0, 1, 2, 0)
CHUNK = 4 * S
NCHUNK = TOK // CHUNK
E, TOPK, HID, SH_HID = 16, 2, 128, 512
BLK = 128
NBLK = (TOK * TOPK + E * (BLK - 1)) // BLK
YR = 8
SH = 8 * S
NSH = TOK // SH
SH1 = 2
SB = SH_HID // 128
EGU = E * KD * 2 * HID
WE = EGU + E * D
SGU = SB * KD * 2 * HID
WSH = SGU + SB * D
STG = 1024
EPS = 1e-5
LAMBDA_INIT = 0.8 - 0.6
BIG = -1e30

C_ID = 0
C_UP = C_ID + 128
C_ONE = C_UP + 128
C_SEL = C_ONE + 128
C_MASK = C_SEL + 128
C_RESET = C_MASK + S
C_IOTA = C_RESET + E * NT
C_BLK = C_IOTA + E
C_END = C_BLK + NBLK


def constants():
    import numpy as np
    c = np.zeros((128, C_END), np.float32)
    p = np.arange(128)
    c[:, C_ID:C_ID + 128] = p[:, None] == p[None, :]
    c[:, C_UP:C_UP + 128] = p[:, None] < p[None, :]
    c[:, C_ONE:C_ONE + 128] = 1.0
    c[:S, C_SEL:C_SEL + 128] = p[:S, None] == (p[None, :] % SLOT)
    c[:S, C_MASK:C_MASK + S] = np.where(p[None, :S] > p[:S, None], BIG, 0.0)
    c[:, C_RESET:C_RESET + E * NT] = (np.arange(E * NT) % NT != 0)
    c[:, C_IOTA:C_IOTA + E] = np.arange(E)
    c[:, C_BLK:C_BLK + NBLK] = np.arange(NBLK)
    return c


def build(nc, xt, wt, tb, wa, wp, gam, lam, wg, we, wsh, cst, out):
    ctx = ExitStack()
    with ctx:
        V, A, T, G, SP = nc.vector, nc.scalar, nc.tensor, nc.gpsimd, nc.sync

        def sem(name):
            return ctx.enter_context(nc.semaphore(name))

        def bc(ap, shape):
            return ap.broadcast_to(shape)

        slots_x = nc.dram_tensor("slots_x", (NBLK * BLK, D), F32, kind="Internal").ap()
        slots_y = nc.dram_tensor("slots_y", (NBLK * BLK, D), F32, kind="Internal").ap()
        h2_dram = nc.dram_tensor("h2_dram", (TOK, D), F32, kind="Internal").ap()
        acc_dram = nc.dram_tensor("acc_dram", (TOK, D), F32, kind="Internal").ap()

        def keep(name, shape, dt=F32):
            return ctx.enter_context(nc.sbuf_tensor(name, shape, dt))

        cs = keep("cs", [128, C_END])
        ident = cs[:, C_ID:C_ID + 128]
        hn2 = keep("hn2", [TT, NT, D])
        hn2T_h = keep("hn2T_h", [128, KD, TOK], F32R)
        hn2T_l = keep("hn2T_l", [128, KD, TOK], F32R)
        logits = keep("logits", [TT, NT, E + 1])
        slot_u = keep("slot_u", [TT, TOPK, NT], U32)
        w1 = keep("w1", [TT, NT])
        w2 = keep("w2", [TT, NT])
        sig = keep("sig", [TT, NT])
        woff = keep("woff", [1, NBLK // 4 + 1, 8], I32)
        one_bf = keep("one_bf", [128, 128], BF16)
        up_bf = keep("up_bf", [128, 128], BF16)

        early = ExitStack()

        def ea(name, shape, dt=F32):
            return early.enter_context(nc.sbuf_tensor(name, shape, dt))

        wa_h = ea("wa_h", [128, KD, 3 * D], F32R)
        wa_l = ea("wa_l", [128, KD, 3 * D], F32R)
        wpr = ea("wpr", [128, 2, D])
        wpg = ea("wpg", [128, 2, D])
        wp_h = ea("wp_h", [128, 2, D], F32R)
        wp_l = ea("wp_l", [128, 2, D], F32R)
        wg_sb = ea("wg_sb", [128, KD, E + 1])
        gam_sb = ea("gam_sb", [128, 1])
        lam_sb = ea("lam_sb", [128, 4, 8])
        lamt = ea("lamt", [128, 2, 8])
        lam2 = ea("lam2", [128, 2])
        laml = ea("laml", [128, 2])
        lamd = ea("lamd", [128, 1])
        neglam = ea("neglam", [128, 1])
        bias = ea("bias", [TT, D])
        h = ea("h", [TT, NT, D])
        hT_h = ea("hT_h", [128, KD, TOK], F32R)
        hT_l = ea("hT_l", [128, KD, TOK], F32R)
        vst = ea("vst", [TT, NT, HP, VW])
        vx = [ea(f"vx{n}", [TT, 2, HP * VW]) for n in range(4)]
        sel_bf = ea("sel_bf", [S, 128], BF16)
        mask_bf = ea("mask_bf", [S, 8, S], BF16)
        zero = ea("zero", [128, 1280])
        three = ea("three", [128, 2 * HP])
        first = ExitStack()

        def fa(name, shape, dt=F32):
            return first.enter_context(nc.sbuf_tensor(name, shape, dt))

        wraw = fa("wraw", [128, KP * D])
        wt_h = fa("wt_h", [128, KP, D], F32R)
        wt_l = fa("wt_l", [128, KP, D], F32R)
        war = fa("war", [128, KD, 3 * D])
        xr = [fa(f"xr{n}", [128, KP, TT]) for n in range(2)]
        x_h = [fa(f"x_h{n}", [128, KP, TT], F32R) for n in range(2)]
        x_l = [fa(f"x_l{n}", [128, KP, TT], F32R) for n in range(2)]
        st1 = [fa(f"st1{n}", [TT, 6]) for n in range(2)]
        mv1 = [fa(f"mv1{n}", [TT, 2]) for n in range(2)]
        ve1 = [fa(f"ve1{n}", [TT, 1]) for n in range(2)]
        ln1 = [fa(f"ln1{n}", [TT, 1]) for n in range(2)]
        y1 = [fa(f"y1{n}", [TT, 1]) for n in range(2)]
        yx1 = [fa(f"yx1{n}", [TT, 1]) for n in range(2)]
        yn1 = [fa(f"yn1{n}", [TT, 1]) for n in range(2)]
        rs1 = [fa(f"rs1{n}", [TT, 1]) for n in range(2)]
        hn = [fa(f"hn{n}", [TT, D]) for n in range(2)]
        first.close()
        parts = ea("parts", [128, 4, 3, CHUNK], BF16)
        rest = [ea(f"rest{n}", [128, CHUNK]) for n in range(2)]
        Qs = [ea(f"Qs{n}", [112, 2 * HP, CHUNK], BF16) for n in range(2)]
        Ks = [ea(f"Ks{n}", [112, 2 * HP, CHUNK], BF16) for n in range(2)]
        smax = [ea(f"smax{n}", [128, 8]) for n in range(2)]
        Sm = [ea(f"Sm{n}", [128, 4, TT]) for n in range(2)]
        PT = [ea(f"PT{n}", [TT, 4, 128]) for n in range(2)]
        rz = ea("rz", [128, 8])
        on = ea("on", [128, 8, 16])
        att = [ea(f"att{n}", [128, 2, HP, 16]) for n in range(2)]
        sq = ea("sq", [128, 2 * HP, 16])
        ms = ea("ms", [128, 2 * HP])
        ms2 = ea("ms2", [128, 2 * HP])
        lnr = ea("lnr", [128, 2 * HP])
        r0 = ea("r0", [128, 2 * HP])
        nt1 = ea("nt1", [128, 2 * HP])
        nt2 = ea("nt2", [128, 2 * HP])
        nt3 = ea("nt3", [128, 2 * HP])
        rr = ea("rr", [128, 2 * HP])
        ao = ea("ao", [128, 2, HP, 16])
        aT_h = ea("aT_h", [128, 2, 2, S], F32R)
        aT_l = ea("aT_l", [128, 2, 2, S], F32R)
        h2 = [ea(f"h2{n}", [TT, D]) for n in range(2)]
        hn2w = [ea(f"hn2w{n}", [TT, D]) for n in range(2)]
        st2 = ea("st2", [TT, 6])
        mv2 = ea("mv2", [TT, 2])
        ve2 = ea("ve2", [TT, 1])
        ln2 = ea("ln2", [TT, 1])
        q0 = ea("q0", [TT, 1])
        q1 = ea("q1", [TT, 1])
        q2 = ea("q2", [TT, 1])
        q3 = ea("q3", [TT, 1])
        rs2 = ea("rs2", [TT, 1])
        h2T = ea("h2T", [128, KD, TT])
        early.close()

        def la(name, shape, dt=F32):
            return ctx.enter_context(nc.sbuf_tensor(name, shape, dt))

        we_h = la("we_h", [128, WE], F32R)
        we_l = la("we_l", [128, WE], F32R)
        wsh_h = la("wsh_h", [128, WSH], F32R)
        wsh_l = la("wsh_l", [128, WSH], F32R)
        sgl = la("sgl", [128, SH])
        hs = la("hs", [128, SH])
        hs_h = la("hs_h", [128, SB, SH], F32R)
        hs_l = la("hs_l", [128, SB, SH], F32R)
        h2r = [la(f"h2r{n}", [TT, D]) for n in range(2)]
        acc = [la(f"acc{n}", [TT, D]) for n in range(2)]

        middle = ExitStack()

        def ma(name, shape, dt=F32):
            return middle.enter_context(nc.sbuf_tensor(name, shape, dt))

        stg = [ma(f"stg{n}", [128, STG]) for n in range(3)]
        mx8 = ma("mx8", [TT, NT, 8])
        ix8 = ma("ix8", [TT, NT, 8], U32)
        ixf = ma("ixf", [TT, TOPK, NT])
        oh = ma("oh", [TT, TOPK, E, NT])
        both = ma("both", [TT, E, NT], BF16)
        cuminc = ma("cuminc", [TT, E, NT])
        excl = ma("excl", [TT, E, NT])
        cnt = ma("cnt", [TT, E], I32)
        cnts = ma("cnts", [TT, E], I32)
        nblk = ma("nblk", [TT, E])
        cumb = ma("cumb", [TT, E])
        base = ma("base", [TT, E])
        slotf = ma("slotf", [TT, E, NT])
        slot2 = ma("slot2", [TT, E, NT])
        ecmp = ma("ecmp", [1, NBLK, E], BF16)
        slotr = ma("slotr", [TT, TOPK, NT])
        esum = ma("esum", [1, NBLK])
        eid = ma("eid", [1, NBLK // 4, 4])
        dl = ma("dl", [TT, NT])
        ed = ma("ed", [TT, NT])
        ed1 = ma("ed1", [TT, NT])
        ez = ma("ez", [TT, NT])
        ez1 = ma("ez1", [TT, NT])
        middle.close()
        bx = [la(f"bx{n}", [BLK, D]) for n in range(4)]
        bxT_h = [la(f"bxT_h{n}", [128, KD, BLK], F32R) for n in range(2)]
        bxT_l = [la(f"bxT_l{n}", [128, KD, BLK], F32R) for n in range(2)]
        bsg = [la(f"bsg{n}", [BLK, HID]) for n in range(2)]
        bh = [la(f"bh{n}", [BLK, HID]) for n in range(2)]
        bhT_h = [la(f"bhT_h{n}", [HID, BLK], F32R) for n in range(2)]
        bhT_l = [la(f"bhT_l{n}", [HID, BLK], F32R) for n in range(2)]
        by = [la(f"by{n}", [BLK, D]) for n in range(4)]
        accr = [la(f"accr{n}", [TT, D]) for n in range(2)]
        psum1 = [la(f"psum1{n}", [TT, D]) for n in range(2)]
        fin = [la(f"fin{n}", [TT, D]) for n in range(2)]

        bank = [ctx.enter_context(nc.psum_tensor(f"bank{n}", [128, 512], F32)) for n in range(8)]

        cst_in = sem("cst_in")
        wt_in = [sem(f"wt_in{n}") for n in range(WTP)]
        wa_in = sem("wa_in")
        wp_in = sem("wp_in")
        small_in = sem("small_in")
        x_in = [sem(f"x_in{n}") for n in range(2)]
        init_done = sem("init_done")
        pool_init = sem("pool_init")
        zeroed = sem("zeroed")
        wt_hi, wt_lo = sem("wt_hi"), sem("wt_lo")
        x_hi, x_lo = sem("x_hi"), sem("x_lo")
        embedded = sem("embedded")
        h_done, h_stats, h_aggr, h_var = (sem(n) for n in ("h_done", "h_stats", "h_aggr", "h_var"))
        h_ln, h_guess, h_newton = (sem(n) for n in ("h_ln", "h_guess", "h_newton"))
        hn_done, hn_turned, hT_hi, hT_lo = sem("hn_done"), sem("hn_turned"), sem("hT_hi"), sem("hT_lo")
        wa_hi, wa_lo, wp_g, wp_hi, wp_lo = sem("wa_hi"), sem("wa_lo"), sem("wp_g"), sem("wp_hi"), sem("wp_lo")
        lam_a, lam_b, lam_c, lam_d, lam_e = (sem(f"lam_{n}") for n in "abcde")
        v_made, v_kept = sem("v_made"), sem("v_kept")
        qk_made, part0, rest1, part1, part2 = (sem(n) for n in ("qk_made", "part0", "rest1", "part1", "part2"))
        stacked = [sem(f"stacked{n}") for n in range(2)]
        vx_in = [sem(f"vx_in{n}") for n in range(4)]
        scored, maxed, centred, turned, exped, weighed = (
            sem(n) for n in ("scored", "maxed", "centred", "turned", "exped", "weighed"))
        rz_done, on_done, att_done = sem("rz_done"), sem("on_done"), sem("att_done")
        sq_done, ms_done, ms2_done, ln_done, r0_done = (
            sem(n) for n in ("sq_done", "ms_done", "ms2_done", "ln_done", "r0_done"))
        newton = sem("newton")
        ao_done, ao_turned, aT_hi, aT_lo, projected = (
            sem(n) for n in ("ao_done", "ao_turned", "aT_hi", "aT_lo", "projected"))
        h2_done, st2_done, mv2_done, ve2_done, ln2_done, q0_done = (
            sem(n) for n in ("h2_done", "st2_done", "mv2_done", "ve2_done", "ln2_done", "q0_done"))
        hn2_kept = sem("hn2_kept")
        newton2, hn2_done, hn2_turned, h2T_done, h2T_hi, h2T_lo = (
            sem(n) for n in ("newton2", "hn2_done", "hn2_turned", "h2T_done", "h2T_hi", "h2T_lo"))
        gated, logit_done = sem("gated"), sem("logit_done")
        h2_out = [sem(f"h2_out{n}") for n in range(2)]
        gate_diff, slots_known, eids_known, weights_known, routing = (
            sem(n) for n in ("gate_diff", "slots_known", "eids_known", "weights_known", "routing"))
        chosen = sem("chosen")
        counted, e_exp = sem("counted"), sem("e_exp")
        scattered = sem("scattered")
        stg_in = [sem(f"stg_in{n}") for n in range(3)]
        w_hi, w_lo = sem("w_hi"), sem("w_lo")
        sh_g, sh_u, sh_silu, sh_h, sh_hi, sh_lo, sh_y, sh_acc = (
            sem(n) for n in ("sh_g", "sh_u", "sh_silu", "sh_h", "sh_hi", "sh_lo", "sh_y", "sh_acc"))
        h2_in = [sem(f"h2_in{n}") for n in range(2)]
        acc_out = [sem(f"acc_out{n}") for n in range(2)]
        bx_in = [sem(f"bx_in{n}") for n in range(4)]
        b_turned, b_hi, b_lo, b_gu, b_silu, b_h, b_hturned, b_hhi, b_hlo, b_y, b_ykept = (
            sem("b_" + n) for n in ("turned", "hi", "lo", "gu", "silu", "h", "hturned", "hhi", "hlo", "y", "ykept"))
        by_out = [sem(f"by_out{n}") for n in range(4)]
        acc_in = [sem(f"acc_in{n}") for n in range(2)]
        y_in = [sem(f"y_in{n}") for n in range(YR)]
        part_sum, fin_done = sem("part_sum"), sem("fin_done")
        fin_out = [sem(f"fin_out{n}") for n in range(2)]

        def need(eng, s, value):
            if isinstance(value, int) and value <= 0:
                return
            eng.wait_ge(s, value)

        NZ = NBLK * BLK // (128 * 5)
        assert NZ == NT // 2
        NW, NS = WE // STG, WSH // STG
        SPLITS = ((0, 1), (2,), (3, 4), (5,))
        assert NW == SH1 * 6

        def pipeline(eng, steps, count, mod, lead, lag, begin=None):
            def turn(b, q):
                if begin and q == 0:
                    begin(b)
                for ahead, step in steps:
                    if isinstance(b, int) and not 0 <= b + ahead < count:
                        continue
                    step(b + ahead, (q + ahead) % mod)
            for b in range(-lead, 4):
                turn(b, b % mod)
            with eng.Fori(4 // mod, count // mod - 1) as t:
                for q in range(mod):
                    turn(mod * t + q, q)
            for b in range(count - mod, count + lag):
                turn(b, b % mod)

        def embedding(eng, steps):
            pipeline(eng, steps, NT, 2, 1, 2)

        def blocks(eng, steps, begin=None):
            pipeline(eng, steps, NBLK, 4, 1, 2, begin)

        POSTS = {0: [("P", -2)], 1: [("N", -2)], 2: [("G", -2), ("R", -1)], 3: [("A", -1)],
                 4: [("P", -1)], 5: [("N", -1)], 6: [("G", -1), ("R", 0)], 7: [("A", 0)]}

        def attention(eng, steps, qk, post):
            def half(c, k, cc, last):
                for item in steps:
                    if item == "rest":
                        if k < 4 and not last:
                            qk(c + 1, k, 1 - cc)
                        for what, ahead in POSTS.get(k, ()):
                            tile = 2 * c + ahead
                            if not (isinstance(tile, int) and tile < 0):
                                post(what, tile, ahead % 2, c, k, last)
                        continue
                    lag, step = item
                    c_, k_, cc_ = (c, k - lag, cc) if k >= lag else (c - 1, k - lag + 8, 1 - cc)
                    if not (isinstance(c_, int) and c_ < 0) and k_ < 8:
                        step(c_, k_, cc_)

            def chunk(c, cc, last=False):
                for k in range(8):
                    half(c, k, cc, last)

            chunk(0, 0)
            chunk(1, 1)
            with eng.Fori(1, NCHUNK // 2 - 1) as s:
                chunk(2 * s, 0)
                chunk(2 * s + 1, 1)
            chunk(NCHUNK - 2, 0)
            chunk(NCHUNK - 1, 1, last=True)
            half(NCHUNK - 1, 8, 1, True)
            half(NCHUNK - 1, 9, 1, True)
            for what, tile in (("P", NT - 2), ("N", NT - 2), ("G", NT - 2), ("R", NT - 1), ("A", NT - 1),
                               ("P", NT - 1), ("N", NT - 1), ("G", NT - 1)):
                post(what, tile, tile % 2, NCHUNK - 1, 8, True)

        block = ctx.enter_context(nc.Block())

        @block.sync
        def _(sp):
            def row(value):
                return value if isinstance(value, int) else sp.snap(value)

            def load_x(i, b):
                r = row(i * 128)
                need(sp, x_lo, i - 1)
                need(sp, x_hi, i - 1)
                sp.dma_start(xr[b][:].rearrange("p k t -> p (k t)"), xt[bass.ds(r, 128), :]).then_inc(x_in[b], 16)

            load_x(0, 0)
            for n in range(WTP):
                cols = slice(n * KP * D // WTP, (n + 1) * KP * D // WTP)
                sp.dma_start(wraw[:, cols], wt[:, cols]).then_inc(wt_in[n], 16)
            load_x(1, 1)
            sp.dma_start(war[:], wa).then_inc(wa_in, 16)
            sp.dma_start(cs[:], cst).then_inc(cst_in, 16)
            sp.dma_start(bias[:], tb.broadcast_to([TT, D])).then_inc(small_in, 16)
            sp.dma_start(gam_sb[:], gam).then_inc(small_in, 16)
            sp.dma_start(lam_sb[:], lam.broadcast_to([128, 4, 8])).then_inc(small_in, 16)
            sp.dma_start(wg_sb[:], wg).then_inc(small_in, 16)
            with sp.Fori(1, NT // 2) as t:
                load_x(2 * t, 0)
                load_x(2 * t + 1, 1)
            sp.dma_start(wpr[:], wp).then_inc(wp_in, 16)

            def load_vx(n, c):
                tile = row(2 * c + n // 2)
                free = row(8 * c - 6 + 2 * n)
                sp.wait_ge(v_kept, NT)
                need(sp, weighed, free)
                r = 49 * (n % 2)
                for j in range(2):
                    sp.dma_start(vx[n][49 * j:49 * j + 49, j, :],
                                 vst[r:r + 49, bass.ds(tile, 1), :, :].rearrange("p a b c -> p (a b c)")).then_inc(vx_in[n], 16)

            def stack(c, cc):
                free = row(8 * (c - 1))
                for m in range(4):
                    dst = (Qs, Ks)[m // 2][cc]
                    jj = m % 2
                    made = row(4 * c + m + 1)
                    if m == 0:
                        need(sp, scored, free)
                    sp.wait_ge(part2, made)
                    sp.wait_ge(part1, made)
                    for r, part in enumerate((QPART, KPART)[m // 2]):
                        at_row = SLOT * jj + 8 * r
                        sp.dma_start(dst[at_row:at_row + 8, :, :], parts[:, m, part, :]).then_inc(stacked[cc], 16)

            sp.wait_ge(init_done, 1)
            stack(0, 0)
            for n in range(4):
                load_vx(n, 0)

            def chunk(c, cc, last=False):
                if not last:
                    stack(c + 1, 1 - cc)
                for p in range(2):
                    if not (isinstance(c, int) and c == 0):
                        store_h2(2 * c - 2 + p, p)
                    if not last:
                        load_vx(2 * p, c + 1)
                        load_vx(2 * p + 1, c + 1)

            def store_h2(pair, b):
                r = row(pair * TT)
                sp.wait_ge(h2_done, pair + 1)
                sp.dma_start(h2_dram[bass.ds(r, TT), :], h2[b][:]).then_inc(h2_out[b], 16)

            chunk(0, 0)
            chunk(1, 1)
            with sp.Fori(1, NCHUNK // 2 - 1) as s:
                chunk(2 * s, 0)
                chunk(2 * s + 1, 1)
            chunk(NCHUNK - 2, 0)
            chunk(NCHUNK - 1, 1, last=True)
            store_h2(NT - 2, 0)
            store_h2(NT - 1, 1)

            sp.wait_ge(logit_done, NT)
            for b in range(2):
                sp.wait_ge(h2_out[b], 16 * NT // 2)

            def stage(n, b, weights, at):
                at = row(at)
                need(sp, w_lo, n - 2)
                sp.dma_start(stg[b][:], weights[:, bass.ds(at, STG)]).then_inc(stg_in[b], 16)

            def load_h2r(t, b):
                r = row(t * TT)
                need(sp, sh_acc, t - 1)
                sp.dma_start(h2r[b][:], h2_dram[bass.ds(r, TT), :]).then_inc(h2_in[b], 16)

            def store_acc(t, b):
                r = row(t * TT)
                sp.wait_ge(sh_acc, t + 1)
                sp.dma_start(acc_dram[bass.ds(r, TT), :], acc[b][:]).then_inc(acc_out[b], 16)

            def shared_tiles(c, last):
                for tt in range(4):
                    if not (last and tt >= 2):
                        load_h2r(4 * c + tt + 2, tt % 2)
                    store_acc(4 * c + tt, tt % 2)

            for n in range(NS):
                stage(n, n, wsh, n * STG)
            load_h2r(0, 0)
            load_h2r(1, 1)
            for n in range(3):
                stage(NS + n, n, we, n * STG)
            for c in range(SH1):
                for n in range(NW // SH1 * c + 3, min(NW // SH1 * (c + 1) + 3, NW)):
                    stage(NS + n, n % 3, we, n * STG)
                shared_tiles(c, False)

            def load_block(b, q):
                r = row(b * BLK)
                need(sp, b_turned, b - 3)
                sp.dma_start(bx[q][:], slots_x[bass.ds(r, BLK), :]).then_inc(bx_in[q], 16)

            def store_block(b, q):
                r = row(b * BLK)
                sp.wait_ge(b_ykept, b + 1)
                sp.dma_start(slots_y[bass.ds(r, BLK), :], by[q][:]).then_inc(by_out[q], 16)

            sp.wait_ge(w_lo, NS + NW)
            sp.wait_ge(scattered, 16 * TOPK * NT)
            for b in range(6):
                load_block(b, b % 4)
            for b in range(2):
                store_block(b, b)
                load_block(b + 6, (b + 6) % 4)
            with sp.Fori(0, (NBLK - 8) // 4) as t:
                for q in range(4):
                    store_block(4 * t + 2 + q, (2 + q) % 4)
                    load_block(4 * t + 8 + q, q)
            for b in range(NBLK - 6, NBLK):
                store_block(b, b % 4)

            def load_acc(t, par):
                sp.wait_ge(acc_out[par], 16 * (t // 2 + 1))
                need(sp, part_sum, t - 1)
                sp.dma_start(accr[par][:], acc_dram[t * TT:(t + 1) * TT, :]).then_inc(acc_in[par], 16)

            def store_out(t, par):
                sp.wait_ge(fin_done, t + 1)
                sp.dma_start(out[t * TT:(t + 1) * TT, :], fin[par][:]).then_inc(fin_out[par], 16)

            load_acc(0, 0)
            load_acc(1, 1)
            for c in range(SH1, NSH):
                shared_tiles(c, c == NSH - 1)
                for t in range(4 * (c - SH1), 4 * (c - SH1) + 4):
                    load_acc(t + 2, t % 2)
                    store_out(t, t % 2)
            for t in range(4 * (NSH - SH1), NT):
                if t + 2 < NT:
                    load_acc(t + 2, t % 2)
                store_out(t, t % 2)
            sp.wait_ge(fin_out[0], 16 * NT // 2)
            sp.wait_ge(fin_out[1], 16 * NT // 2)

        @block.gpsimd
        def _(pool):
            def split_lo(i, b):
                pool.wait_ge(x_hi, i + 1)
                need(pool, embedded, i - 1)
                G.tensor_tensor(x_l[b][:], xr[b][:], x_h[b][:].bitcast(F32), ALU.subtract).then_inc(x_lo, 1)

            split_lo(0, 0)
            split_lo(1, 1)
            with pool.Fori(1, NT // 2) as t:
                split_lo(2 * t, 0)
                split_lo(2 * t + 1, 1)
            G.memset(zero[:], 0.0).then_inc(pool_init, 1)
            G.memset(three[:], 3.0).then_inc(pool_init, 1)
            G.memset(woff[:], 0).then_inc(pool_init, 1)
            G.memset(vst[:, :, :, 32:VW], 1.0).then_inc(pool_init, 1)
            for n in range(4):
                G.memset(vx[n][:], 0.0).then_inc(pool_init, 1)

            zx = slots_x.rearrange("(n p r) d -> n p (r d)", p=128, r=5)

            def norm_tile(tile, b):
                pool.wait_ge(att_done, 4 * tile + 4)
                need(pool, ms_done, tile)
                a = att[b][:].rearrange("p i h d -> p (i h) d")
                G.tensor_tensor(sq[:], a, a, ALU.mult).then_inc(sq_done, 1)
                pool.wait_ge(r0_done, tile + 1)
                G.tensor_tensor(nt1[:], r0[:], r0[:], ALU.mult).then_inc(newton, 1)
                pool.wait_ge(newton, 4 * tile + 1)
                G.tensor_tensor(nt2[:], nt1[:], ms2[:], ALU.mult).then_inc(newton, 1)
                pool.wait_ge(newton, 4 * tile + 2)
                G.tensor_tensor(nt3[:], three[:], nt2[:], ALU.subtract).then_inc(newton, 1)
                pool.wait_ge(newton, 4 * tile + 3)
                G.tensor_tensor(rr[:], r0[:], nt3[:], ALU.mult).then_inc(newton, 1)
                pool.wait_ge(newton, 4 * tile + 4)
                need(pool, ao_turned, tile)
                G.tensor_tensor(ao[:].rearrange("p i h d -> p (i h) d"), a,
                                bc(rr[:].unsqueeze(2), [128, 2 * HP, 16]), ALU.mult).then_inc(ao_done, 1)

            pool.wait_ge(pool_init, 8)
            with pool.Fori(0, NZ) as t:
                G.dma_start(zx[bass.ds(t, 1)].rearrange("a p n -> (a p) n"), zero[:]).then_inc(zeroed, 16)
                norm_tile(2 * t, 0)
                norm_tile(2 * t + 1, 1)
            pool.wait_ge(slots_known, 1)
            pool.wait_ge(zeroed, 16 * NZ)
            for k in range(TOPK):
                for i in range(NT):
                    G.indirect_dma_start(out=slots_x, out_offset=bass.IndirectOffsetOnAxis(ap=slot_u[:, k, i:i + 1], axis=0),
                                         in_=hn2[:, i, :], in_offset=None).then_inc(scattered, 16)
            for q in range(4):
                pool.wait_ge(by_out[q], 16 * NBLK // 4)
            for i in range(NT):
                if i >= YR:
                    pool.wait_ge(fin_done, i - YR + 1)
                for k in range(TOPK):
                    G.indirect_dma_start(out=hn2[:, TOPK * (i % YR) + k, :], out_offset=None, in_=slots_y,
                                         in_offset=bass.IndirectOffsetOnAxis(ap=slot_u[:, k, i:i + 1], axis=0)).then_inc(y_in[i % YR], 16)

        @block.scalar
        def _(act):
            A.preload_act_table_set("natural_log_exp_and_others")
            for n in range(WTP):
                k = slice(n * KP // WTP, (n + 1) * KP // WTP)
                if n == 0:
                    act.wait_ge(x_in[0], 16)
                    A.activation(x_h[0][:], xr[0][:], ACT.Copy).then_inc(x_hi, 1)
                act.wait_ge(wt_in[n], 16)
                A.activation(wt_h[:, k], wraw[:].rearrange("p (k n) -> p k n", k=KP)[:, k], ACT.Copy).then_inc(wt_hi, 1)

            def split_x(i, b):
                if isinstance(i, int) and i == 0:
                    return
                act.wait_ge(x_in[b], 8 * i + 16 - 8 * b)
                need(act, embedded, i - 1)
                A.activation(x_h[b][:], xr[b][:], ACT.Copy).then_inc(x_hi, 1)

            def split_wa(i, b):
                if isinstance(i, int) and i == 2:
                    act.wait_ge(wa_in, 16)
                    A.activation(wa_h[:], war[:], ACT.Copy).then_inc(wa_hi, 1)

            def guess(i, b):
                act.wait_ge(h_var, i + 1)
                A.activation(ln1[b][:], ve1[b][:], ACT.Ln).then_inc(h_ln, 1)
                act.wait_ge(h_ln, i + 1)
                need(act, h_newton, 3 * i - 3)
                A.activation(y1[b][:], ln1[b][:], ACT.Exp, scale=-0.5).then_inc(h_guess, 1)

            def keep_hT(i, b):
                act.wait_ge(hn_turned, i + 1)
                A.activation(hT_h[:, :, bass.ds(i * TT, TT)],
                             bank[4 + b][:, 0:KD * TT].rearrange("p (k t) -> p k t", k=KD), ACT.Copy).then_inc(hT_hi, 1)

            embedding(act, [(1, split_x), (0, guess), (-2, keep_hT), (0, split_wa)])
            act.wait_ge(lam_b, 1)
            A.activation(laml[:], lam2[:], ACT.Exp).then_inc(lam_c, 1)
            act.wait_ge(wp_g, 1)
            A.activation(wp_h[:], wpg[:], ACT.Copy).then_inc(wp_hi, 1)

            def qk(c, m, cc):
                act.wait_ge(qk_made, 4 * c + m + 1)
                need(act, stacked[1 - cc], 192 * (c + cc))
                A.activation(parts[:, m, 0, :], bank[6 + m % 2][:, 0:CHUNK], ACT.Copy,
                             scale=0.125 if m < 2 else 1.0).then_inc(part0, 1)
                act.wait_ge(rest1, 4 * c + m + 1)
                A.activation(parts[:, m, 1, :], rest[m % 2][:], ACT.Copy).then_inc(part1, 1)

            for m in range(4):
                qk(0, m, 0)
            act.wait_ge(pool_init, 8)
            for i in range(NT):
                act.wait_ge(v_made, i + 1)
                A.activation(vst[:, i, :, 0:32], bank[4 + i % 2][0:TT, 0:D].rearrange("p (h n) -> p h n", h=HP),
                             ACT.Copy).then_inc(v_kept, 1)

            def exp_half(c, k, cc):
                u, b = 8 * c + k, k % 2
                act.wait_ge(turned, u + 1)
                need(act, weighed, u - 1)
                A.activation(PT[b][:].rearrange("p a t -> p (a t)"), bank[2 + b][0:TT, :], ACT.Exp).then_inc(exped, 1)

            def post(what, tile, b, c, k, last):
                if what == "R":
                    act.wait_ge(ms2_done, tile + 1)
                    A.activation(lnr[:], ms2[:], ACT.Ln).then_inc(ln_done, 1)
                    act.wait_ge(ln_done, tile + 1)
                    need(act, newton, 4 * tile)
                    A.activation(r0[:], lnr[:], ACT.Exp, scale=-0.5).then_inc(r0_done, 1)
                elif what == "A":
                    act.wait_ge(ao_turned, tile + 1)
                    need(act, projected, tile)
                    A.activation(aT_h[:], bank[6][:, 0:256].rearrange("p (i j t) -> p j i t", i=2, j=2)[:, :, :, 0:S],
                                 ACT.Copy).then_inc(aT_hi, 1)
                elif what == "P":
                    act.wait_ge(ve2_done, tile + 1)
                    A.activation(ln2[:], ve2[:], ACT.Ln).then_inc(ln2_done, 1)
                    act.wait_ge(ln2_done, tile + 1)
                    need(act, newton2, 4 * tile)
                    A.activation(q0[:], ln2[:], ACT.Exp, scale=-0.5).then_inc(q0_done, 1)
                elif what == "N":
                    act.wait_ge(hn2_done, tile + 1)
                    A.activation(hn2[:, bass.ds(tile, 1), :].rearrange("p a n -> p (a n)"), hn2w[b][:], ACT.Copy).then_inc(hn2_kept, 1)
                    act.wait_ge(hn2_turned, tile + 1)
                    need(act, h2T_lo, tile)
                    need(act, gated, tile)
                    A.activation(h2T[:].rearrange("p k t -> p (k t)"), bank[6][:, 0:KD * TT], ACT.Copy).then_inc(h2T_done, 1)

            attention(act, [(1, exp_half), "rest"], qk=qk, post=post)

            act.wait_ge(gate_diff, 1)
            A.activation(ed[:], dl[:], ACT.Exp).then_inc(e_exp, 1)
            A.activation(ez[:], logits[:, :, E], ACT.Exp, scale=-1.0).then_inc(e_exp, 1)

            def split_hi(n, b, dst):
                act.wait_ge(stg_in[b], 16 * ((n - b) // 3 + 1) if isinstance(n, int) else 16 * (n + 1))
                A.activation(dst, stg[b][:], ACT.Copy).then_inc(w_hi, 1)

            for n in range(NS):
                split_hi(n, n, wsh_h[:, n * STG:(n + 1) * STG])
            def shared_chunk(c, split):
                for b in range(SB):
                    u = SB * c + b
                    act.wait_ge(sh_g, u + 1)
                    act.wait_ge(sh_h, u)
                    A.activation(sgl[:], bank[(2 * b) % 4][:, 0:SH], ACT.Silu).then_inc(sh_silu, 1)
                    act.wait_ge(sh_h, u + 1)
                    act.wait_ge(sh_y, 4 * c)
                    A.activation(hs_h[:, b, :], hs[:], ACT.Copy).then_inc(sh_hi, 1)
                    for j in (SPLITS[b] if split else ()):
                        act.wait_ge(stg_in[j % 3], 32 * c + 32 + 16 * (j // 3))
                        A.activation(we_h[:, bass.ds((NW // SH1 * c + j) * STG, STG)], stg[j % 3][:], ACT.Copy).then_inc(w_hi, 1)

            with act.Fori(0, SH1) as c:
                shared_chunk(c, True)

            def block_hi(b, q):
                par = q % 2
                act.wait_ge(b_turned, b + 1)
                need(act, b_gu, b - 1)
                A.activation(bxT_h[par][:].rearrange("p k t -> p (k t)"), bank[par][:, 0:D], ACT.Copy).then_inc(b_hi, 1)

            def block_silu(b, q):
                par = q % 2
                act.wait_ge(b_gu, b + 1)
                need(act, b_h, b - 1)
                A.activation(bsg[par][:], bank[2 + par][:, 0:HID], ACT.Silu).then_inc(b_silu, 1)

            def block_hhi(b, q):
                par = q % 2
                act.wait_ge(b_hturned, b + 1)
                need(act, b_y, b - 1)
                A.activation(bhT_h[par][:], bank[4 + par][:, 0:BLK], ACT.Copy).then_inc(b_hhi, 1)

            def block_keep(b, q):
                act.wait_ge(b_y, b + 1)
                need(act, by_out[q], 4 * b - 4 * q)
                A.activation(by[q][:], bank[6 + q % 2][:, 0:D], ACT.Copy).then_inc(b_ykept, 1)

            blocks(act, [(1, block_hi), (0, block_silu), (-1, block_hhi), (-2, block_keep)])
            with act.Fori(SH1, NSH) as c:
                shared_chunk(c, False)

        @block.vector
        def _(dve):
            for n in range(WTP):
                k = slice(n * KP // WTP, (n + 1) * KP // WTP)
                dve.wait_ge(wt_hi, n + 1)
                V.tensor_tensor(wt_l[:, k], wraw[:].rearrange("p (k n) -> p k n", k=KP)[:, k],
                                wt_h[:, k].bitcast(F32), ALU.subtract).then_inc(wt_lo, 1)
            dve.wait_ge(small_in, 64)

            def h_of(i):
                return h[:, bass.ds(i, 1), :].rearrange("p a n -> p (a n)")

            def embed_out(i, b):
                dve.wait_ge(embedded, i + 1)
                V.tensor_tensor(h_of(i), bank[6 + b][0:TT, 0:D], bias[:], ALU.add).then_inc(h_done, 1)

            def stats(i, b):
                dve.wait_ge(small_in, 64)
                dve.wait_ge(h_done, i + 1)
                V.bn_stats(st1[b][:], h_of(i)).then_inc(h_stats, 1)

            def aggregate(i, b):
                dve.wait_ge(small_in, 64)
                dve.wait_ge(h_stats, i + 1)
                V.bn_aggr(mv1[b][:], st1[b][:]).then_inc(h_aggr, 1)

            def variance(i, b):
                dve.wait_ge(h_aggr, i + 1)
                V.tensor_scalar(ve1[b][:], mv1[b][:, 1:2], EPS, None, ALU.add).then_inc(h_var, 1)

            def newton_a(i, b):
                dve.wait_ge(h_guess, i + 1)
                V.scalar_tensor_tensor(yx1[b][:], y1[b][:], ve1[b][:], y1[b][:], ALU.mult, ALU.mult).then_inc(h_newton, 1)

            def newton_b(i, b):
                dve.wait_ge(h_newton, 3 * i + 1)
                V.tensor_scalar(yn1[b][:], yx1[b][:], -0.5, 1.5, ALU.mult, ALU.add).then_inc(h_newton, 1)

            def newton_c(i, b):
                dve.wait_ge(h_newton, 3 * i + 2)
                V.tensor_tensor(rs1[b][:], y1[b][:], yn1[b][:], ALU.mult).then_inc(h_newton, 1)

            def norm(i, b):
                dve.wait_ge(h_newton, 3 * i + 3)
                need(dve, hn_turned, i - 1)
                V.tensor_scalar(hn[b][:], h_of(i), mv1[b][:, 0:1], rs1[b][:], ALU.subtract, ALU.mult).then_inc(hn_done, 1)

            def keep_lo(i, b):
                dve.wait_ge(hT_hi, i + 1)
                V.tensor_tensor(hT_l[:, :, bass.ds(i * TT, TT)],
                                bank[4 + b][:, 0:KD * TT].rearrange("p (k t) -> p k t", k=KD),
                                hT_h[:, :, bass.ds(i * TT, TT)].bitcast(F32), ALU.subtract).then_inc(hT_lo, 1)

            def split_wa(i, b):
                if isinstance(i, int) and i == 2:
                    dve.wait_ge(wa_hi, 1)
                    V.tensor_tensor(wa_l[:], war[:], wa_h[:].bitcast(F32), ALU.subtract).then_inc(wa_lo, 1)

            embedding(dve, [(-1, newton_a), (0, embed_out), (-1, newton_b), (0, stats), (-1, newton_c), (0, aggregate),
                            (-1, norm), (0, variance), (-2, keep_lo), (0, split_wa)])

            V.tensor_tensor(lamt[:], lam_sb[:, 0:2, :], lam_sb[:, 2:4, :], ALU.mult).then_inc(lam_a, 1)
            dve.wait_ge(lam_a, 1)
            V.tensor_reduce(lam2[:], lamt[:], AX.X, ALU.add).then_inc(lam_b, 1)
            dve.wait_ge(lam_c, 1)
            V.tensor_tensor(lamd[:], laml[:, 1:2], laml[:, 0:1], ALU.subtract).then_inc(lam_d, 1)
            dve.wait_ge(lam_d, 1)
            V.tensor_scalar(neglam[:], lamd[:], -LAMBDA_INIT, None, ALU.add).then_inc(lam_e, 1)
            dve.wait_ge(wp_in, 16)
            V.tensor_scalar(wpg[:], wpr[:], gam_sb[:], (1.0 - LAMBDA_INIT) / 2, ALU.mult, ALU.mult).then_inc(wp_g, 1)
            dve.wait_ge(cst_in, 16)
            V.tensor_copy(sel_bf[:], cs[0:S, C_SEL:C_SEL + 128]).then_inc(init_done, 1)
            V.tensor_copy(mask_bf[:], bc(cs[0:S, C_MASK:C_MASK + S].unsqueeze(1), [S, 8, S])).then_inc(init_done, 1)
            V.tensor_copy(one_bf[:], cs[:, C_ONE:C_ONE + 128]).then_inc(init_done, 1)
            V.tensor_copy(up_bf[:], cs[:, C_UP:C_UP + 128]).then_inc(init_done, 1)

            dve.wait_ge(wp_hi, 1)
            V.tensor_tensor(wp_l[:], wpg[:], wp_h[:].bitcast(F32), ALU.subtract).then_inc(wp_lo, 1)

            def qk(c, m, cc):
                scale = 0.125 if m < 2 else 1.0
                dve.wait_ge(part0, 4 * c + m + 1)
                V.scalar_tensor_tensor(rest[m % 2][:], bank[6 + m % 2][:, 0:CHUNK], scale, parts[:, m, 0, :],
                                       ALU.mult, ALU.subtract).then_inc(rest1, 1)
                dve.wait_ge(part1, 4 * c + m + 1)
                V.tensor_tensor(parts[:, m, 2, :], rest[m % 2][:], parts[:, m, 1, :], ALU.subtract).then_inc(part2, 1)

            for m in range(4):
                qk(0, m, 0)

            dve.wait_ge(lam_e, 1)

            def halves(c, k):
                return 8 * c + k, k % 2, bank[k % 2][:, 0:8 * S].rearrange("p (m s) -> p m s", m=8)

            def row_max(c, k, cc):
                u, b, s3 = halves(c, k)
                dve.wait_ge(scored, u + 1)
                V.tensor_reduce(smax[b][:], s3, AX.X, ALU.max).then_inc(maxed, 1)

            def centre(c, k, cc):
                u, b, s3 = halves(c, k)
                dve.wait_ge(maxed, u + 1)
                need(dve, turned, u - 1)
                V.tensor_tensor(Sm[b][:].rearrange("p m (j s) -> p (m j) s", j=2), s3,
                                bc(smax[b][:].unsqueeze(2), [128, 8, S]), ALU.subtract).then_inc(centred, 1)

            def products(b):
                return bank[4 + b][:, 0:4 * 2 * VW].rearrange("p (m n) -> p m n", n=VW)

            def row_sums(c, k, cc):
                u, b = 8 * c + k, k % 2
                dve.wait_ge(weighed, u + 1)
                V.reciprocal(rz[:], products(b)[:, :, 32]).then_inc(rz_done, 1)

            def normalise(c, k, cc):
                u, b = 8 * c + k, k % 2
                dve.wait_ge(rz_done, u + 1)
                for jj in range(2):
                    r = slice(SLOT * jj, SLOT * jj + SLOT)
                    V.tensor_tensor(on[r, :, :], products(b)[r, :, 16 * jj:16 * jj + 16],
                                    bc(rz[r, :].unsqueeze(2), [SLOT, 8, 16]), ALU.mult).then_inc(on_done, 1)

            def difference(c, k, cc):
                u, b, tile, tb_, img = 8 * c + k, k % 2, 2 * c + k // 4, k // 4, k // 2 % 2
                dve.wait_ge(on_done, 2 * u + 2)
                o4 = on[:].rearrange("p (m j) d -> p m j d", j=2)
                need(dve, ao_done, tile - 1)
                V.scalar_tensor_tensor(att[tb_][:, img, 4 * b:4 * b + 4, :], o4[:, :, 1, :], neglam[:, 0:1], o4[:, :, 0, :],
                                       ALU.mult, ALU.add).then_inc(att_done, 1)

            def newton_step(s, tile, x, y0, a1, a2, a3, y):
                V.tensor_tensor(a1, y0, y0, ALU.mult).then_inc(s, 1)
                dve.wait_ge(s, 4 * tile + 1)
                V.tensor_tensor(a2, a1, x, ALU.mult).then_inc(s, 1)
                dve.wait_ge(s, 4 * tile + 2)
                V.tensor_scalar(a3, a2, -0.5, 1.5, ALU.mult, ALU.add).then_inc(s, 1)
                dve.wait_ge(s, 4 * tile + 3)
                V.tensor_tensor(y, y0, a3, ALU.mult).then_inc(s, 1)

            def post(what, tile, b, c, k, last):
                if what == "R":
                    dve.wait_ge(sq_done, tile + 1)
                    V.tensor_reduce(ms[:], sq[:], AX.X, ALU.add).then_inc(ms_done, 1)
                    dve.wait_ge(ms_done, tile + 1)
                    V.tensor_scalar(ms2[:], ms[:], 1.0 / 16.0, EPS, ALU.mult, ALU.add).then_inc(ms2_done, 1)
                elif what == "A":
                    dve.wait_ge(aT_hi, tile + 1)
                    V.tensor_tensor(aT_l[:], bank[6][:, 0:256].rearrange("p (i j t) -> p j i t", i=2, j=2)[:, :, :, 0:S],
                                    aT_h[:].bitcast(F32), ALU.subtract).then_inc(aT_lo, 1)
                elif what == "P":
                    dve.wait_ge(projected, tile + 1)
                    need(dve, h2_out[b], 8 * tile - 8 * b)
                    V.tensor_tensor(h2[b][:], bank[7][0:TT, 0:D], h[:, bass.ds(tile, 1), :].rearrange("p a n -> p (a n)"),
                                    ALU.add).then_inc(h2_done, 1)
                    dve.wait_ge(h2_done, tile + 1)
                    V.bn_stats(st2[:], h2[b][:]).then_inc(st2_done, 1)
                    dve.wait_ge(small_in, 64)
                    dve.wait_ge(st2_done, tile + 1)
                    V.bn_aggr(mv2[:], st2[:]).then_inc(mv2_done, 1)
                    dve.wait_ge(mv2_done, tile + 1)
                    V.tensor_scalar(ve2[:], mv2[:, 1:2], EPS, None, ALU.add).then_inc(ve2_done, 1)
                    dve.wait_ge(q0_done, tile + 1)
                    newton_step(newton2, tile, ve2[:], q0[:], q1[:], q2[:], q3[:], rs2[:])
                    dve.wait_ge(newton2, 4 * tile + 4)
                    need(dve, hn2_turned, tile - 1)
                    need(dve, hn2_kept, tile - 1)
                    V.tensor_scalar(hn2w[b][:], h2[b][:], mv2[:, 0:1], rs2[:],
                                    ALU.subtract, ALU.mult).then_inc(hn2_done, 1)
                elif what == "N":
                    dve.wait_ge(h2T_done, tile + 1)
                    tok = bass.ds(tile * TT, TT)
                    V.tensor_copy(hn2T_h[:, :, tok], h2T[:]).then_inc(h2T_hi, 1)
                    dve.wait_ge(h2T_hi, tile + 1)
                    V.tensor_tensor(hn2T_l[:, :, tok], h2T[:], hn2T_h[:, :, tok].bitcast(F32), ALU.subtract).then_inc(h2T_lo, 1)
                elif what == "G":
                    dve.wait_ge(gated, tile + 1)
                    V.tensor_copy(logits[:, bass.ds(tile, 1), :].rearrange("p a n -> p (a n)"),
                                  bank[7][0:TT, 0:E + 1]).then_inc(logit_done, 1)

            attention(dve, [(0, row_max), (2, row_sums), (0, centre), (2, normalise), "rest", (2, difference)], qk=qk, post=post)

            dve.wait_ge(h2_out[0], 16 * NT // 2)
            dve.wait_ge(h2_out[1], 16 * NT // 2)
            dve.wait_ge(logit_done, NT)
            dve.wait_ge(zeroed, 16 * NZ)
            done = [0]

            def link(ins):
                done[0] += 1
                ins.then_inc(routing, 1)
                dve.wait_ge(routing, done[0])

            for i in range(NT):
                V.max(mx8[:, i, :], logits[:, i, 0:E]).then_inc(routing, 1)
            done[0] += NT
            dve.wait_ge(routing, done[0])
            for i in range(NT):
                V.max_index(ix8[:, i, :], mx8[:, i, :], logits[:, i, 0:E]).then_inc(routing, 1)
            V.tensor_tensor(dl[:], mx8[:, :, 1], mx8[:, :, 0], ALU.subtract).then_inc(gate_diff, 1)
            done[0] += NT
            dve.wait_ge(routing, done[0])
            link(V.tensor_copy(ixf[:], ix8[:, :, 0:TOPK].rearrange("p i k -> p k i")))
            iota = cs[0:TT, C_IOTA:C_IOTA + E]
            for k in range(TOPK):
                link(V.tensor_tensor(oh[:, k], bc(iota.unsqueeze(2), [TT, E, NT]), bc(ixf[:, k:k + 1, :], [TT, E, NT]), ALU.is_equal))
            V.tensor_tensor(both[:], oh[:, 0], oh[:, 1], ALU.add).then_inc(chosen, 1)
            dve.wait_ge(counted, 1)
            tot = bank[1][0:TT, 0:E * NT]
            link(V.tensor_tensor_scan(cuminc[:].rearrange("p e i -> p (e i)"), cs[0:TT, C_RESET:C_RESET + E * NT], tot, 0.0, ALU.mult, ALU.add))
            link(V.tensor_tensor(excl[:].rearrange("p e i -> p (e i)"), cuminc[:].rearrange("p e i -> p (e i)"), tot, ALU.subtract))
            link(V.tensor_scalar(cnt[:], cuminc[:, :, NT - 1], float(BLK - 1), None, ALU.add))
            link(V.tensor_scalar(cnts[:], cnt[:], 7, None, ALU.logical_shift_right))
            link(V.tensor_copy(nblk[:], cnts[:]))
            link(V.tensor_tensor_scan(cumb[:], cs[0:TT, C_ONE:C_ONE + E], nblk[:], 0.0, ALU.mult, ALU.add))
            link(V.tensor_tensor(base[:], cumb[:], nblk[:], ALU.subtract))
            link(V.tensor_tensor(slotf[:].rearrange("p e i -> p (e i)"), bank[0][0:TT, 0:E * NT], excl[:].rearrange("p e i -> p (e i)"), ALU.add))
            link(V.scalar_tensor_tensor(slot2[:], bc(base[:].unsqueeze(2), [TT, E, NT]), float(BLK), slotf[:], ALU.mult, ALU.add))
            for k in range(TOPK):
                link(V.tensor_tensor(slotf[:], oh[:, k], slot2[:], ALU.mult))
                link(V.tensor_reduce(slotr[:, k], slotf[:].rearrange("p e i -> p i e"), AX.X, ALU.add))
            V.tensor_copy(slot_u[:], slotr[:]).then_inc(slots_known, 1)
            link(V.tensor_tensor(ecmp[:], bc(cumb[0:1, :].unsqueeze(1), [1, NBLK, E]),
                                 bc(cs[0:1, C_BLK:C_BLK + NBLK].unsqueeze(2), [1, NBLK, E]), ALU.is_le))
            link(V.tensor_reduce(esum[:], ecmp[:], AX.X, ALU.add))
            link(V.tensor_scalar(eid[:].rearrange("p a b -> p (a b)"), esum[:], float(E - 1), None, ALU.min))
            nq = NBLK // 4
            V.tensor_scalar(woff[:, 0:nq, 0:4], eid[:], float(KD * 2 * HID), None, ALU.mult).then_inc(eids_known, 1)
            V.tensor_scalar(woff[:, 1:nq + 1, 4:6], eid[:, :, 2:4], float(D), float(EGU), ALU.mult, ALU.add).then_inc(eids_known, 1)
            V.tensor_scalar(woff[:, 0:nq, 6:8], eid[:, :, 0:2], float(D), float(EGU), ALU.mult, ALU.add).then_inc(eids_known, 1)
            dve.wait_ge(e_exp, 2)
            link(V.tensor_scalar(ed1[:], ed[:], 1.0, None, ALU.add))
            link(V.reciprocal(w1[:], ed1[:]))
            V.tensor_tensor(w2[:], w1[:], ed[:], ALU.mult).then_inc(weights_known, 1)
            link(V.tensor_scalar(ez1[:], ez[:], 1.0, None, ALU.add))
            V.reciprocal(sig[:], ez1[:]).then_inc(weights_known, 1)

            for n in range(NS):
                dve.wait_ge(w_hi, n + 1)
                V.tensor_tensor(wsh_l[:, n * STG:(n + 1) * STG], stg[n][:], wsh_h[:, n * STG:(n + 1) * STG].bitcast(F32),
                                ALU.subtract).then_inc(w_lo, 1)
            dve.wait_ge(weights_known, 2)
            def shared_chunk(c, split):
                for b in range(SB):
                    u = SB * c + b
                    dve.wait_ge(sh_silu, u + 1)
                    dve.wait_ge(sh_u, u + 1)
                    dve.wait_ge(sh_hi, u)
                    dve.wait_ge(sh_lo, u)
                    V.tensor_tensor(hs[:], sgl[:], bank[(2 * b + 1) % 4][:, 0:SH], ALU.mult).then_inc(sh_h, 1)
                    dve.wait_ge(sh_hi, u + 1)
                    dve.wait_ge(sh_y, 4 * c)
                    V.tensor_tensor(hs_l[:, b, :], hs[:], hs_h[:, b, :].bitcast(F32), ALU.subtract).then_inc(sh_lo, 1)
                    for j in (SPLITS[b] if split else ()):
                        n = NW // SH1 * c + j
                        dve.wait_ge(w_hi, NS + n + 1)
                        V.tensor_tensor(we_l[:, bass.ds(n * STG, STG)], stg[j % 3][:], we_h[:, bass.ds(n * STG, STG)].bitcast(F32),
                                        ALU.subtract).then_inc(w_lo, 1)
                for tt in range(4):
                    t = 4 * c + tt
                    dve.wait_ge(sh_y, t + 1)
                    dve.wait_ge(h2_in[tt % 2], 32 * c + 16 * (tt // 2) + 16)
                    dve.wait_ge(acc_out[tt % 2], 32 * c + 16 * (tt // 2))
                    V.scalar_tensor_tensor(acc[tt % 2][:], bank[4 + tt % 2][0:TT, 0:D], sig[:, bass.ds(t, 1)], h2r[tt % 2][:],
                                           ALU.mult, ALU.add).then_inc(sh_acc, 1)

            with dve.Fori(0, SH1) as c:
                shared_chunk(c, True)

            def block_lo(b, q):
                par = q % 2
                dve.wait_ge(b_hi, b + 1)
                V.tensor_tensor(bxT_l[par][:].rearrange("p k t -> p (k t)"), bank[par][:, 0:D],
                                bxT_h[par][:].rearrange("p k t -> p (k t)").bitcast(F32), ALU.subtract).then_inc(b_lo, 1)

            def block_h(b, q):
                par = q % 2
                dve.wait_ge(b_silu, b + 1)
                need(dve, b_hturned, b - 1)
                V.tensor_tensor(bh[par][:], bsg[par][:], bank[2 + par][:, HID:2 * HID], ALU.mult).then_inc(b_h, 1)

            def block_hlo(b, q):
                par = q % 2
                dve.wait_ge(b_hhi, b + 1)
                V.tensor_tensor(bhT_l[par][:], bank[4 + par][:, 0:BLK], bhT_h[par][:].bitcast(F32), ALU.subtract).then_inc(b_hlo, 1)

            blocks(dve, [(1, block_lo), (0, block_h), (-1, block_hlo)])

            def combine(t):
                par, y = t % 2, TOPK * (t % YR)
                dve.wait_ge(acc_in[par], 16 * (t // 2 + 1))
                dve.wait_ge(y_in[t % YR], 32 * (t // YR + 1))
                need(dve, fin_done, t - 1)
                V.scalar_tensor_tensor(psum1[par][:], hn2[:, y, :], w1[:, t:t + 1], accr[par][:], ALU.mult, ALU.add).then_inc(part_sum, 1)
                dve.wait_ge(part_sum, t + 1)
                need(dve, fin_out[par], 16 * (t // 2))
                V.scalar_tensor_tensor(fin[par][:], hn2[:, y + 1, :], w2[:, t:t + 1], psum1[par][:], ALU.mult, ALU.add).then_inc(fin_done, 1)

            for c in range(SH1, NSH):
                shared_chunk(c, False)
                for t in range(4 * (c - SH1), 4 * (c - SH1) + 4):
                    combine(t)
            for t in range(4 * (NSH - SH1), NT):
                combine(t)

        @block.tensor
        def _(pe):
            def product(out, pairs):
                n = 3 * len(pairs)
                for m, (lh, ll, rh, rl) in enumerate(pairs):
                    for q, (a, b) in enumerate(((lh, rh), (lh, rl), (ll, rh))):
                        last = T.matmul(out, a, b, start=(3 * m + q == 0), stop=(3 * m + q == n - 1))
                return last

            def embed(i, b):
                pe.wait_ge(x_lo, i + 1)
                need(pe, h_done, i - 1)
                for k in range(KP):
                    if isinstance(i, int) and i == 0 and k % (KP // WTP) == 0:
                        pe.wait_ge(wt_lo, k // (KP // WTP) + 1)
                    xh, xl, wh, wl = x_h[b][:, k, :], x_l[b][:, k, :], wt_h[:, k, :], wt_l[:, k, :]
                    for q, (lhs, rhs) in enumerate(((xh, wh), (xh, wl), (xl, wh))):
                        last = T.matmul(bank[6 + b][0:TT, 0:D], lhs, rhs, start=(k == 0 and q == 0), stop=(k == KP - 1 and q == 2))
                last.then_inc(embedded, 1)

            def turn_hn(i, b):
                pe.wait_ge(cst_in, 16)
                pe.wait_ge(hn_done, i + 1)
                need(pe, hT_lo, i - 1)
                for k in range(KD):
                    last = T.transpose(bank[4 + b][:, k * TT:(k + 1) * TT], hn[b][:, k * 128:(k + 1) * 128], ident[0:TT, 0:TT])
                last.then_inc(hn_turned, 1)

            embedding(pe, [(0, embed), (-2, turn_hn)])
            pe.wait_ge(wa_lo, 1)
            pe.wait_ge(hT_lo, NT)

            def qk(c, m, cc):
                need(pe, rest1, 4 * c + m - 1)
                need(pe, (aT_lo, h2_done, h2T_done, logit_done)[m], 2 * c - 3)
                tok = bass.ds(c * CHUNK, CHUNK)
                w = slice(m * 128, (m + 1) * 128)
                product(bank[6 + m % 2][:, 0:CHUNK], [(wa_h[:, k, w], wa_l[:, k, w], hT_h[:, k, tok], hT_l[:, k, tok])
                                                      for k in range(KD)]).then_inc(qk_made, 1)

            for m in range(4):
                qk(0, m, 0)
            for i in range(NT):
                need(pe, v_kept, i - 1)
                tok = slice(i * TT, (i + 1) * TT)
                product(bank[4 + i % 2][0:TT, 0:D], [(hT_h[:, k, tok], hT_l[:, k, tok], wa_h[:, k, 2 * D:], wa_l[:, k, 2 * D:])
                                                     for k in range(KD)]).then_inc(v_made, 1)
            pe.wait_ge(v_kept, NT)
            pe.wait_ge(init_done, 4)
            pe.wait_ge(wp_lo, 1)
            pe.wait_ge(small_in, 64)

            def scores(c, k, cc):
                u, b, n = 8 * c + k, k % 2, k // 2
                pe.wait_ge(stacked[cc], 192 * c - 192 * cc + 384)
                need(pe, centred, u - 1)
                T.matmul(bank[b][:, 0:8 * S], sel_bf[:], mask_bf[:].rearrange("p m s -> p (m s)"), start=True, stop=False, skip_group_check=True)
                for m in range(8):
                    for jj in range(2):
                        r = slice(SLOT * jj, SLOT * jj + 8 * PARTS)
                        q = 8 * b + m
                        last = T.matmul(bank[b][SLOT * jj:SLOT * jj + S, m * S:(m + 1) * S], Qs[cc][r, q, n * S:(n + 1) * S],
                                        Ks[cc][r, q, n * S:(n + 1) * S], start=False, stop=(m == 7), skip_group_check=True)
                last.then_inc(scored, 1)

            def turn(c, k, cc):
                u, b = 8 * c + k, k % 2
                pe.wait_ge(centred, u + 1)
                need(pe, exped, u - 1)
                for m in range(4):
                    last = T.transpose(bank[2 + b][0:TT, m * 128:(m + 1) * 128], Sm[b][:, m, :], ident)
                last.then_inc(turned, 1)

            def weigh(c, k, cc):
                u, b, n = 8 * c + k, k % 2, k // 2
                pe.wait_ge(exped, u + 1)
                pe.wait_ge(vx_in[n], 32 * c + 32)
                need(pe, on_done, 2 * (u - 1))
                for m in range(4):
                    h0 = (4 * b + m) * VW
                    last = T.matmul(bank[4 + b][:, m * 2 * VW:(m + 1) * 2 * VW].rearrange("p (j n) -> p j n", j=2), PT[b][:, m, :],
                                    vx[n][:, :, h0:h0 + VW], start=True, stop=True)
                last.then_inc(weighed, 1)

            def post(what, tile, b, c, k, last):
                made6 = 4 * c + 4 + (1, 1, 3, 3, 3, 3, 3, 3)[k] if not last else 4 * NCHUNK
                made7 = 4 * c + 4 + (0, 2, 2, 4, 4, 4, 4, 4)[k] if not last else 4 * NCHUNK
                if what == "A":
                    pe.wait_ge(ao_done, tile + 1)
                    pe.wait_ge(rest1, made6)
                    need(pe, h2T_done, tile)
                    for i in range(2):
                        end = T.transpose(bank[6][:, i * 128:(i + 1) * 128], ao[:, i, :, :].rearrange("p h d -> p (h d)"), ident)
                    end.then_inc(ao_turned, 1)
                elif what == "P":
                    pe.wait_ge(aT_lo, tile + 1)
                    pe.wait_ge(rest1, made7)
                    need(pe, logit_done, tile)
                    product(bank[7][0:TT, 0:D], [(aT_h[:, j].rearrange("p i t -> p (i t)"), aT_l[:, j].rearrange("p i t -> p (i t)"), wp_h[:, j, :], wp_l[:, j, :])
                                                 for j in range(2)]).then_inc(projected, 1)
                elif what == "N":
                    pe.wait_ge(hn2_done, tile + 1)
                    pe.wait_ge(rest1, made6)
                    pe.wait_ge(aT_lo, tile + 1)
                    for k_ in range(KD):
                        end = T.transpose(bank[6][:, k_ * TT:(k_ + 1) * TT], hn2w[b][:, k_ * 128:(k_ + 1) * 128], ident[0:TT, 0:TT])
                    end.then_inc(hn2_turned, 1)
                elif what == "G":
                    pe.wait_ge(h2T_done, tile + 1)
                    pe.wait_ge(rest1, made7)
                    pe.wait_ge(h2_done, tile + 1)
                    for k_ in range(KD):
                        end = T.matmul(bank[7][0:TT, 0:E + 1], h2T[:, k_, :], wg_sb[:, k_, :], start=(k_ == 0), stop=(k_ == KD - 1))
                    end.then_inc(gated, 1)

            attention(pe, [(0, scores), (1, turn), (2, weigh), "rest"], qk=qk, post=post)

            pe.wait_ge(chosen, 1)
            rhs = both[:].rearrange("p e i -> p (e i)")
            T.matmul(bank[0][0:TT, 0:E * NT], up_bf[0:TT, 0:TT], rhs, start=True, stop=True)
            T.matmul(bank[1][0:TT, 0:E * NT], one_bf[0:TT, 0:TT], rhs, start=True, stop=True).then_inc(counted, 1)
            pe.wait_ge(slots_known, 1)

            pe.wait_ge(w_lo, NS)
            def shared_chunk(c):
                tok = bass.ds(c * SH, SH)
                for b in range(SB):
                    for half_, (s_, free) in enumerate(((sh_g, sh_silu), (sh_u, sh_h))):
                        pe.wait_ge(free, SB * c + max(b - 1, 0))
                        cols = [slice((b * KD + k) * 2 * HID + half_ * HID, (b * KD + k) * 2 * HID + (half_ + 1) * HID) for k in range(KD)]
                        product(bank[(2 * b + half_) % 4][:, 0:SH], [(wsh_h[:, cols[k]], wsh_l[:, cols[k]], hn2T_h[:, k, tok], hn2T_l[:, k, tok])
                                                                     for k in range(KD)]).then_inc(s_, 1)
                for tt in range(4):
                    t = 4 * c + tt
                    pe.wait_ge(sh_lo, SB * c + SB)
                    if tt >= 2:
                        pe.wait_ge(sh_acc, t - 1)
                    else:
                        pe.wait_ge(sh_acc, 4 * c)
                    product(bank[4 + tt % 2][0:TT, 0:D], [(hs_h[:, b, tt * TT:(tt + 1) * TT], hs_l[:, b, tt * TT:(tt + 1) * TT],
                                                           wsh_h[:, SGU + b * D:SGU + (b + 1) * D], wsh_l[:, SGU + b * D:SGU + (b + 1) * D])
                                                          for b in range(SB)]).then_inc(sh_y, 1)

            with pe.Fori(0, SH1) as c:
                shared_chunk(c)

            pe.wait_ge(w_lo, NS + NW)
            pe.wait_ge(eids_known, 3)
            pe.wait_ge(sh_acc, 4 * SH1)

            def block_turn(b, q):
                par = q % 2
                pe.wait_ge(bx_in[q], 4 * b + 16 - 4 * q)
                need(pe, b_lo, b - 1)
                for k in range(KD):
                    last = T.transpose(bank[par][:, k * BLK:(k + 1) * BLK], bx[q][:, k * 128:(k + 1) * 128], ident)
                last.then_inc(b_turned, 1)

            offsets = [T.alloc_register(f"offset{n}") for n in range(8)]
            at = [None] * 8

            def expert_weights(b):
                T.load(offsets, woff[:].rearrange("p a n -> p (a n)")[0:1, bass.ds(2 * b, 8)])
                for n in range(8):
                    low, high = (0, (E - 1) * KD * 2 * HID) if n < 4 else (0, EGU + (E - 1) * D)
                    at[n] = T.snap(offsets[n], min_val=low, max_val=high)

            def block_gu(b, q):
                par = q % 2
                e = at[q]
                pe.wait_ge(b_lo, b + 1)
                need(pe, b_h, b - 1)
                product(bank[2 + par][:, 0:2 * HID], [(bxT_h[par][:, k, :], bxT_l[par][:, k, :],
                                                       we_h[:, bass.ds(e + k * 2 * HID, 2 * HID)],
                                                       we_l[:, bass.ds(e + k * 2 * HID, 2 * HID)])
                                                      for k in range(KD)]).then_inc(b_gu, 1)

            def block_hturn(b, q):
                par = q % 2
                pe.wait_ge(b_h, b + 1)
                need(pe, b_hlo, b - 1)
                T.transpose(bank[4 + par][:, 0:BLK], bh[par][:], ident).then_inc(b_hturned, 1)

            def block_down(b, q):
                par = q % 2
                e = at[4 + (q + 2) % 4]
                pe.wait_ge(b_hlo, b + 1)
                need(pe, b_ykept, b - 1)
                product(bank[6 + par][:, 0:D], [(bhT_h[par][:], bhT_l[par][:], we_h[:, bass.ds(e, D)],
                                                 we_l[:, bass.ds(e, D)])]).then_inc(b_y, 1)

            blocks(pe, [(1, block_turn), (0, block_gu), (-1, block_hturn), (-2, block_down)], begin=expert_weights)
            pe.wait_ge(b_hlo, NBLK)
            with pe.Fori(SH1, NSH) as c:
                shared_chunk(c)


def kernel(**inputs):
    import numpy as np
    import concourse.bacc as bacc
    from concourse import mybir as mb
    from concourse.bass_utils import run_bass_kernel_spmd

    a = {k: np.asarray(v) for k, v in inputs.items()}
    P_, G_ = 16, 7
    x = a["x"].reshape(IMAGES, 3, G_, P_, G_, P_).transpose(1, 3, 5, 0, 2, 4).reshape(KP, 128, NT, TT)
    wq, wk, wv = (a["L0_attn_w_attn"][:, n * D:(n + 1) * D] for n in range(3))
    turned = [w.reshape(D, HP, 2, 2, 8).transpose(0, 2, 4, 1, 3).reshape(D, D) for w in (wq, wk)]
    wa = np.concatenate(turned + [wv], axis=1)
    gu = np.concatenate([a["L0_ffn_We_gate"], a["L0_ffn_We_up"]], axis=1)
    sgu = np.concatenate([a["L0_ffn_Ws_gate"].reshape(SB, HID, D), a["L0_ffn_Ws_up"].reshape(SB, HID, D)], axis=1)

    def gate_up(w):
        return w.reshape(w.shape[0], 2 * HID, KD, 128).transpose(3, 0, 2, 1).reshape(128, -1)

    arrays = {
        "xt": x.transpose(2, 1, 0, 3).reshape(NT * 128, KP * TT),
        "wt": a["L0_tok_W"].T.reshape(KP, 128, D).transpose(1, 0, 2).reshape(128, KP * D),
        "tb": a["L0_tok_b"].reshape(1, D),
        "wa": wa.reshape(KD, 128, 3 * D).transpose(1, 0, 2),
        "wp": a["L0_attn_w_proj"].reshape(HP, 2, 16, D).transpose(0, 2, 1, 3).reshape(128, 2, D),
        "gam": np.tile(a["L0_attn_gamma"], HP).reshape(128, 1),
        "lam": np.stack([a["L0_attn_lambda_" + n] for n in ("q1", "q2", "k1", "k2")]).reshape(1, 4, 8),
        "wg": np.concatenate([a["L0_ffn_Wg"], a["L0_ffn_Wsg"]]).T.reshape(KD, 128, E + 1).transpose(1, 0, 2),
        "we": np.concatenate([gate_up(gu), a["L0_ffn_We_down"].transpose(2, 0, 1).reshape(HID, -1)], axis=1),
        "wsh": np.concatenate([gate_up(sgu), a["L0_ffn_Ws_down"].reshape(D, SB, HID).transpose(2, 1, 0).reshape(HID, -1)], axis=1),
        "cst": constants(),
    }
    arrays = {k: np.ascontiguousarray(v) for k, v in arrays.items()}
    nc = bacc.Bacc("TRN2", target_bir_lowering=False, num_devices=1)
    aps = [nc.dram_tensor(k, v.shape, mb.dt.from_np(v.dtype), kind="ExternalInput").ap() for k, v in arrays.items()]
    aps.append(nc.dram_tensor("out", (TOK, D), F32, kind="ExternalOutput").ap())
    build(nc, *aps)
    r = run_bass_kernel_spmd(nc, [arrays], core_ids=[0])
    return np.asarray(r.results[0]["out"]).reshape(IMAGES, S, D)
```

```python
from contextlib import ExitStack

import concourse.bass as bass
from concourse import mybir

F32 = mybir.dt.float32
F32R = mybir.dt.float32r
BF16 = mybir.dt.bfloat16
I32 = mybir.dt.int32
U32 = mybir.dt.uint32
ALU = mybir.AluOpType
ACT = mybir.ActivationFunctionType
AX = mybir.AxisListType

IMAGES, S, D, PIX = 32, 49, 256, 768
TOK = IMAGES * S
TT = 2 * S
NT = TOK // TT
WTP = 3
KP = PIX // 128
KD = D // 128
HP = 8
VW = 34
SLOT = 64
PARTS = 6
QPART = (0, 0, 1, 1, 0, 2)
KPART = (0, 1, 0, 1, 2, 0)
CHUNK = 4 * S
NCHUNK = TOK // CHUNK
E, TOPK, HID, SH_HID = 16, 2, 128, 512
BLK = 128
NBLK = (TOK * TOPK + E * (BLK - 1)) // BLK
YR = 8
SH = 8 * S
NSH = TOK // SH
SH1 = 2
SB = SH_HID // 128
EGU = E * KD * 2 * HID
WE = EGU + E * D
SGU = SB * KD * 2 * HID
WSH = SGU + SB * D
STG = 1024
EPS = 1e-5
LAMBDA_INIT = 0.8 - 0.6
BIG = -1e30

C_ID = 0
C_UP = C_ID + 128
C_ONE = C_UP + 128
C_SEL = C_ONE + 128
C_MASK = C_SEL + 128
C_RESET = C_MASK + S
C_IOTA = C_RESET + E * NT
C_BLK = C_IOTA + E
C_END = C_BLK + NBLK


def constants():
    import numpy as np
    c = np.zeros((128, C_END), np.float32)
    p = np.arange(128)
    c[:, C_ID:C_ID + 128] = p[:, None] == p[None, :]
    c[:, C_UP:C_UP + 128] = p[:, None] < p[None, :]
    c[:, C_ONE:C_ONE + 128] = 1.0
    c[:S, C_SEL:C_SEL + 128] = p[:S, None] == (p[None, :] % SLOT)
    c[:S, C_MASK:C_MASK + S] = np.where(p[None, :S] > p[:S, None], BIG, 0.0)
    c[:, C_RESET:C_RESET + E * NT] = (np.arange(E * NT) % NT != 0)
    c[:, C_IOTA:C_IOTA + E] = np.arange(E)
    c[:, C_BLK:C_BLK + NBLK] = np.arange(NBLK)
    return c


def build(nc, xt, wt, tb, wa, wp, gam, lam, wg, we, wsh, cst, out):
    ctx = ExitStack()
    with ctx:
        V, A, T, G, SP = nc.vector, nc.scalar, nc.tensor, nc.gpsimd, nc.sync

        def sem(name):
            return ctx.enter_context(nc.semaphore(name))

        def bc(ap, shape):
            return ap.broadcast_to(shape)

        slots_x = nc.dram_tensor("slots_x", (NBLK * BLK, D), F32, kind="Internal").ap()
        slots_y = nc.dram_tensor("slots_y", (NBLK * BLK, D), F32, kind="Internal").ap()
        h2_dram = nc.dram_tensor("h2_dram", (TOK, D), F32, kind="Internal").ap()
        acc_dram = nc.dram_tensor("acc_dram", (TOK, D), F32, kind="Internal").ap()

        def keep(name, shape, dt=F32):
            return ctx.enter_context(nc.sbuf_tensor(name, shape, dt))

        cs = keep("cs", [128, C_END])
        ident = cs[:, C_ID:C_ID + 128]
        hn2 = keep("hn2", [TT, NT, D])
        hn2T_h = keep("hn2T_h", [128, KD, TOK], F32R)
        hn2T_l = keep("hn2T_l", [128, KD, TOK], F32R)
        logits = keep("logits", [TT, NT, E + 1])
        slot_u = keep("slot_u", [TT, TOPK, NT], U32)
        w1 = keep("w1", [TT, NT])
        w2 = keep("w2", [TT, NT])
        sig = keep("sig", [TT, NT])
        woff = keep("woff", [1, NBLK // 4 + 1, 8], I32)
        one_bf = keep("one_bf", [128, 128], BF16)
        up_bf = keep("up_bf", [128, 128], BF16)

        early = ExitStack()

        def ea(name, shape, dt=F32):
            return early.enter_context(nc.sbuf_tensor(name, shape, dt))

        wa_h = ea("wa_h", [128, KD, 3 * D], F32R)
        wa_l = ea("wa_l", [128, KD, 3 * D], F32R)
        wpr = ea("wpr", [128, 2, D])
        wpg = ea("wpg", [128, 2, D])
        wp_h = ea("wp_h", [128, 2, D], F32R)
        wp_l = ea("wp_l", [128, 2, D], F32R)
        wg_sb = ea("wg_sb", [128, KD, E + 1])
        gam_sb = ea("gam_sb", [128, 1])
        lam_sb = ea("lam_sb", [128, 4, 8])
        lamt = ea("lamt", [128, 2, 8])
        lam2 = ea("lam2", [128, 2])
        laml = ea("laml", [128, 2])
        lamd = ea("lamd", [128, 1])
        neglam = ea("neglam", [128, 1])
        bias = ea("bias", [TT, D])
        h = ea("h", [TT, NT, D])
        hT_h = ea("hT_h", [128, KD, TOK], F32R)
        hT_l = ea("hT_l", [128, KD, TOK], F32R)
        vst = ea("vst", [TT, NT, HP, VW])
        vx = [ea(f"vx{n}", [TT, 2, HP * VW]) for n in range(4)]
        sel_bf = ea("sel_bf", [S, 128], BF16)
        mask_bf = ea("mask_bf", [S, 8, S], BF16)
        zero = ea("zero", [128, 1280])
        three = ea("three", [128, 2 * HP])
        first = ExitStack()

        def fa(name, shape, dt=F32):
            return first.enter_context(nc.sbuf_tensor(name, shape, dt))

        wraw = fa("wraw", [128, KP * D])
        wt_h = fa("wt_h", [128, KP, D], F32R)
        wt_l = fa("wt_l", [128, KP, D], F32R)
        war = fa("war", [128, KD, 3 * D])
        xr = [fa(f"xr{n}", [128, KP, TT]) for n in range(2)]
        x_h = [fa(f"x_h{n}", [128, KP, TT], F32R) for n in range(2)]
        x_l = [fa(f"x_l{n}", [128, KP, TT], F32R) for n in range(2)]
        st1 = [fa(f"st1{n}", [TT, 6]) for n in range(2)]
        mv1 = [fa(f"mv1{n}", [TT, 2]) for n in range(2)]
        ve1 = [fa(f"ve1{n}", [TT, 1]) for n in range(2)]
        ln1 = [fa(f"ln1{n}", [TT, 1]) for n in range(2)]
        y1 = [fa(f"y1{n}", [TT, 1]) for n in range(2)]
        yx1 = [fa(f"yx1{n}", [TT, 1]) for n in range(2)]
        yn1 = [fa(f"yn1{n}", [TT, 1]) for n in range(2)]
        rs1 = [fa(f"rs1{n}", [TT, 1]) for n in range(2)]
        hn = [fa(f"hn{n}", [TT, D]) for n in range(2)]
        first.close()
        parts = ea("parts", [128, 4, 3, CHUNK], BF16)
        rest = [ea(f"rest{n}", [128, CHUNK]) for n in range(2)]
        Qs = [ea(f"Qs{n}", [112, 2 * HP, CHUNK], BF16) for n in range(2)]
        Ks = [ea(f"Ks{n}", [112, 2 * HP, CHUNK], BF16) for n in range(2)]
        smax = [ea(f"smax{n}", [128, 8]) for n in range(2)]
        Sm = [ea(f"Sm{n}", [128, 4, TT]) for n in range(2)]
        PT = [ea(f"PT{n}", [TT, 4, 128]) for n in range(2)]
        rz = ea("rz", [128, 8])
        on = ea("on", [128, 8, 16])
        att = [ea(f"att{n}", [128, 2, HP, 16]) for n in range(2)]
        sq = ea("sq", [128, 2 * HP, 16])
        ms = ea("ms", [128, 2 * HP])
        ms2 = ea("ms2", [128, 2 * HP])
        lnr = ea("lnr", [128, 2 * HP])
        r0 = ea("r0", [128, 2 * HP])
        nt1 = ea("nt1", [128, 2 * HP])
        nt2 = ea("nt2", [128, 2 * HP])
        nt3 = ea("nt3", [128, 2 * HP])
        rr = ea("rr", [128, 2 * HP])
        ao = ea("ao", [128, 2, HP, 16])
        aT_h = ea("aT_h", [128, 2, 2, S], F32R)
        aT_l = ea("aT_l", [128, 2, 2, S], F32R)
        h2 = [ea(f"h2{n}", [TT, D]) for n in range(2)]
        hn2w = [ea(f"hn2w{n}", [TT, D]) for n in range(2)]
        st2 = ea("st2", [TT, 6])
        mv2 = ea("mv2", [TT, 2])
        ve2 = ea("ve2", [TT, 1])
        ln2 = ea("ln2", [TT, 1])
        q0 = ea("q0", [TT, 1])
        q1 = ea("q1", [TT, 1])
        q2 = ea("q2", [TT, 1])
        rs2 = ea("rs2", [TT, 1])
        h2T = ea("h2T", [128, KD, TT])
        early.close()

        def la(name, shape, dt=F32):
            return ctx.enter_context(nc.sbuf_tensor(name, shape, dt))

        we_h = la("we_h", [128, WE], F32R)
        we_l = la("we_l", [128, WE], F32R)
        wsh_h = la("wsh_h", [128, WSH], F32R)
        wsh_l = la("wsh_l", [128, WSH], F32R)
        sgl = la("sgl", [128, SH])
        hs = la("hs", [128, SH])
        hs_h = la("hs_h", [128, SB, SH], F32R)
        hs_l = la("hs_l", [128, SB, SH], F32R)
        h2r = [la(f"h2r{n}", [TT, D]) for n in range(2)]
        acc = [la(f"acc{n}", [TT, D]) for n in range(2)]

        middle = ExitStack()

        def ma(name, shape, dt=F32):
            return middle.enter_context(nc.sbuf_tensor(name, shape, dt))

        stg = [ma(f"stg{n}", [128, STG]) for n in range(3)]
        mx8 = ma("mx8", [TT, NT, 8])
        ix8 = ma("ix8", [TT, NT, 8], U32)
        ixf = ma("ixf", [TT, TOPK, NT])
        oh = ma("oh", [TT, TOPK, E, NT])
        both = ma("both", [TT, E, NT], BF16)
        cuminc = ma("cuminc", [TT, E, NT])
        excl = ma("excl", [TT, E, NT])
        cnt = ma("cnt", [TT, E], I32)
        cnts = ma("cnts", [TT, E], I32)
        nblk = ma("nblk", [TT, E])
        cumb = ma("cumb", [TT, E])
        base = ma("base", [TT, E])
        slotf = ma("slotf", [TT, E, NT])
        slot2 = ma("slot2", [TT, E, NT])
        ecmp = ma("ecmp", [1, NBLK, E], BF16)
        slotr = ma("slotr", [TT, TOPK, NT])
        esum = ma("esum", [1, NBLK])
        eid = ma("eid", [1, NBLK // 4, 4])
        dl = ma("dl", [TT, NT])
        ed = ma("ed", [TT, NT])
        ed1 = ma("ed1", [TT, NT])
        ez = ma("ez", [TT, NT])
        ez1 = ma("ez1", [TT, NT])
        middle.close()
        bx = [la(f"bx{n}", [BLK, D]) for n in range(4)]
        bxT_h = [la(f"bxT_h{n}", [128, KD, BLK], F32R) for n in range(2)]
        bxT_l = [la(f"bxT_l{n}", [128, KD, BLK], F32R) for n in range(2)]
        bsg = [la(f"bsg{n}", [BLK, HID]) for n in range(2)]
        bh = [la(f"bh{n}", [BLK, HID]) for n in range(2)]
        bhT_h = [la(f"bhT_h{n}", [HID, BLK], F32R) for n in range(2)]
        bhT_l = [la(f"bhT_l{n}", [HID, BLK], F32R) for n in range(2)]
        by = [la(f"by{n}", [BLK, D]) for n in range(4)]
        psum1 = [la(f"psum1{n}", [TT, D]) for n in range(2)]
        fin = [la(f"fin{n}", [TT, D]) for n in range(2)]

        bank = [ctx.enter_context(nc.psum_tensor(f"bank{n}", [128, 512], F32)) for n in range(8)]

        cst_in = sem("cst_in")
        wt_in = [sem(f"wt_in{n}") for n in range(WTP)]
        wa_in = sem("wa_in")
        wp_in = sem("wp_in")
        small_in = sem("small_in")
        x_in = [sem(f"x_in{n}") for n in range(2)]
        init_done = sem("init_done")
        pool_init = sem("pool_init")
        zeroed = sem("zeroed")
        wt_hi, wt_lo = sem("wt_hi"), sem("wt_lo")
        x_hi, x_lo = sem("x_hi"), sem("x_lo")
        embedded = sem("embedded")
        h_done, h_stats, h_aggr, h_var = (sem(n) for n in ("h_done", "h_stats", "h_aggr", "h_var"))
        h_ln, h_guess, h_newton = (sem(n) for n in ("h_ln", "h_guess", "h_newton"))
        hn_done, hn_turned, hT_hi, hT_lo = sem("hn_done"), sem("hn_turned"), sem("hT_hi"), sem("hT_lo")
        wa_hi, wa_lo, wp_g, wp_hi, wp_lo = sem("wa_hi"), sem("wa_lo"), sem("wp_g"), sem("wp_hi"), sem("wp_lo")
        lam_a, lam_b, lam_c, lam_d, lam_e = (sem(f"lam_{n}") for n in "abcde")
        v_made, v_kept = sem("v_made"), sem("v_kept")
        qk_made, part0, rest1, part1, part2 = (sem(n) for n in ("qk_made", "part0", "rest1", "part1", "part2"))
        stacked = [sem(f"stacked{n}") for n in range(2)]
        vx_in = [sem(f"vx_in{n}") for n in range(4)]
        scored, maxed, centred, turned, exped, weighed = (
            sem(n) for n in ("scored", "maxed", "centred", "turned", "exped", "weighed"))
        rz_done, on_done, att_done = sem("rz_done"), sem("on_done"), sem("att_done")
        sq_done, ms_done, ms2_done, ln_done, r0_done = (
            sem(n) for n in ("sq_done", "ms_done", "ms2_done", "ln_done", "r0_done"))
        newton = sem("newton")
        ao_done, ao_turned, aT_hi, aT_lo, projected = (
            sem(n) for n in ("ao_done", "ao_turned", "aT_hi", "aT_lo", "projected"))
        h2_done, st2_done, mv2_done, ve2_done, ln2_done, q0_done = (
            sem(n) for n in ("h2_done", "st2_done", "mv2_done", "ve2_done", "ln2_done", "q0_done"))
        hn2_kept = sem("hn2_kept")
        newton2, hn2_done, hn2_turned, h2T_done, h2T_hi, h2T_lo = (
            sem(n) for n in ("newton2", "hn2_done", "hn2_turned", "h2T_done", "h2T_hi", "h2T_lo"))
        gated, logit_done = sem("gated"), sem("logit_done")
        h2_out = [sem(f"h2_out{n}") for n in range(2)]
        gate_diff, slots_known, eids_known, weights_known, routing = (
            sem(n) for n in ("gate_diff", "slots_known", "eids_known", "weights_known", "routing"))
        chosen = sem("chosen")
        counted, e_exp = sem("counted"), sem("e_exp")
        scattered = sem("scattered")
        stg_in = [sem(f"stg_in{n}") for n in range(3)]
        wsh_hi, wsh_lo, w_hi, w_lo = (sem(n) for n in ("wsh_hi", "wsh_lo", "w_hi", "w_lo"))
        sh_g, sh_u, sh_silu, sh_h, sh_hi, sh_lo, sh_y, sh_acc = (
            sem(n) for n in ("sh_g", "sh_u", "sh_silu", "sh_h", "sh_hi", "sh_lo", "sh_y", "sh_acc"))
        h2_in = [sem(f"h2_in{n}") for n in range(2)]
        acc_out = [sem(f"acc_out{n}") for n in range(2)]
        bx_in = [sem(f"bx_in{n}") for n in range(4)]
        b_turned, b_hi, b_lo, b_gu, b_silu, b_h, b_hturned, b_hhi, b_hlo, b_y, b_ykept = (
            sem("b_" + n) for n in ("turned", "hi", "lo", "gu", "silu", "h", "hturned", "hhi", "hlo", "y", "ykept"))
        by_out = [sem(f"by_out{n}") for n in range(4)]
        acc_in = [sem(f"acc_in{n}") for n in range(4)]
        y_in = [sem(f"y_in{n}") for n in range(YR)]
        part_sum, fin_done = sem("part_sum"), sem("fin_done")
        fin_out = [sem(f"fin_out{n}") for n in range(2)]

        def need(eng, s, value):
            if isinstance(value, int) and value <= 0:
                return
            eng.wait_ge(s, value)

        NZ = NBLK * BLK // (128 * 5)
        assert NZ == NT // 2
        NW, NS = WE // STG, WSH // STG
        SPLITS, TILE_SPLITS = ((0,), (1,), (2,), (3,)), ((4,), (5,), (), ())
        assert NW == SH1 * 6
        COMBINE = {2: ((), (), (0,), (1,), (2,), (3,), (4,), (5,)), 3: ((), (6,), (7,), (8,), (9,), (10,), (11,), ())}
        assert SH1 == 2 and NSH == 4

        def pipeline(eng, steps, count, mod, lead, lag, peel, begin=None):
            def turn(b, q):
                if begin and q == 0:
                    begin(b)
                for ahead, step in steps:
                    if isinstance(b, int) and not 0 <= b + ahead < count:
                        continue
                    step(b + ahead, (q + ahead) % mod)
            for b in range(-lead, peel):
                turn(b, b % mod)
            with eng.Fori(peel // mod, count // mod - 1) as t:
                for q in range(mod):
                    turn(mod * t + q, q)
            for b in range(count - mod, count + lag):
                turn(b, b % mod)

        def embedding(eng, steps):
            pipeline(eng, steps, NT, 2, 1, 3, 4)

        def blocks(eng, steps, begin=None):
            pipeline(eng, steps, NBLK, 4, 1, 2, 8, begin)

        POSTS = (("N", -3),), (("A", -2),), (("P", -2),), (("n", -2), ("G", -3), ("R", -1)), \
            (("N", -2),), (("A", -1),), (("P", -1),), (("n", -1), ("G", -2), ("R", 0))

        LAST_POSTS = (("N", -3),), (("A", -2),), (("P", -2),), (("R", -1), ("n", -2), ("G", -3)), \
            (("N", -2), ("A", -1)), (("P", -1),), (("n", -1), ("G", -2)), (("N", -1), ("G", -1))

        def attention(eng, *steps):
            def half(c, k, cc, last):
                for kind, *lag, step in steps:
                    if kind == "half":
                        back = k < lag[0]
                        c_, k_, cc_ = (c - 1, k - lag[0] + 8, 1 - cc) if back else (c, k - lag[0], cc)
                        if not isinstance(c_, int) or 0 <= c_ < NCHUNK:
                            step(c_, k_, cc_)
                    elif kind == "qk":
                        m = k - lag[0]
                        if 0 <= m < 4 and not last:
                            step(c + 1, m, 1 - cc)
                    else:
                        for what, ahead in (LAST_POSTS if isinstance(c, int) and c == NCHUNK else POSTS)[k]:
                            tile = 2 * c + ahead
                            if not isinstance(tile, int) or 0 <= tile < NT:
                                step(what, tile, ahead % 2, c, k)

            def chunk(c, cc):
                for k in range(8):
                    half(c, k, cc, isinstance(c, int) and c >= NCHUNK - 1)

            chunk(0, 0)
            chunk(1, 1)
            with eng.Fori(1, NCHUNK // 2 - 1) as s:
                chunk(2 * s, 0)
                chunk(2 * s + 1, 1)
            for c in range(NCHUNK - 2, NCHUNK + 1):
                chunk(c, c % 2)

        block = ctx.enter_context(nc.Block())

        @block.sync
        def _(sp):
            def row(value):
                return value if isinstance(value, int) else sp.snap(value)

            def load_x(i, b):
                r = row(i * 128)
                need(sp, x_lo, i - 1)
                need(sp, x_hi, i - 1)
                sp.dma_start(xr[b][:].rearrange("p k t -> p (k t)"), xt[bass.ds(r, 128), :]).then_inc(x_in[b], 16)

            load_x(0, 0)
            for n in range(WTP):
                cols = slice(n * KP * D // WTP, (n + 1) * KP * D // WTP)
                sp.dma_start(wraw[:, cols], wt[:, cols]).then_inc(wt_in[n], 16)
            load_x(1, 1)
            sp.dma_start(war[:], wa).then_inc(wa_in, 16)
            sp.dma_start(cs[:], cst).then_inc(cst_in, 16)
            sp.dma_start(bias[:], tb.broadcast_to([TT, D])).then_inc(small_in, 16)
            sp.dma_start(gam_sb[:], gam).then_inc(small_in, 16)
            sp.dma_start(lam_sb[:], lam.broadcast_to([128, 4, 8])).then_inc(small_in, 16)
            sp.dma_start(wg_sb[:], wg).then_inc(small_in, 16)
            with sp.Fori(1, NT // 2) as t:
                load_x(2 * t, 0)
                load_x(2 * t + 1, 1)
            sp.dma_start(wpr[:], wp).then_inc(wp_in, 16)

            def load_vx(n, c):
                tile = row(2 * c + n // 2)
                free = row(8 * c - 6 + 2 * n)
                sp.wait_ge(v_kept, NT)
                need(sp, weighed, free)
                r = 49 * (n % 2)
                for j in range(2):
                    sp.dma_start(vx[n][49 * j:49 * j + 49, j, :],
                                 vst[r:r + 49, bass.ds(tile, 1), :, :].rearrange("p a b c -> p (a b c)")).then_inc(vx_in[n], 16)

            def stack(c, cc):
                free = row(8 * (c - 1))
                for m in range(4):
                    dst = (Qs, Ks)[m // 2][cc]
                    jj = m % 2
                    made = row(4 * c + m + 1)
                    if m == 0:
                        need(sp, scored, free)
                    sp.wait_ge(part2, made)
                    sp.wait_ge(part1, made)
                    for r, part in enumerate((QPART, KPART)[m // 2]):
                        at_row = SLOT * jj + 8 * r
                        sp.dma_start(dst[at_row:at_row + 8, :, :], parts[:, m, part, :]).then_inc(stacked[cc], 16)

            stack(0, 0)
            for n in range(4):
                load_vx(n, 0)

            def chunk(c, cc, last=False):
                if not last:
                    stack(c + 1, 1 - cc)
                for p in range(2):
                    if not (isinstance(c, int) and c == 0):
                        store_h2(2 * c - 2 + p, p)
                    if not last:
                        load_vx(2 * p, c + 1)
                        load_vx(2 * p + 1, c + 1)

            def store_h2(pair, b):
                r = row(pair * TT)
                sp.wait_ge(h2_done, pair + 1)
                sp.dma_start(h2_dram[bass.ds(r, TT), :], h2[b][:]).then_inc(h2_out[b], 16)

            chunk(0, 0)
            chunk(1, 1)
            with sp.Fori(1, NCHUNK // 2 - 1) as s:
                chunk(2 * s, 0)
                chunk(2 * s + 1, 1)
            chunk(NCHUNK - 2, 0)
            chunk(NCHUNK - 1, 1, last=True)
            store_h2(NT - 2, 0)
            store_h2(NT - 1, 1)

            sp.wait_ge(logit_done, NT)
            sp.wait_ge(h2T_lo, NT)
            for b in range(2):
                sp.wait_ge(h2_out[b], 16 * NT // 2)

            def stage(n, b, weights):
                sp.dma_start(stg[b][:], weights[:, n * STG:(n + 1) * STG]).then_inc(stg_in[b], 16)

            def stage_expert(n):
                if n < 3:
                    sp.wait_ge(wsh_lo, n + 1)
                else:
                    sp.wait_ge(w_lo, n - 2)
                stage(n, n % 3, we)

            def load_h2r(t, b):
                r = row(t * TT)
                need(sp, sh_acc, t - 1)
                sp.dma_start(h2r[b][:], h2_dram[bass.ds(r, TT), :]).then_inc(h2_in[b], 16)

            def store_acc(t, b):
                r = row(t * TT)
                sp.wait_ge(sh_acc, t + 1)
                sp.dma_start(acc_dram[bass.ds(r, TT), :], acc[b][:]).then_inc(acc_out[b], 16)

            for n in range(NS):
                stage(n, n, wsh)
            load_h2r(0, 0)
            load_h2r(1, 1)
            for n in range(3):
                stage_expert(n)
            for c in range(SH1):
                for n in range(NW // SH1 * c + 3, min(NW // SH1 * (c + 1) + 1, NW)):
                    stage_expert(n)
                for tt in range(4):
                    load_h2r(4 * c + tt + 2, tt % 2)
                    if tt < 2 and NW // SH1 * (c + 1) + 1 + tt < NW:
                        stage_expert(NW // SH1 * (c + 1) + 1 + tt)
                    store_acc(4 * c + tt, tt % 2)

            def load_block(b, q):
                r = row(b * BLK)
                need(sp, b_turned, b - 3)
                sp.dma_start(bx[q][:], slots_x[bass.ds(r, BLK), :]).then_inc(bx_in[q], 16)

            def store_block(b, q):
                r = row(b * BLK)
                sp.wait_ge(b_ykept, b + 1)
                sp.dma_start(slots_y[bass.ds(r, BLK), :], by[q][:]).then_inc(by_out[q], 16)

            sp.wait_ge(w_lo, NW)
            sp.wait_ge(scattered, 16 * TOPK * NT)
            for b in range(7):
                load_block(b, b % 4)
            store_block(0, 0)
            with sp.Fori(0, (NBLK - 8) // 8) as t:
                for q in range(8):
                    load_block(8 * t + 7 + q, (7 + q) % 4)
                    store_block(8 * t + 1 + q, (1 + q) % 4)
            load_block(NBLK - 1, (NBLK - 1) % 4)
            for b in range(NBLK - 7, NBLK):
                store_block(b, b % 4)

            def load_acc(t):
                sp.wait_ge(acc_out[t % 2], 16 * (t // 2 + 1))
                need(sp, part_sum, t - 3)
                sp.dma_start(bx[t % 4][0:TT, :], acc_dram[t * TT:(t + 1) * TT, :]).then_inc(acc_in[t % 4], 16)

            def store_out(t, par):
                sp.wait_ge(fin_done, t + 1)
                sp.dma_start(out[t * TT:(t + 1) * TT, :], fin[par][:]).then_inc(fin_out[par], 16)

            def combined(tiles):
                for t in tiles:
                    store_out(t, t % 2)
                    if t + 4 < 4 * (NSH - 1):
                        load_acc(t + 4)

            for t in range(4):
                load_acc(t)
            for c in range(SH1, NSH):
                last = c == NSH - 1
                for b in range(SB):
                    combined(COMBINE[c][b])
                for tt in range(4):
                    t = 4 * c + tt
                    store_acc(t, tt % 2)
                    if t + 2 < NT:
                        load_h2r(t + 2, tt % 2)
                    combined(COMBINE[c][SB + tt])
                    if last and tt > 0:
                        load_acc(t - 1)
            load_acc(NT - 1)
            for t in range(4 * (NSH - 1), NT):
                store_out(t, t % 2)
            sp.wait_ge(fin_out[0], 16 * NT // 2)
            sp.wait_ge(fin_out[1], 16 * NT // 2)

        @block.gpsimd
        def _(pool):
            def split_lo(i, b):
                pool.wait_ge(x_hi, i + 1)
                need(pool, embedded, i - 1)
                G.tensor_tensor(x_l[b][:], xr[b][:], x_h[b][:].bitcast(F32), ALU.subtract).then_inc(x_lo, 1)

            split_lo(0, 0)
            split_lo(1, 1)
            with pool.Fori(1, NT // 2) as t:
                split_lo(2 * t, 0)
                split_lo(2 * t + 1, 1)
            G.memset(zero[:], 0.0).then_inc(pool_init, 1)
            G.memset(three[:], 3.0).then_inc(pool_init, 1)
            G.memset(woff[:], 0).then_inc(pool_init, 1)
            G.memset(vst[:, :, :, 32:VW], 1.0).then_inc(pool_init, 1)
            for n in range(4):
                G.memset(vx[n][:], 0.0).then_inc(pool_init, 1)

            zx = slots_x.rearrange("(n p r) d -> n p (r d)", p=128, r=5)

            def norm_tile(tile, b):
                pool.wait_ge(att_done, 4 * tile + 4)
                need(pool, ms_done, tile)
                a = att[b][:].rearrange("p i h d -> p (i h) d")
                G.tensor_tensor(sq[:], a, a, ALU.mult).then_inc(sq_done, 1)
                pool.wait_ge(r0_done, tile + 1)
                G.tensor_tensor(nt1[:], r0[:], r0[:], ALU.mult).then_inc(newton, 1)
                pool.wait_ge(newton, 4 * tile + 1)
                G.tensor_tensor(nt2[:], nt1[:], ms2[:], ALU.mult).then_inc(newton, 1)
                pool.wait_ge(newton, 4 * tile + 2)
                G.tensor_tensor(nt3[:], three[:], nt2[:], ALU.subtract).then_inc(newton, 1)
                pool.wait_ge(newton, 4 * tile + 3)
                G.tensor_tensor(rr[:], r0[:], nt3[:], ALU.mult).then_inc(newton, 1)
                pool.wait_ge(newton, 4 * tile + 4)
                need(pool, ao_turned, tile)
                G.tensor_tensor(ao[:].rearrange("p i h d -> p (i h) d"), a,
                                bc(rr[:].unsqueeze(2), [128, 2 * HP, 16]), ALU.mult).then_inc(ao_done, 1)

            pool.wait_ge(pool_init, 8)

            def norm_pair(t):
                G.dma_start(zx[bass.ds(t, 1)].rearrange("a p n -> (a p) n"), zero[:]).then_inc(zeroed, 16)
                norm_tile(2 * t, 0)
                norm_tile(2 * t + 1, 1)

            norm_pair(0)
            with pool.Fori(1, NZ) as t:
                norm_pair(t)
            for n in range(NS):
                pool.wait_ge(wsh_hi, n + 1)
                G.tensor_tensor(wsh_l[:, n * STG:(n + 1) * STG], stg[n][:], wsh_h[:, n * STG:(n + 1) * STG].bitcast(F32),
                                ALU.subtract).then_inc(wsh_lo, 1)
            pool.wait_ge(slots_known, 1)
            pool.wait_ge(zeroed, 16 * NZ)
            for k in range(TOPK):
                for i in range(NT):
                    G.indirect_dma_start(out=slots_x, out_offset=bass.IndirectOffsetOnAxis(ap=slot_u[:, k, i:i + 1], axis=0),
                                         in_=hn2[:, i, :], in_offset=None).then_inc(scattered, 16)
            for q in range(4):
                pool.wait_ge(by_out[q], 16 * NBLK // 4)
            for i in range(NT):
                if i >= YR:
                    pool.wait_ge(fin_done, i - YR + 1)
                for k in range(TOPK):
                    G.indirect_dma_start(out=hn2[:, TOPK * (i % YR) + k, :], out_offset=None, in_=slots_y,
                                         in_offset=bass.IndirectOffsetOnAxis(ap=slot_u[:, k, i:i + 1], axis=0)).then_inc(y_in[i % YR], 16)

        @block.scalar
        def _(act):
            A.preload_act_table_set("natural_log_exp_and_others")
            for n in range(WTP):
                k = slice(n * KP // WTP, (n + 1) * KP // WTP)
                if n == 0:
                    act.wait_ge(x_in[0], 16)
                    A.activation(x_h[0][:], xr[0][:], ACT.Copy).then_inc(x_hi, 1)
                act.wait_ge(wt_in[n], 16)
                A.activation(wt_h[:, k], wraw[:].rearrange("p (k n) -> p k n", k=KP)[:, k], ACT.Copy).then_inc(wt_hi, 1)

            def split_x(i, b):
                if isinstance(i, int) and i == 0:
                    return
                act.wait_ge(x_in[b], 8 * i + 16 - 8 * b)
                need(act, embedded, i - 1)
                A.activation(x_h[b][:], xr[b][:], ACT.Copy).then_inc(x_hi, 1)

            def split_wa(i, b):
                if isinstance(i, int) and i == 2:
                    act.wait_ge(wa_in, 16)
                    A.activation(wa_h[:], war[:], ACT.Copy).then_inc(wa_hi, 1)

            def guess(i, b):
                act.wait_ge(h_var, i + 1)
                A.activation(ln1[b][:], ve1[b][:], ACT.Ln).then_inc(h_ln, 1)
                act.wait_ge(h_ln, i + 1)
                need(act, h_newton, 3 * i - 3)
                A.activation(y1[b][:], ln1[b][:], ACT.Exp, scale=-0.5).then_inc(h_guess, 1)

            def keep_hT(i, b):
                act.wait_ge(hn_turned, i + 1)
                A.activation(hT_h[:, :, bass.ds(i * TT, TT)],
                             bank[4 + b][:, 0:KD * TT].rearrange("p (k t) -> p k t", k=KD), ACT.Copy).then_inc(hT_hi, 1)

            def part_0(c, m, cc):
                act.wait_ge(qk_made, 4 * c + m + 1)
                need(act, stacked[1 - cc], 192 * (c + cc))
                A.activation(parts[:, m, 0, :], bank[6 + m % 2][:, 0:CHUNK], ACT.Copy,
                             scale=0.125 if m < 2 else 1.0).then_inc(part0, 1)

            def part_1(c, m, cc):
                act.wait_ge(rest1, 4 * c + m + 1)
                A.activation(parts[:, m, 1, :], rest[m % 2][:], ACT.Copy).then_inc(part1, 1)

            def first_qk(m):
                def step(i, b):
                    if isinstance(i, int) and i == NT - 1:
                        for n in (m, m + 1):
                            part_0(0, n, 0)
                            part_1(0, n, 0)
                return step

            embedding(act, [(1, split_x), (-1, guess), (-3, keep_hT), (0, split_wa), (-1, first_qk(0)), (-2, first_qk(2))])
            act.wait_ge(lam_b, 1)
            A.activation(laml[:], lam2[:], ACT.Exp).then_inc(lam_c, 1)
            act.wait_ge(wp_g, 1)
            A.activation(wp_h[:], wpg[:], ACT.Copy).then_inc(wp_hi, 1)

            act.wait_ge(pool_init, 8)
            for i in range(NT):
                act.wait_ge(v_made, i + 1)
                A.activation(vst[:, i, :, 0:32], bank[4 + i % 2][0:TT, 0:D].rearrange("p (h n) -> p h n", h=HP),
                             ACT.Copy).then_inc(v_kept, 1)

            def exp_half(c, k, cc):
                u, b = 8 * c + k, k % 2
                act.wait_ge(turned, u + 1)
                need(act, weighed, u - 1)
                A.activation(PT[b][:].rearrange("p a t -> p (a t)"), bank[2 + b][0:TT, :], ACT.Exp).then_inc(exped, 1)

            def post(what, tile, b, c, k):
                if what == "R":
                    act.wait_ge(ms2_done, tile + 1)
                    A.activation(lnr[:], ms2[:], ACT.Ln).then_inc(ln_done, 1)
                    act.wait_ge(ln_done, tile + 1)
                    need(act, newton, 4 * tile)
                    A.activation(r0[:], lnr[:], ACT.Exp, scale=-0.5).then_inc(r0_done, 1)
                elif what == "A":
                    act.wait_ge(ao_turned, tile + 1)
                    need(act, projected, tile)
                    A.activation(aT_h[:], bank[6 + b][:, 0:256].rearrange("p (i j t) -> p j i t", i=2, j=2)[:, :, :, 0:S],
                                 ACT.Copy).then_inc(aT_hi, 1)
                elif what == "P":
                    act.wait_ge(ve2_done, tile + 1)
                    A.activation(ln2[:], ve2[:], ACT.Ln).then_inc(ln2_done, 1)
                    act.wait_ge(ln2_done, tile + 1)
                    need(act, newton2, 3 * tile)
                    A.activation(q0[:], ln2[:], ACT.Exp, scale=-0.5).then_inc(q0_done, 1)
                elif what == "N":
                    act.wait_ge(hn2_turned, tile + 1)
                    need(act, h2T_lo, tile)
                    need(act, gated, tile)
                    A.activation(h2T[:].rearrange("p k t -> p (k t)"), bank[6 + b][:, 0:KD * TT], ACT.Copy).then_inc(h2T_done, 1)
                    A.activation(hn2[:, bass.ds(tile, 1), :].rearrange("p a n -> p (a n)"), hn2w[b][:], ACT.Copy).then_inc(hn2_kept, 1)
                    act.wait_ge(h2T_done, tile + 1)
                    A.activation(hn2T_h[:, :, bass.ds(tile * TT, TT)], h2T[:], ACT.Copy).then_inc(h2T_hi, 1)
                elif what == "G":
                    act.wait_ge(gated, tile + 1)
                    A.activation(logits[:, bass.ds(tile, 1), :].rearrange("p a n -> p (a n)"),
                                 bank[7 - b][0:TT, 0:E + 1], ACT.Copy).then_inc(logit_done, 1)

            attention(act, ("qk", 0, part_0), ("half", 1, exp_half), ("qk", 0, part_1), ("post", post))

            for n in range(NS):
                act.wait_ge(stg_in[n], 16)
                A.activation(wsh_h[:, n * STG:(n + 1) * STG], stg[n][:], ACT.Copy).then_inc(wsh_hi, 1)
            act.wait_ge(gate_diff, 1)
            A.activation(ed[:], dl[:], ACT.Exp).then_inc(e_exp, 1)
            A.activation(ez[:], logits[:, :, E], ACT.Exp, scale=-1.0).then_inc(e_exp, 1)

            def split_expert(n):
                act.wait_ge(stg_in[n % 3], 32 + 16 * (n // 3))
                A.activation(we_h[:, n * STG:(n + 1) * STG], stg[n % 3][:], ACT.Copy).then_inc(w_hi, 1)

            def shared_chunk(c, split):
                for b in range(SB):
                    u = SB * c + b
                    act.wait_ge(sh_g, u + 1)
                    need(act, sh_h, u)
                    A.activation(sgl[:], bank[(2 * b) % 4][:, 0:SH], ACT.Silu).then_inc(sh_silu, 1)
                    for j in (SPLITS[b] if split else ()):
                        split_expert(NW // SH1 * c + j)
                    act.wait_ge(sh_h, u + 1)
                    need(act, sh_y, 4 * c)
                    A.activation(hs_h[:, b, :], hs[:], ACT.Copy).then_inc(sh_hi, 1)
                for tt in range(4):
                    for j in (TILE_SPLITS[tt] if split else ()):
                        split_expert(NW // SH1 * c + j)

            for c in range(SH1):
                shared_chunk(c, True)

            def block_hi(b, q):
                par = q % 2
                act.wait_ge(b_turned, b + 1)
                need(act, b_gu, b - 1)
                A.activation(bxT_h[par][:].rearrange("p k t -> p (k t)"), bank[par][:, 0:D], ACT.Copy).then_inc(b_hi, 1)

            def block_silu(b, q):
                par = q % 2
                act.wait_ge(b_gu, b + 1)
                need(act, b_h, b - 1)
                A.activation(bsg[par][:], bank[2 + par][:, 0:HID], ACT.Silu).then_inc(b_silu, 1)

            def block_hhi(b, q):
                par = q % 2
                act.wait_ge(b_hturned, b + 1)
                need(act, b_y, b - 1)
                A.activation(bhT_h[par][:], bank[4 + par][:, 0:BLK], ACT.Copy).then_inc(b_hhi, 1)

            def block_keep(b, q):
                act.wait_ge(b_y, b + 1)
                need(act, by_out[q], 4 * b - 4 * q)
                A.activation(by[q][:], bank[6 + q % 2][:, 0:D], ACT.Copy).then_inc(b_ykept, 1)

            blocks(act, [(1, block_hi), (0, block_silu), (-1, block_hhi), (-2, block_keep)])
            for c in range(SH1, NSH):
                shared_chunk(c, False)

        @block.vector
        def _(dve):
            for n in range(WTP):
                k = slice(n * KP // WTP, (n + 1) * KP // WTP)
                dve.wait_ge(wt_hi, n + 1)
                V.tensor_tensor(wt_l[:, k], wraw[:].rearrange("p (k n) -> p k n", k=KP)[:, k],
                                wt_h[:, k].bitcast(F32), ALU.subtract).then_inc(wt_lo, 1)
            dve.wait_ge(small_in, 64)

            def h_of(i):
                return h[:, bass.ds(i, 1), :].rearrange("p a n -> p (a n)")

            def embed_out(i, b):
                dve.wait_ge(embedded, i + 1)
                V.tensor_tensor(h_of(i), bank[6 + b][0:TT, 0:D], bias[:], ALU.add).then_inc(h_done, 1)

            def stats(i, b):
                dve.wait_ge(small_in, 64)
                dve.wait_ge(h_done, i + 1)
                V.bn_stats(st1[b][:], h_of(i)).then_inc(h_stats, 1)

            def aggregate(i, b):
                dve.wait_ge(small_in, 64)
                dve.wait_ge(h_stats, i + 1)
                V.bn_aggr(mv1[b][:], st1[b][:]).then_inc(h_aggr, 1)

            def variance(i, b):
                dve.wait_ge(h_aggr, i + 1)
                V.tensor_scalar(ve1[b][:], mv1[b][:, 1:2], EPS, None, ALU.add).then_inc(h_var, 1)

            def newton_a(i, b):
                dve.wait_ge(h_guess, i + 1)
                V.scalar_tensor_tensor(yx1[b][:], y1[b][:], ve1[b][:], y1[b][:], ALU.mult, ALU.mult).then_inc(h_newton, 1)

            def newton_b(i, b):
                dve.wait_ge(h_newton, 3 * i + 1)
                V.tensor_scalar(yn1[b][:], yx1[b][:], -0.5, 1.5, ALU.mult, ALU.add).then_inc(h_newton, 1)

            def newton_c(i, b):
                dve.wait_ge(h_newton, 3 * i + 2)
                V.tensor_tensor(rs1[b][:], y1[b][:], yn1[b][:], ALU.mult).then_inc(h_newton, 1)

            def norm(i, b):
                dve.wait_ge(h_newton, 3 * i + 3)
                need(dve, hn_turned, i - 1)
                V.tensor_scalar(hn[b][:], h_of(i), mv1[b][:, 0:1], rs1[b][:], ALU.subtract, ALU.mult).then_inc(hn_done, 1)

            def keep_lo(i, b):
                dve.wait_ge(hT_hi, i + 1)
                V.tensor_tensor(hT_l[:, :, bass.ds(i * TT, TT)],
                                bank[4 + b][:, 0:KD * TT].rearrange("p (k t) -> p k t", k=KD),
                                hT_h[:, :, bass.ds(i * TT, TT)].bitcast(F32), ALU.subtract).then_inc(hT_lo, 1)

            def split_wa(i, b):
                if isinstance(i, int) and i == 2:
                    dve.wait_ge(wa_hi, 1)
                    V.tensor_tensor(wa_l[:], war[:], wa_h[:].bitcast(F32), ALU.subtract).then_inc(wa_lo, 1)

            def qk_rest(c, m, cc):
                dve.wait_ge(part0, 4 * c + m + 1)
                V.scalar_tensor_tensor(rest[m % 2][:], bank[6 + m % 2][:, 0:CHUNK], 0.125 if m < 2 else 1.0, parts[:, m, 0, :],
                                       ALU.mult, ALU.subtract).then_inc(rest1, 1)

            def part_2(c, m, cc):
                dve.wait_ge(part1, 4 * c + m + 1)
                V.tensor_tensor(parts[:, m, 2, :], rest[m % 2][:], parts[:, m, 1, :], ALU.subtract).then_inc(part2, 1)

            def first_qk(m):
                def step(i, b):
                    if isinstance(i, int) and i == NT - 1:
                        for n in (m, m + 1):
                            qk_rest(0, n, 0)
                            part_2(0, n, 0)
                return step

            embedding(dve, [(-1, newton_a), (0, embed_out), (-1, newton_b), (0, stats), (-1, newton_c), (0, aggregate),
                            (-1, norm), (0, variance), (-3, keep_lo), (0, split_wa),
                            (-1, first_qk(0)), (-2, first_qk(2))])

            V.tensor_tensor(lamt[:], lam_sb[:, 0:2, :], lam_sb[:, 2:4, :], ALU.mult).then_inc(lam_a, 1)
            dve.wait_ge(lam_a, 1)
            V.tensor_reduce(lam2[:], lamt[:], AX.X, ALU.add).then_inc(lam_b, 1)
            dve.wait_ge(lam_c, 1)
            V.tensor_tensor(lamd[:], laml[:, 1:2], laml[:, 0:1], ALU.subtract).then_inc(lam_d, 1)
            dve.wait_ge(lam_d, 1)
            V.tensor_scalar(neglam[:], lamd[:], -LAMBDA_INIT, None, ALU.add).then_inc(lam_e, 1)
            dve.wait_ge(wp_in, 16)
            V.tensor_scalar(wpg[:], wpr[:], gam_sb[:], (1.0 - LAMBDA_INIT) / 2, ALU.mult, ALU.mult).then_inc(wp_g, 1)
            dve.wait_ge(cst_in, 16)
            V.tensor_copy(sel_bf[:], cs[0:S, C_SEL:C_SEL + 128]).then_inc(init_done, 1)
            V.tensor_copy(mask_bf[:], bc(cs[0:S, C_MASK:C_MASK + S].unsqueeze(1), [S, 8, S])).then_inc(init_done, 1)
            V.tensor_copy(one_bf[:], cs[:, C_ONE:C_ONE + 128]).then_inc(init_done, 1)
            V.tensor_copy(up_bf[:], cs[:, C_UP:C_UP + 128]).then_inc(init_done, 1)

            dve.wait_ge(wp_hi, 1)
            V.tensor_tensor(wp_l[:], wpg[:], wp_h[:].bitcast(F32), ALU.subtract).then_inc(wp_lo, 1)

            dve.wait_ge(lam_e, 1)

            def halves(c, k):
                return 8 * c + k, k % 2, bank[k % 2][:, 0:8 * S].rearrange("p (m s) -> p m s", m=8)

            def row_max(c, k, cc):
                u, b, s3 = halves(c, k)
                dve.wait_ge(scored, u + 1)
                V.tensor_reduce(smax[b][:], s3, AX.X, ALU.max).then_inc(maxed, 1)

            def centre(c, k, cc):
                u, b, s3 = halves(c, k)
                dve.wait_ge(maxed, u + 1)
                need(dve, turned, u - 1)
                V.tensor_tensor(Sm[b][:].rearrange("p m (j s) -> p (m j) s", j=2), s3,
                                bc(smax[b][:].unsqueeze(2), [128, 8, S]), ALU.subtract).then_inc(centred, 1)

            def products(b):
                return bank[4 + b][:, 0:4 * 2 * VW].rearrange("p (m n) -> p m n", n=VW)

            def row_sums(c, k, cc):
                u, b = 8 * c + k, k % 2
                dve.wait_ge(weighed, u + 1)
                V.reciprocal(rz[:], products(b)[:, :, 32]).then_inc(rz_done, 1)

            def normalise(c, k, cc):
                u, b = 8 * c + k, k % 2
                dve.wait_ge(rz_done, u + 1)
                for jj in range(2):
                    r = slice(SLOT * jj, SLOT * jj + SLOT)
                    V.tensor_tensor(on[r, :, :], products(b)[r, :, 16 * jj:16 * jj + 16],
                                    bc(rz[r, :].unsqueeze(2), [SLOT, 8, 16]), ALU.mult).then_inc(on_done, 1)

            def difference(c, k, cc):
                u, b, tile, tb_, img = 8 * c + k, k % 2, 2 * c + k // 4, k // 4, k // 2 % 2
                dve.wait_ge(on_done, 2 * u + 2)
                o4 = on[:].rearrange("p (m j) d -> p m j d", j=2)
                need(dve, ao_done, tile - 1)
                V.scalar_tensor_tensor(att[tb_][:, img, 4 * b:4 * b + 4, :], o4[:, :, 1, :], neglam[:, 0:1], o4[:, :, 0, :],
                                       ALU.mult, ALU.add).then_inc(att_done, 1)

            def post(what, tile, b, c, k):
                if what == "R":
                    dve.wait_ge(sq_done, tile + 1)
                    V.tensor_reduce(ms[:], sq[:], AX.X, ALU.add).then_inc(ms_done, 1)
                    dve.wait_ge(ms_done, tile + 1)
                    V.tensor_scalar(ms2[:], ms[:], 1.0 / 16.0, EPS, ALU.mult, ALU.add).then_inc(ms2_done, 1)
                elif what == "A":
                    dve.wait_ge(aT_hi, tile + 1)
                    V.tensor_tensor(aT_l[:], bank[6 + b][:, 0:256].rearrange("p (i j t) -> p j i t", i=2, j=2)[:, :, :, 0:S],
                                    aT_h[:].bitcast(F32), ALU.subtract).then_inc(aT_lo, 1)
                elif what == "P":
                    dve.wait_ge(projected, tile + 1)
                    need(dve, h2_out[b], 8 * tile - 8 * b)
                    V.tensor_tensor(h2[b][:], bank[7 - b][0:TT, 0:D], h_of(tile), ALU.add).then_inc(h2_done, 1)
                    dve.wait_ge(h2_done, tile + 1)
                    V.bn_stats(st2[:], h2[b][:]).then_inc(st2_done, 1)
                    dve.wait_ge(small_in, 64)
                    dve.wait_ge(st2_done, tile + 1)
                    V.bn_aggr(mv2[:], st2[:]).then_inc(mv2_done, 1)
                    dve.wait_ge(mv2_done, tile + 1)
                    V.tensor_scalar(ve2[:], mv2[:, 1:2], EPS, None, ALU.add).then_inc(ve2_done, 1)
                elif what == "n":
                    dve.wait_ge(q0_done, tile + 1)
                    V.scalar_tensor_tensor(q1[:], q0[:], ve2[:], q0[:], ALU.mult, ALU.mult).then_inc(newton2, 1)
                    dve.wait_ge(newton2, 3 * tile + 1)
                    V.tensor_scalar(q2[:], q1[:], -0.5, 1.5, ALU.mult, ALU.add).then_inc(newton2, 1)
                    dve.wait_ge(newton2, 3 * tile + 2)
                    V.tensor_tensor(rs2[:], q0[:], q2[:], ALU.mult).then_inc(newton2, 1)
                    dve.wait_ge(newton2, 3 * tile + 3)
                    need(dve, hn2_turned, tile - 1)
                    need(dve, hn2_kept, tile - 1)
                    V.tensor_scalar(hn2w[b][:], h2[b][:], mv2[:, 0:1], rs2[:],
                                    ALU.subtract, ALU.mult).then_inc(hn2_done, 1)
                elif what == "N":
                    dve.wait_ge(h2T_hi, tile + 1)
                    tok = bass.ds(tile * TT, TT)
                    V.tensor_tensor(hn2T_l[:, :, tok], h2T[:], hn2T_h[:, :, tok].bitcast(F32), ALU.subtract).then_inc(h2T_lo, 1)

            attention(dve, ("half", 0, row_max), ("half", 3, row_sums), ("half", 0, centre), ("half", 3, normalise),
                      ("qk", 1, part_2), ("qk", 0, qk_rest), ("post", post), ("half", 3, difference))

            dve.wait_ge(h2_out[0], 16 * NT // 2)
            dve.wait_ge(h2_out[1], 16 * NT // 2)
            dve.wait_ge(logit_done, NT)
            dve.wait_ge(zeroed, 16 * NZ)
            done = [0]

            def link(ins):
                done[0] += 1
                ins.then_inc(routing, 1)
                dve.wait_ge(routing, done[0])

            for i in range(NT):
                V.max(mx8[:, i, :], logits[:, i, 0:E]).then_inc(routing, 1)
            done[0] += NT
            dve.wait_ge(routing, done[0])
            for i in range(NT):
                V.max_index(ix8[:, i, :], mx8[:, i, :], logits[:, i, 0:E]).then_inc(routing, 1)
            V.tensor_tensor(dl[:], mx8[:, :, 1], mx8[:, :, 0], ALU.subtract).then_inc(gate_diff, 1)
            done[0] += NT
            dve.wait_ge(routing, done[0])
            link(V.tensor_copy(ixf[:], ix8[:, :, 0:TOPK].rearrange("p i k -> p k i")))
            iota = cs[0:TT, C_IOTA:C_IOTA + E]
            for k in range(TOPK):
                link(V.tensor_tensor(oh[:, k], bc(iota.unsqueeze(2), [TT, E, NT]), bc(ixf[:, k:k + 1, :], [TT, E, NT]), ALU.is_equal))
            V.tensor_tensor(both[:], oh[:, 0], oh[:, 1], ALU.add).then_inc(chosen, 1)
            dve.wait_ge(counted, 1)
            tot = bank[7][0:TT, 0:E * NT]
            link(V.tensor_tensor_scan(cuminc[:].rearrange("p e i -> p (e i)"), cs[0:TT, C_RESET:C_RESET + E * NT], tot, 0.0, ALU.mult, ALU.add))
            link(V.tensor_tensor(excl[:].rearrange("p e i -> p (e i)"), cuminc[:].rearrange("p e i -> p (e i)"), tot, ALU.subtract))
            link(V.tensor_scalar(cnt[:], cuminc[:, :, NT - 1], float(BLK - 1), None, ALU.add))
            link(V.tensor_scalar(cnts[:], cnt[:], 7, None, ALU.logical_shift_right))
            link(V.tensor_copy(nblk[:], cnts[:]))
            link(V.tensor_tensor_scan(cumb[:], cs[0:TT, C_ONE:C_ONE + E], nblk[:], 0.0, ALU.mult, ALU.add))
            link(V.tensor_tensor(base[:], cumb[:], nblk[:], ALU.subtract))
            link(V.tensor_tensor(slotf[:].rearrange("p e i -> p (e i)"), bank[6][0:TT, 0:E * NT], excl[:].rearrange("p e i -> p (e i)"), ALU.add))
            link(V.scalar_tensor_tensor(slot2[:], bc(base[:].unsqueeze(2), [TT, E, NT]), float(BLK), slotf[:], ALU.mult, ALU.add))
            for k in range(TOPK):
                link(V.tensor_tensor(slotf[:], oh[:, k], slot2[:], ALU.mult))
                link(V.tensor_reduce(slotr[:, k], slotf[:].rearrange("p e i -> p i e"), AX.X, ALU.add))
            V.tensor_copy(slot_u[:], slotr[:]).then_inc(slots_known, 1)
            link(V.tensor_tensor(ecmp[:], bc(cumb[0:1, :].unsqueeze(1), [1, NBLK, E]),
                                 bc(cs[0:1, C_BLK:C_BLK + NBLK].unsqueeze(2), [1, NBLK, E]), ALU.is_le))
            link(V.tensor_reduce(esum[:], ecmp[:], AX.X, ALU.add))
            link(V.tensor_scalar(eid[:].rearrange("p a b -> p (a b)"), esum[:], float(E - 1), None, ALU.min))
            nq = NBLK // 4
            V.tensor_scalar(woff[:, 0:nq, 0:4], eid[:], float(KD * 2 * HID), None, ALU.mult).then_inc(eids_known, 1)
            V.tensor_scalar(woff[:, 1:nq + 1, 4:6], eid[:, :, 2:4], float(D), float(EGU), ALU.mult, ALU.add).then_inc(eids_known, 1)
            V.tensor_scalar(woff[:, 0:nq, 6:8], eid[:, :, 0:2], float(D), float(EGU), ALU.mult, ALU.add).then_inc(eids_known, 1)
            dve.wait_ge(e_exp, 2)
            link(V.tensor_scalar(ed1[:], ed[:], 1.0, None, ALU.add))
            link(V.reciprocal(w1[:], ed1[:]))
            V.tensor_tensor(w2[:], w1[:], ed[:], ALU.mult).then_inc(weights_known, 1)
            link(V.tensor_scalar(ez1[:], ez[:], 1.0, None, ALU.add))
            V.reciprocal(sig[:], ez1[:]).then_inc(weights_known, 1)

            def split_expert(n):
                dve.wait_ge(w_hi, n + 1)
                V.tensor_tensor(we_l[:, n * STG:(n + 1) * STG], stg[n % 3][:], we_h[:, n * STG:(n + 1) * STG].bitcast(F32),
                                ALU.subtract).then_inc(w_lo, 1)

            dve.wait_ge(weights_known, 2)

            def shared_chunk(c, split):
                for b in range(SB):
                    u = SB * c + b
                    dve.wait_ge(sh_silu, u + 1)
                    dve.wait_ge(sh_u, u + 1)
                    need(dve, sh_hi, u)
                    need(dve, sh_lo, u)
                    V.tensor_tensor(hs[:], sgl[:], bank[(2 * b + 1) % 4][:, 0:SH], ALU.mult).then_inc(sh_h, 1)
                    for j in (SPLITS[b] if split else ()):
                        split_expert(NW // SH1 * c + j)
                    for t in COMBINE[c][b] if c in COMBINE else ():
                        combine(t)
                    dve.wait_ge(sh_hi, u + 1)
                    need(dve, sh_y, 4 * c)
                    V.tensor_tensor(hs_l[:, b, :], hs[:], hs_h[:, b, :].bitcast(F32), ALU.subtract).then_inc(sh_lo, 1)
                for tt in range(4):
                    for j in (TILE_SPLITS[tt] if split else ()):
                        split_expert(NW // SH1 * c + j)
                    t = 4 * c + tt
                    dve.wait_ge(sh_y, t + 1)
                    dve.wait_ge(h2_in[tt % 2], 32 * c + 16 * (tt // 2) + 16)
                    need(dve, acc_out[tt % 2], 32 * c + 16 * (tt // 2))
                    V.scalar_tensor_tensor(acc[tt % 2][:], bank[4 + tt % 2][0:TT, 0:D], sig[:, t:t + 1], h2r[tt % 2][:],
                                           ALU.mult, ALU.add).then_inc(sh_acc, 1)
                    for t in COMBINE[c][SB + tt] if c in COMBINE else ():
                        combine(t)

            for c in range(SH1):
                shared_chunk(c, True)

            def block_lo(b, q):
                par = q % 2
                dve.wait_ge(b_hi, b + 1)
                V.tensor_tensor(bxT_l[par][:].rearrange("p k t -> p (k t)"), bank[par][:, 0:D],
                                bxT_h[par][:].rearrange("p k t -> p (k t)").bitcast(F32), ALU.subtract).then_inc(b_lo, 1)

            def block_h(b, q):
                par = q % 2
                dve.wait_ge(b_silu, b + 1)
                need(dve, b_hturned, b - 1)
                V.tensor_tensor(bh[par][:], bsg[par][:], bank[2 + par][:, HID:2 * HID], ALU.mult).then_inc(b_h, 1)

            def block_hlo(b, q):
                par = q % 2
                dve.wait_ge(b_hhi, b + 1)
                V.tensor_tensor(bhT_l[par][:], bank[4 + par][:, 0:BLK], bhT_h[par][:].bitcast(F32), ALU.subtract).then_inc(b_hlo, 1)

            blocks(dve, [(1, block_lo), (0, block_h), (-1, block_hlo)])

            def combine(t):
                par, y = t % 2, TOPK * (t % YR)
                dve.wait_ge(acc_in[t % 4], 16 * (t // 4 + 1))
                dve.wait_ge(y_in[t % YR], 32 * (t // YR + 1))
                need(dve, fin_done, t - 1)
                V.scalar_tensor_tensor(psum1[par][:], hn2[:, y, :], w1[:, t:t + 1], bx[t % 4][0:TT, :], ALU.mult, ALU.add).then_inc(part_sum, 1)
                dve.wait_ge(part_sum, t + 1)
                need(dve, fin_out[par], 16 * (t // 2))
                V.scalar_tensor_tensor(fin[par][:], hn2[:, y + 1, :], w2[:, t:t + 1], psum1[par][:], ALU.mult, ALU.add).then_inc(fin_done, 1)

            for c in range(SH1, NSH):
                shared_chunk(c, False)
            for t in range(4 * (NSH - 1), NT):
                combine(t)

        @block.tensor
        def _(pe):
            def product(out, pairs):
                n = 3 * len(pairs)
                for m, (lh, ll, rh, rl) in enumerate(pairs):
                    for q, (a, b) in enumerate(((lh, rh), (lh, rl), (ll, rh))):
                        last = T.matmul(out, a, b, start=(3 * m + q == 0), stop=(3 * m + q == n - 1))
                return last

            def embed(i, b):
                pe.wait_ge(x_lo, i + 1)
                need(pe, h_done, i - 1)
                for k in range(KP):
                    if isinstance(i, int) and i == 0 and k % (KP // WTP) == 0:
                        pe.wait_ge(wt_lo, k // (KP // WTP) + 1)
                    xh, xl, wh, wl = x_h[b][:, k, :], x_l[b][:, k, :], wt_h[:, k, :], wt_l[:, k, :]
                    for q, (lhs, rhs) in enumerate(((xh, wh), (xh, wl), (xl, wh))):
                        last = T.matmul(bank[6 + b][0:TT, 0:D], lhs, rhs, start=(k == 0 and q == 0), stop=(k == KP - 1 and q == 2))
                last.then_inc(embedded, 1)

            def turn_hn(i, b):
                pe.wait_ge(cst_in, 16)
                pe.wait_ge(hn_done, i + 1)
                need(pe, hT_lo, i - 1)
                for k in range(KD):
                    last = T.transpose(bank[4 + b][:, k * TT:(k + 1) * TT], hn[b][:, k * 128:(k + 1) * 128], ident[0:TT, 0:TT])
                last.then_inc(hn_turned, 1)

            def qk(c, m, cc):
                need(pe, rest1, 4 * c + m - 1)
                need(pe, (h2_done, h2T_done, aT_lo, h2_done)[m], 2 * c + (-4, -4, -3, -3)[m])
                tok = bass.ds(c * CHUNK, CHUNK)
                w = slice(m * 128, (m + 1) * 128)
                product(bank[6 + m % 2][:, 0:CHUNK], [(wa_h[:, k, w], wa_l[:, k, w], hT_h[:, k, tok], hT_l[:, k, tok])
                                                      for k in range(KD)]).then_inc(qk_made, 1)

            def first_qk(m):
                def step(i, b):
                    if isinstance(i, int) and i == NT - 1:
                        pe.wait_ge(wa_lo, 1)
                        pe.wait_ge(h_done, NT)
                        for n in (m, m + 1):
                            qk(0, n, 0)
                return step

            embedding(pe, [(0, embed), (-1, first_qk(0)), (-2, turn_hn), (-2, first_qk(2))])
            pe.wait_ge(wa_lo, 1)
            pe.wait_ge(hT_lo, NT)

            for i in range(NT):
                need(pe, v_kept, i - 1)
                tok = slice(i * TT, (i + 1) * TT)
                product(bank[4 + i % 2][0:TT, 0:D], [(hT_h[:, k, tok], hT_l[:, k, tok], wa_h[:, k, 2 * D:], wa_l[:, k, 2 * D:])
                                                     for k in range(KD)]).then_inc(v_made, 1)
            pe.wait_ge(v_kept, NT)
            pe.wait_ge(init_done, 4)
            pe.wait_ge(wp_lo, 1)
            pe.wait_ge(small_in, 64)

            def scores(c, k, cc):
                u, b, n = 8 * c + k, k % 2, k // 2
                pe.wait_ge(stacked[cc], 192 * c - 192 * cc + 384)
                need(pe, centred, u - 1)
                T.matmul(bank[b][:, 0:8 * S], sel_bf[:], mask_bf[:].rearrange("p m s -> p (m s)"), start=True, stop=False, skip_group_check=True)
                for m in range(8):
                    for jj in range(2):
                        r = slice(SLOT * jj, SLOT * jj + 8 * PARTS)
                        q = 8 * b + m
                        last = T.matmul(bank[b][SLOT * jj:SLOT * jj + S, m * S:(m + 1) * S], Qs[cc][r, q, n * S:(n + 1) * S],
                                        Ks[cc][r, q, n * S:(n + 1) * S], start=False, stop=(m == 7), skip_group_check=True)
                last.then_inc(scored, 1)

            def turn(c, k, cc):
                u, b = 8 * c + k, k % 2
                pe.wait_ge(centred, u + 1)
                need(pe, exped, u - 1)
                for m in range(4):
                    last = T.transpose(bank[2 + b][0:TT, m * 128:(m + 1) * 128], Sm[b][:, m, :], ident)
                last.then_inc(turned, 1)

            def weigh(c, k, cc):
                u, b, n = 8 * c + k, k % 2, k // 2
                pe.wait_ge(exped, u + 1)
                pe.wait_ge(vx_in[n], 32 * c + 32)
                need(pe, on_done, 2 * (u - 1))
                for m in range(4):
                    h0 = (4 * b + m) * VW
                    last = T.matmul(bank[4 + b][:, m * 2 * VW:(m + 1) * 2 * VW].rearrange("p (j n) -> p j n", j=2), PT[b][:, m, :],
                                    vx[n][:, :, h0:h0 + VW], start=True, stop=True)
                last.then_inc(weighed, 1)

            def post(what, tile, b, c, k):
                made = 4 * (c + 1) + min(k, 4) if not isinstance(c, int) else min(4 * (c + 1) + min(k, 4), 4 * NCHUNK)
                if what == "A":
                    pe.wait_ge(ao_done, tile + 1)
                    pe.wait_ge(rest1, made)
                    need(pe, h2_done, tile)
                    for i in range(2):
                        end = T.transpose(bank[6 + b][:, i * 128:(i + 1) * 128], ao[:, i, :, :].rearrange("p h d -> p (h d)"), ident)
                    end.then_inc(ao_turned, 1)
                elif what == "P":
                    pe.wait_ge(aT_lo, tile + 1)
                    pe.wait_ge(rest1, made)
                    need(pe, h2T_done, tile)
                    product(bank[7 - b][0:TT, 0:D], [(aT_h[:, j].rearrange("p i t -> p (i t)"), aT_l[:, j].rearrange("p i t -> p (i t)"), wp_h[:, j, :], wp_l[:, j, :])
                                                     for j in range(2)]).then_inc(projected, 1)
                elif what == "N":
                    pe.wait_ge(hn2_done, tile + 1)
                    need(pe, logit_done, tile)
                    for k_ in range(KD):
                        end = T.transpose(bank[6 + b][:, k_ * TT:(k_ + 1) * TT], hn2w[b][:, k_ * 128:(k_ + 1) * 128], ident[0:TT, 0:TT])
                    end.then_inc(hn2_turned, 1)
                elif what == "G":
                    pe.wait_ge(h2T_done, tile + 1)
                    pe.wait_ge(aT_lo, min(tile + 2, NT) if isinstance(tile, int) else tile + 2)
                    if b == 1:
                        pe.wait_ge(rest1, made)
                        pe.wait_ge(h2_done, tile + 1)
                    for k_ in range(KD):
                        end = T.matmul(bank[7 - b][0:TT, 0:E + 1], h2T[:, k_, :], wg_sb[:, k_, :], start=(k_ == 0), stop=(k_ == KD - 1))
                    end.then_inc(gated, 1)

            attention(pe, ("half", 0, scores), ("qk", 0, qk), ("half", 1, turn), ("post", post), ("half", 2, weigh))

            pe.wait_ge(chosen, 1)
            rhs = both[:].rearrange("p e i -> p (e i)")
            T.matmul(bank[6][0:TT, 0:E * NT], up_bf[0:TT, 0:TT], rhs, start=True, stop=True)
            T.matmul(bank[7][0:TT, 0:E * NT], one_bf[0:TT, 0:TT], rhs, start=True, stop=True).then_inc(counted, 1)

            pe.wait_ge(wsh_lo, NS)
            def shared_chunk(c):
                tok = slice(c * SH, (c + 1) * SH)
                for b in range(SB):
                    for half_, (s_, free) in enumerate(((sh_g, sh_silu), (sh_u, sh_h))):
                        need(pe, free, SB * c + max(b - 1, 0))
                        cols = [slice((b * KD + k) * 2 * HID + half_ * HID, (b * KD + k) * 2 * HID + (half_ + 1) * HID) for k in range(KD)]
                        product(bank[(2 * b + half_) % 4][:, 0:SH], [(wsh_h[:, cols[k]], wsh_l[:, cols[k]], hn2T_h[:, k, tok], hn2T_l[:, k, tok])
                                                                     for k in range(KD)]).then_inc(s_, 1)
                for tt in range(4):
                    t = 4 * c + tt
                    pe.wait_ge(sh_lo, SB * c + SB)
                    need(pe, sh_acc, t - 1 if tt >= 2 else 4 * c)
                    product(bank[4 + tt % 2][0:TT, 0:D], [(hs_h[:, b, tt * TT:(tt + 1) * TT], hs_l[:, b, tt * TT:(tt + 1) * TT],
                                                           wsh_h[:, SGU + b * D:SGU + (b + 1) * D], wsh_l[:, SGU + b * D:SGU + (b + 1) * D])
                                                          for b in range(SB)]).then_inc(sh_y, 1)

            for c in range(SH1):
                shared_chunk(c)

            pe.wait_ge(w_lo, NW)
            pe.wait_ge(slots_known, 1)
            pe.wait_ge(eids_known, 3)
            pe.wait_ge(sh_acc, 4 * SH1)

            def block_turn(b, q):
                par = q % 2
                pe.wait_ge(bx_in[q], 4 * b + 16 - 4 * q)
                need(pe, b_lo, b - 1)
                for k in range(KD):
                    last = T.transpose(bank[par][:, k * BLK:(k + 1) * BLK], bx[q][:, k * 128:(k + 1) * 128], ident)
                last.then_inc(b_turned, 1)

            offsets = [T.alloc_register(f"offset{n}") for n in range(8)]
            at = [None] * 8

            def expert_weights(b):
                T.load(offsets, woff[:].rearrange("p a n -> p (a n)")[0:1, bass.ds(2 * b, 8)])
                for n in range(8):
                    low, high = (0, (E - 1) * KD * 2 * HID) if n < 4 else (0, EGU + (E - 1) * D)
                    at[n] = T.snap(offsets[n], min_val=low, max_val=high)

            def block_gu(b, q):
                par = q % 2
                e = at[q]
                pe.wait_ge(b_lo, b + 1)
                need(pe, b_h, b - 1)
                product(bank[2 + par][:, 0:2 * HID], [(bxT_h[par][:, k, :], bxT_l[par][:, k, :],
                                                       we_h[:, bass.ds(e + k * 2 * HID, 2 * HID)],
                                                       we_l[:, bass.ds(e + k * 2 * HID, 2 * HID)])
                                                      for k in range(KD)]).then_inc(b_gu, 1)

            def block_hturn(b, q):
                par = q % 2
                pe.wait_ge(b_h, b + 1)
                need(pe, b_hlo, b - 1)
                T.transpose(bank[4 + par][:, 0:BLK], bh[par][:], ident).then_inc(b_hturned, 1)

            def block_down(b, q):
                par = q % 2
                e = at[4 + (q + 2) % 4]
                pe.wait_ge(b_hlo, b + 1)
                need(pe, b_ykept, b - 1)
                product(bank[6 + par][:, 0:D], [(bhT_h[par][:], bhT_l[par][:], we_h[:, bass.ds(e, D)],
                                                 we_l[:, bass.ds(e, D)])]).then_inc(b_y, 1)

            blocks(pe, [(1, block_turn), (0, block_gu), (-1, block_hturn), (-2, block_down)], begin=expert_weights)
            pe.wait_ge(b_hlo, NBLK)
            for c in range(SH1, NSH):
                shared_chunk(c)


def kernel(**inputs):
    import numpy as np
    import concourse.bacc as bacc
    from concourse import mybir as mb
    from concourse.bass_utils import run_bass_kernel_spmd

    a = {k: np.asarray(v) for k, v in inputs.items()}
    P_, G_ = 16, 7
    x = a["x"].reshape(IMAGES, 3, G_, P_, G_, P_).transpose(1, 3, 5, 0, 2, 4).reshape(KP, 128, NT, TT)
    wq, wk, wv = (a["L0_attn_w_attn"][:, n * D:(n + 1) * D] for n in range(3))
    turned = [w.reshape(D, HP, 2, 2, 8).transpose(0, 2, 4, 1, 3).reshape(D, D) for w in (wq, wk)]
    wa = np.concatenate(turned + [wv], axis=1)
    gu = np.concatenate([a["L0_ffn_We_gate"], a["L0_ffn_We_up"]], axis=1)
    sgu = np.concatenate([a["L0_ffn_Ws_gate"].reshape(SB, HID, D), a["L0_ffn_Ws_up"].reshape(SB, HID, D)], axis=1)

    def gate_up(w):
        return w.reshape(w.shape[0], 2 * HID, KD, 128).transpose(3, 0, 2, 1).reshape(128, -1)

    arrays = {
        "xt": x.transpose(2, 1, 0, 3).reshape(NT * 128, KP * TT),
        "wt": a["L0_tok_W"].T.reshape(KP, 128, D).transpose(1, 0, 2).reshape(128, KP * D),
        "tb": a["L0_tok_b"].reshape(1, D),
        "wa": wa.reshape(KD, 128, 3 * D).transpose(1, 0, 2),
        "wp": a["L0_attn_w_proj"].reshape(HP, 2, 16, D).transpose(0, 2, 1, 3).reshape(128, 2, D),
        "gam": np.tile(a["L0_attn_gamma"], HP).reshape(128, 1),
        "lam": np.stack([a["L0_attn_lambda_" + n] for n in ("q1", "q2", "k1", "k2")]).reshape(1, 4, 8),
        "wg": np.concatenate([a["L0_ffn_Wg"], a["L0_ffn_Wsg"]]).T.reshape(KD, 128, E + 1).transpose(1, 0, 2),
        "we": np.concatenate([gate_up(gu), a["L0_ffn_We_down"].transpose(2, 0, 1).reshape(HID, -1)], axis=1),
        "wsh": np.concatenate([gate_up(sgu), a["L0_ffn_Ws_down"].reshape(D, SB, HID).transpose(2, 1, 0).reshape(HID, -1)], axis=1),
        "cst": constants(),
    }
    arrays = {k: np.ascontiguousarray(v) for k, v in arrays.items()}
    nc = bacc.Bacc("TRN2", target_bir_lowering=False, num_devices=1)
    aps = [nc.dram_tensor(k, v.shape, mb.dt.from_np(v.dtype), kind="ExternalInput").ap() for k, v in arrays.items()]
    aps.append(nc.dram_tensor("out", (TOK, D), F32, kind="ExternalOutput").ap())
    build(nc, *aps)
    r = run_bass_kernel_spmd(nc, [arrays], core_ids=[0])
    return np.asarray(r.results[0]["out"]).reshape(IMAGES, S, D)
```
